# Optimizing a Trainium2 kernel written in Bass

```python
import numpy as np
import jax
import jax.numpy as jnp

def _softmax(x, axis=-1):
    return jax.nn.softmax(x, axis=axis)

def _gelu(x):
    return jax.nn.gelu(x, approximate=True)

def _silu(x):
    return jax.nn.silu(x)

def _sigmoid(x):
    return jax.nn.sigmoid(x)

def _layernorm(x, axis=-1, eps=1e-05):
    m = jnp.mean(x, axis=axis, keepdims=True)
    v = jnp.var(x, axis=axis, keepdims=True)
    return (x - m) / jnp.sqrt(v + eps)

def _scatter_add(tgt, idx, src, axis=0):
    return tgt.at[idx].add(src)

def _segment_sum(src, seg, n):
    return jax.ops.segment_sum(src, seg, n)
kernel_name = 'mk_gnn_preln_d2_gnn_r32_e14020'

def setup_inputs(seed: int=0):
    np.random.seed(seed)
    _w = jnp.asarray

    def _rec_inputs():
        import jax
        import jax.numpy as jnp
        _gk = jax.random.key(seed)
        x = -0.0003713 + 1 * jax.random.normal(jax.random.fold_in(_gk, 1), (3125, 128), jnp.float32)
        _s = jax.random.randint(jax.random.fold_in(_gk, 2), (25000,), 0, 3125, jnp.int32)
        _d = jax.random.randint(jax.random.fold_in(_gk, 3), (25000,), 0, 3125, jnp.int32)
        _loop = jnp.arange(3125, dtype=jnp.int32)
        src = jnp.concatenate([_s, _d, _loop])
        dst = jnp.concatenate([_d, _s, _loop])
        _o = jnp.argsort(dst, stable=True)
        src = src[_o]
        dst = dst[_o]
        edge_attr_32 = 0.000196303 + 1.00016 * jax.random.normal(jax.random.fold_in(_gk, 11), (53125, 32), jnp.float32)
        return (x, src, dst, edge_attr_32)
    x, src, dst, edge_attr_32 = _rec_inputs()

    def _L0_gnn_setup():
        import jax, jax.numpy as jnp
        import numpy as np
        HEADS = 8
        NEG_SLOPE = 0.2
        N_NODES = 3125
        N_EDGES = 50000
        C_IN = 128
        OUT_CH = 16
        key = jax.random.key(seed)
        k1, k2, k3, k4 = jax.random.split(key, 4)
        x = jax.random.normal(k1, (N_NODES, C_IN), dtype=jnp.float32)
        edge_index = jax.random.randint(k2, (2, N_EDGES), 0, N_NODES, dtype=jnp.int64)
        W = jax.random.normal(k3, (HEADS * OUT_CH, C_IN), dtype=jnp.float32) * 0.05
        att = jax.random.normal(k4, (2 * HEADS * OUT_CH,), dtype=jnp.float32) * 0.1
        bias = jnp.zeros((HEADS * OUT_CH,), dtype=jnp.float32)
        return {'x': x, 'W': W, 'att': att, 'bias': bias, 'edge_index': edge_index}
    _L0_gnn_all = _L0_gnn_setup()
    _L0_gnn_in = {k: v for k, v in _L0_gnn_all.items() if k in ('W', 'att', 'bias')}
    del _L0_gnn_all

    def _L1_gnn_setup():
        import jax, jax.numpy as jnp
        import numpy as np
        import math
        N_NODES = 50000
        N_EDGES = 25000
        D = 128
        H = 8
        HD = D // H
        ED = 32
        key = jax.random.key(seed)
        ks = jax.random.split(key, 16)
        s = 1.0 / math.sqrt(D)
        se = 1.0 / math.sqrt(ED)
        return {'x': jax.random.normal(ks[0], (N_NODES, D), jnp.float32), 'edge_index': jax.random.randint(ks[1], (2, N_EDGES), 0, N_NODES, jnp.int64), 'edge_attr': jax.random.normal(ks[2], (N_EDGES, ED), jnp.float32), 'Wq': jax.random.normal(ks[3], (D, D), jnp.float32) * s, 'bq': jnp.zeros((D,), jnp.float32), 'Wk': jax.random.normal(ks[4], (D, D), jnp.float32) * s, 'bk': jnp.zeros((D,), jnp.float32), 'Wv': jax.random.normal(ks[5], (D, D), jnp.float32) * s, 'bv': jnp.zeros((D,), jnp.float32), 'We': jax.random.normal(ks[6], (ED, H), jnp.float32) * se, 'be': jnp.zeros((H,), jnp.float32), 'Wo': jax.random.normal(ks[7], (D, D), jnp.float32) * s, 'bo': jnp.zeros((D,), jnp.float32), 'gamma': jnp.ones((D,), jnp.float32), 'beta': jnp.zeros((D,), jnp.float32)}
    _L1_gnn_all = _L1_gnn_setup()
    _L1_gnn_in = {k: v for k, v in _L1_gnn_all.items() if k in ('Wq', 'bq', 'Wk', 'bk', 'Wv', 'bv', 'We', 'be', 'Wo', 'bo', 'gamma', 'beta')}
    del _L1_gnn_all
    return {'x': x, 'src': src, 'dst': dst, 'edge_attr_32': edge_attr_32, 'L0_gnn_W': _L0_gnn_in['W'], 'L0_gnn_att': _L0_gnn_in['att'], 'L0_gnn_bias': _L0_gnn_in['bias'], 'L1_gnn_Wq': _L1_gnn_in['Wq'], 'L1_gnn_bq': _L1_gnn_in['bq'], 'L1_gnn_Wk': _L1_gnn_in['Wk'], 'L1_gnn_bk': _L1_gnn_in['bk'], 'L1_gnn_Wv': _L1_gnn_in['Wv'], 'L1_gnn_bv': _L1_gnn_in['bv'], 'L1_gnn_We': _L1_gnn_in['We'], 'L1_gnn_be': _L1_gnn_in['be'], 'L1_gnn_Wo': _L1_gnn_in['Wo'], 'L1_gnn_bo': _L1_gnn_in['bo'], 'L1_gnn_gamma': _L1_gnn_in['gamma'], 'L1_gnn_beta': _L1_gnn_in['beta']}

def reference(x, src, dst, edge_attr_32, L0_gnn_W, L0_gnn_att, L0_gnn_bias, L1_gnn_Wq, L1_gnn_bq, L1_gnn_Wk, L1_gnn_bk, L1_gnn_Wv, L1_gnn_bv, L1_gnn_We, L1_gnn_be, L1_gnn_Wo, L1_gnn_bo, L1_gnn_gamma, L1_gnn_beta):
    import jax
    import jax.numpy as jnp

    def _L0_gnn_ref(x, W, att, bias, edge_index):
        import jax, jax.numpy as jnp
        import numpy as np
        HEADS = 8
        NEG_SLOPE = 0.2
        N_NODES = 3125
        N_EDGES = 50000
        C_IN = 128
        OUT_CH = 16
        N = x.shape[0]
        HF = W.shape[0]
        H, F = (HEADS, HF // HEADS)
        loops = jnp.arange(N, dtype=edge_index.dtype)
        src = jnp.concatenate([edge_index[0], loops])
        dst = jnp.concatenate([edge_index[1], loops])
        h = (x @ W.T).reshape(N, H, F)
        att_src, att_dst = att.reshape(2, H, F)
        a_src = jnp.einsum('nhf,hf->nh', h, att_src)
        a_dst = jnp.einsum('nhf,hf->nh', h, att_dst)
        e = a_src[src] + a_dst[dst]
        e = jnp.where(e >= 0, e, NEG_SLOPE * e)
        m = jax.ops.segment_max(e, dst, num_segments=N)
        p = jnp.exp(e - m[dst])
        denom = jax.ops.segment_sum(p, dst, num_segments=N)
        alpha = p / denom[dst]
        msg = alpha[:, :, None] * h[src]
        out = jax.ops.segment_sum(msg, dst, num_segments=N)
        return out.reshape(N, HF) + bias

    def _L1_gnn_ref(x, edge_index, edge_attr, Wq, bq, Wk, bk, Wv, bv, We, be, Wo, bo, gamma, beta):
        import jax, jax.numpy as jnp
        import numpy as np
        import math
        N_NODES = 50000
        N_EDGES = 25000
        D = 128
        H = 8
        HD = D // H
        ED = 32
        n = x.shape[0]
        residual = x
        q = (x @ Wq + bq).reshape(n, H, HD)
        k = (x @ Wk + bk).reshape(n, H, HD)
        v = (x @ Wv + bv).reshape(n, H, HD)
        src = edge_index[0]
        dst = edge_index[1]
        score = jnp.einsum('ehd,ehd->eh', q[dst], k[src]) / math.sqrt(HD)
        score = score + edge_attr @ We + be
        m = jax.ops.segment_max(score, dst, num_segments=n)
        exp_s = jnp.exp(score - m[dst])
        ssum = jax.ops.segment_sum(exp_s, dst, num_segments=n)
        attn = exp_s / (ssum[dst] + 1e-08)
        msg = attn[..., None] * v[src]
        out = jax.ops.segment_sum(msg, dst, num_segments=n)
        out = out.reshape(n, D) @ Wo + bo
        h = out + residual
        mu = h.mean(-1, keepdims=True)
        var = ((h - mu) ** 2).mean(-1, keepdims=True)
        return (h - mu) / jnp.sqrt(var + 1e-05) * gamma + beta
    edge_index = jnp.stack([src, dst])
    h = jnp.maximum(_layernorm(x, axis=-1), 0.0)
    x = x + _L0_gnn_ref(h, L0_gnn_W, L0_gnn_att, L0_gnn_bias, edge_index)
    h = jnp.maximum(_layernorm(x, axis=-1), 0.0)
    x = x + _L1_gnn_ref(h, edge_index, edge_attr_32, L1_gnn_Wq, L1_gnn_bq, L1_gnn_Wk, L1_gnn_bk, L1_gnn_Wv, L1_gnn_bv, L1_gnn_We, L1_gnn_be, L1_gnn_Wo, L1_gnn_bo, L1_gnn_gamma, L1_gnn_beta)
    return x

_drawn_inputs = setup_inputs


def setup_inputs(seed=0):
    import zlib

    import numpy as np

    out = dict(_drawn_inputs(seed))
    spreads = {'L0_gnn_bias': (0.0, 0.1),
     'L1_gnn_bq': (0.0, 0.8),
     'L1_gnn_bk': (0.0, 0.8),
     'L1_gnn_bv': (0.0, 0.1),
     'L1_gnn_be': (0.0, 0.8),
     'L1_gnn_bo': (0.0, 0.1),
     'L1_gnn_gamma': (1.0, 0.2),
     'L1_gnn_beta': (0.0, 0.1)}
    factors = {'L0_gnn_att': 4.966}
    for name, (base, spread) in spreads.items():
        noise = np.random.default_rng([zlib.crc32(name.encode()), seed]).standard_normal(out[name].shape)
        drawn = base * np.exp(spread * noise) if base else spread * noise
        out[name] = jnp.asarray(drawn.astype(out[name].dtype))
    for name, factor in factors.items():
        out[name] = (out[name] * factor).astype(out[name].dtype)
    return out
```

```python
from contextlib import ExitStack

import concourse.bass as bass
from concourse import mybir

F32 = mybir.dt.float32
BF16 = mybir.dt.bfloat16
I32 = mybir.dt.int32
ALU = mybir.AluOpType
ACT = mybir.ActivationFunctionType
AX = mybir.AxisListType

NODES, EDGES, F, ED, H = 3125, 53125, 128, 32, 8
DH = F // H
P = 128
BN = 125
BLOCKS = NODES // BN
TILES = -(-EDGES // P)
FULL = EDGES // P
REST = EDGES - FULL * P
GV = P // H
GROUPS = -(-(TILES + BLOCKS - 1) // GV)
VISITS = GROUPS * GV
UNROLL = 4
QV = 4
VP = 112
VK = VISITS // VP
GK = VP // GV
SLOT = DH + 2
W0 = F + H
W1 = 2 * F
ROW = 2 * P + 2
ATTR_C = 16
PAD_DST = 4000
BIG = float(2 ** 100)
LOW = -BIG
SLOPE = 0.2
CHUNKS = [(s, min(3, BLOCKS - s)) for s in range(0, BLOCKS, 3)]
LN_CHUNK = 5


class Signal:

    def __init__(self, s, base):
        self.s, self.base = s, base


def gnn_kernel(nc, x, src, dst, edge_attr, w0, att, bias0, wq, bq, wk, bk, wv, bv, we, be, wo, bo, gamma,
               beta, out):
    ctx = ExitStack()

    def sb(name, shape, dt=F32):
        return ctx.enter_context(nc.sbuf_tensor(name, shape, dt))

    def sem(name):
        return ctx.enter_context(nc.semaphore(name))

    def wait(eng, s, value):
        if not isinstance(value, int) or value > 0:
            if isinstance(s, Signal):
                eng.wait_ge(s.s, s.base + value)
            else:
                eng.wait_ge(s, value)

    with ctx:
        edge_rows = nc.dram_tensor("edge_rows", (TILES + 1, ROW), I32, kind="Internal").ap()
        bias_rows = nc.dram_tensor("bias_rows", (TILES + 1, P * H), F32, kind="Internal").ap()
        attr_tail = nc.dram_tensor("attr_tail", (GROUPS * ATTR_C, ED), F32, kind="Internal").ap()
        table0 = nc.dram_tensor("table0", (NODES, W0), F32, kind="Internal").ap()
        table1 = nc.dram_tensor("table1", (NODES, W1), F32, kind="Internal").ap()

        xs = sb("xs", [BN, BLOCKS, F])
        hn = sb("hn", [BN, BLOCKS, F])
        h0b = sb("h0b", [P, VISITS * H])
        h0 = h0b[0:BN, 0:BLOCKS * W0].rearrange("p (b f) -> p b f", f=W0)
        ebias = h0b[:, 0:VISITS * H].rearrange("p (v h) -> p v h", h=H)
        nd = sb("nd", [BN, BLOCKS, 2 * H])
        acc = sb("acc", [BN, BLOCKS, H * SLOT])
        qe = sb("qe", [P, VISITS * H])
        eb_nat = qe[:, 0:VISITS * H]
        q_sb = qe[0:BN, 0:BLOCKS * F].rearrange("p (b f) -> p b f", f=F)
        G = sb("G", [P, UNROLL, GV, W1])
        kv = G[0:BN, :, :, :].rearrange("p u v f -> p (u v f)")[:, 0:BLOCKS * W1].rearrange(
            "p (b f) -> p b f", f=W1)
        work = G[0:BN, :, :, :].rearrange("p u v f -> p (u v f)")[:, 0:BLOCKS * F].rearrange(
            "p (b f) -> p b f", f=F)
        work2 = G[0:BN, :, :, :].rearrange("p u v f -> p (u v f)")[:, BLOCKS * F:2 * BLOCKS * F].rearrange(
            "p (b f) -> p b f", f=F)
        bias_v = G[0:VP, :, :, :].rearrange("p u v f -> p (u v f)")[:, 8192:8192 + VK * P * H].rearrange(
            "p (k e h) -> p k e h", k=VK, h=H)
        rows_i = G[0:VP, :, :, :].rearrange("p u v f -> p (u v f)")[:, 0:VK * ROW].bitcast(I32).rearrange(
            "p (k r) -> p k r", k=VK)
        S = sb("S", [P, 2, GV, BN])
        ST_ = sb("ST", [P, GV, P])
        ST = ST_[0:BN, :, :]
        PV = sb("PV", [P, GV, H, SLOT])
        prod = sb("prod", [P, 2, QV * F])
        attr_in = prod
        rows = sb("rows", [P, 2, VISITS])
        chain_pen = rows[0:H, :, :]
        offs = [rows[32 * k + 32:32 * k + 33, 0, :].bitcast(I32) for k in range(3)]

        def views(tensor, start, shapes):
            made, at = [], start
            for parts, shape, dt in shapes:
                size = 1
                for d in shape:
                    size *= d
                v = tensor[0:parts, at:at + size]
                if dt is not F32:
                    v = v.bitcast(dt)
                names = "abc"[:len(shape)]
                made.append(v.rearrange(f"p ({' '.join(names)}) -> p {' '.join(names)}", **dict(zip(names, shape)))
                            if len(shape) > 1 else v)
                at += size
            return made

        S_flat = S[:, :, :, :].rearrange("p k v n -> p (k v n)")
        dst_nat, ge, vend, vtmp, lid_v, FLB_, cmpb, iota_i = views(S_flat, 0, (
            (TILES // QV, (QV * P,), I32), (BLOCKS - 1, (2, TILES), F32), (VP, (TILES,), F32), (VP, (2, TILES), F32),
            (VP, (VK, P), F32), (TILES // QV, (2 * QV, BLOCKS - 1), F32), (VP, (VK, BLOCKS - 1), F32), (P, (P,), I32)))
        HT, Rep = views(ST_[:, :, :].rearrange("p v e -> p (v e)"), 0, (
            (P, (2, 3 * BN), F32), (VP, (GK, GV * H), F32)))
        nst_, rows_f = views(PV[:, :, :, :].rearrange("p v h k -> p (v h k)"), 0, (
            (BN, (6, BLOCKS * H), F32), (VP, (VK, ROW), F32)))
        nst = nst_.rearrange("p k (b h) -> p k b h", h=H)
        pen = sb("pen", [P, GROUPS, P + 1], BF16)
        pcur = sb("pcur", [P, 2, P + 1], BF16)
        idx_all = sb("idx_all", [P, VISITS + UNROLL * GV], I32)
        idx_stage = sb("idx_stage", [P, UNROLL, GV], I32)
        lid = sb("lid", [P, VISITS])
        first_lid = sb("first_lid", [H, GROUPS])
        raw = sb("raw", [P, GV, H])
        sc = sb("sc", [P, GV, H])
        es = sb("es", [P, 2, GV, H])
        esT = sb("esT", [P, P])
        smax = sb("smax", [P, P])
        FR = sb("FR", [P, 2, P])
        RH = sb("RH", [P, 2, GV])
        D = sb("D", [H, 2, 2, GV + 1])
        CCM = sb("CCM", [P, 2, GV])
        CC = sb("CC", [P, 2])
        FF = sb("FF", [P, P])
        MM = sb("MM", [P, P])
        DD = sb("DD", [P, 2, P])
        EP = sb("EP", [P, 2, P])
        PS = sb("PS", [P, P])
        DF = sb("DF", [H, 2])
        R8 = sb("R8", [H, H])
        OHF = sb("OHF", [H, BN])
        AL = sb("AL", [BN, H])
        attrT = sb("attrT", [P, QV * P])
        ident = sb("ident", [P, P])
        ones = sb("ones", [P, P])
        iota_n = sb("iota_n", [P, P])
        thr_row = sb("thr_row", [P, BLOCKS - 1])
        thr_i = sb("thr_i", [P, BLOCKS - 1], I32)
        thr_col = sb("thr_col", [P, 1])
        vcol = sb("vcol", [VP, VK])
        vcol_i = sb("vcol_i", [VP, VK + 1], I32)
        headmask = sb("headmask", [P, H])
        Vsel = sb("Vsel", [P, GV])
        HselT = sb("HselT", [H, GV, H])
        Hsel = sb("Hsel", [P, H])
        E0 = sb("E0", [P, H])
        pad_i = sb("pad_i", [1, 2, P + 2], I32)
        FL = sb("FL", [TILES // QV, 2, QV])
        vstat = sb("vstat", [VP, 10, VK])
        tidx = sb("tidx", [VP, VK], I32)
        chain_b = sb("chain_b", [VP, 2, VK, H])
        w0n = sb("w0n", [F, F])
        attc = sb("attc", [P, 2])
        attblk = sb("attblk", [P, 2 * H])
        WA = sb("WA", [P, F + 2 * H])
        Wqkv = sb("Wqkv", [P, 3 * F])
        Wo = sb("Wo", [P, F])
        WeBD = sb("WeBD", [P, QV, H])
        rowv = sb("rowv", [BN, 7, F])
        be_r = sb("be_r", [P, H])
        st = sb("st", [BN, 6, BLOCKS])

        bank = [ctx.enter_context(nc.psum_tensor(f"bank{i}", [P, 512], F32)) for i in range(8)]
        tp = bank[0:2]
        ex = bank[2:4]
        ms = bank[4:6]
        sT = bank[6]
        sm = bank[7]

        s_dst, s_x, s_w, s_pad, s_er, s_bz = (sem(n) for n in (
            "dst_in", "x_in", "weights_in", "pads_out", "edge_rows_out", "bias_pad_out"))
        s_tail = sem("attr_tail_out")
        s_attr = [sem(f"attr_in{k}") for k in range(2)]
        s_rows = sem("rows_in")
        s_const = sem("constants")
        s_pool = sem("pool_done")
        s_v = sem("vector_done")
        s_fl, s_flT, s_ge, s_diff = sem("firsts_lasts"), sem("firsts_lasts_rows"), sem("block_steps"), sem("steps_summed")
        s_tidx, s_rowsf, s_vlid = sem("tile_index"), sem("rows_as_float"), sem("visit_ids")
        s_vt, s_vte = sem("visit_transposes"), sem("visit_copies")
        s_pent, s_pene = sem("pen_spread"), sem("pen_copied")
        s_penfree = sem("pen_bank_free")
        s_idx0 = sem("first_indices")
        s_watt, s_wps, s_wc = sem("att_blocks"), sem("weights_products"), sem("weights_ready")
        s_tab = [sem("table0_out"), sem("table1_out")]
        s_ebout, s_ebin, s_ebt, s_ebe = sem("bias_rows_out"), sem("bias_rows_in"), sem("bias_transposed"), sem("bias_copied")
        s_ebfin = sem("bias_complete")
        s_out = sem("out_written")
        s_go = sem("quarters_gathered")

        NODE_SEMS = ("xc", "sq", "var", "std", "hn", "hT_ps", "hT", "feat", "feat_out", "feat_done")
        LOOP_SEMS = dict(S_ready=4, t_done=4, st_ready=4, expanded=4, qk_done=0, score_parts=1, scores_ready=1,
                         es_ready=1, scoreT=1, esT_ready=1, smax_ready=1, edge_scans=2, rh_ready=1, hop1=1, x_done=1,
                         carry=1, u_done=1, hop2=1, cc_mul=1, cc_done=1, f_done=1, m_done=1, dd_ready=2, p_ready=1,
                         ps_ready=1, pT=1, pcols=1, pv_ready=4, mm_done=GV, acc_added=GV, df=2, r8_ready=1,
                         ohf_ready=1, al_mm=1, al_ready=1, rescaled=1, idx_staged=1, pcur_ready=1)
        loop_sem = {k: sem(k) for k in LOOP_SEMS}

        class Layer:
            def __init__(self, n):
                self.sem = {k: sem(f"{k}_{n}") for k in NODE_SEMS} | loop_sem
                self.base = {k: (n == 1) * GROUPS * v for k, v in LOOP_SEMS.items()}

            def __getitem__(self, k):
                return Signal(self.sem[k], self.base.get(k, 0))

        L = [Layer(0), Layer(1)]
        s_gath = [[[sem(f"gathered{n}_{u}_{j}") for j in range(GV // QV)] for u in range(UNROLL)] for n in range(1)]
        a_T, a_Te, a_mm, a_out = sem("attrT_ps"), sem("attrT"), sem("bias_mm"), sem("bias_sb")
        s_fin_on, s_fT, s_fTe, s_fo, s_fh = (sem(n) for n in ("mean_msgs", "msgsT_ps", "msgsT", "projected", "projected_used"))
        X1 = sem("x1_ready")
        NODE_SEMS = NODE_SEMS[:5]
        F_ = Layer("f")

        NPOOL = 16
        block = ctx.enter_context(nc.Block())

        def run_groups(eng, step):
            for u in range(UNROLL):
                step(u, u, 0, True, u > 0)
            with eng.Fori(1, GROUPS // UNROLL) as i:
                for u in range(UNROLL):
                    step(UNROLL * i + u, u, i, True, True)
            step(GROUPS, GROUPS % UNROLL, GROUPS // UNROLL, False, True)

        @block.sync
        def _(sp):
            sp.wait_ge(s_const, 1)
            a = 96 * QV * P
            sp.dma_start(dst_nat[0:96, :], dst[0:a].rearrange("(p c) -> p c", p=96)).then_inc(s_dst, 16)
            b = 103 * QV * P
            sp.dma_start(dst_nat[96:103, :], dst[a:b].rearrange("(p c) -> p c", c=QV * P)).then_inc(s_dst, 16)
            sp.dma_start(dst_nat[103:104, 0:EDGES - b], dst[b:EDGES].rearrange("(a c) -> a c", a=1)).then_inc(s_dst, 16)
            sp.dma_start(edge_rows[0:FULL, 0:P], src[0:FULL * P].rearrange("(t c) -> t c", c=P)).then_inc(s_er, 16)
            sp.dma_start(edge_rows[1:FULL, P:ROW],
                         bass.AP(tensor=dst.tensor, offset=P - 1, ap=[[P, FULL - 1], [1, P + 2]])).then_inc(s_er, 16)
            sp.dma_start(edge_rows[0:1, P + 1:ROW], dst[0:P + 1].rearrange("(a c) -> a c", a=1)).then_inc(s_er, 16)
            sp.dma_start(edge_rows[FULL:FULL + 1, 0:REST], src[FULL * P:EDGES].rearrange("(a c) -> a c", a=1)).then_inc(s_er, 16)
            sp.dma_start(edge_rows[FULL:FULL + 1, P:P + 1 + REST],
                         dst[FULL * P - 1:EDGES].rearrange("(a c) -> a c", a=1)).then_inc(s_er, 16)
            sp.dma_start(edge_rows[0:1, P:P + 1], pad_i[0:1, 0, P:P + 1]).then_inc(s_er, 16)
            sp.dma_start(edge_rows[FULL:FULL + 1, REST:P], pad_i[0:1, 0, 0:P - REST]).then_inc(s_er, 16)
            sp.dma_start(edge_rows[FULL + 1:FULL + 2, 0:P], pad_i[0:1, 0, 0:P]).then_inc(s_er, 16)
            sp.dma_start(edge_rows[FULL:FULL + 1, P + 1 + REST:ROW], pad_i[0:1, 1, 0:P + 1 - REST]).then_inc(s_er, 16)
            sp.dma_start(edge_rows[FULL + 1:FULL + 2, P:ROW], pad_i[0:1, 1, :]).then_inc(s_er, 16)
            sp.dma_start(xs[:, :, :], x.rearrange("(b p) f -> p b f", p=BN)).then_inc(s_x, 16)
            m = EDGES - 127 * TILES
            sp.dma_start(attr_tail[0:m, :], edge_attr[127 * TILES:EDGES, :]).then_inc(s_tail, 16)
            sp.dma_start(attr_tail[m:m + P, :], ones[:, 0:ED]).then_inc(s_tail, 16)
            rest = GROUPS * ATTR_C - m - P
            sp.dma_start(attr_tail[m + P:m + P + rest, :], ones[0:rest, 0:ED]).then_inc(s_tail, 16)
            sp.wait_ge(s_v, 5)
            sp.dma_start(bias_rows[TILES:TILES + 1, :], acc[0:1, :, :].rearrange("p b f -> p (b f)")[:, 0:P * H]).then_inc(s_bz, 16)
            table0_v = table0.rearrange("(b p) f -> p b f", p=BN)
            for n, (b0, nb) in enumerate(CHUNKS):
                wait(sp, L[0]["feat_out"], n + 1)
                sp.dma_start(table0_v[:, b0:b0 + nb, :], h0[:, b0:b0 + nb, :]).then_inc(s_tab[0], 16)
            sp.wait_ge(s_tail, 48)
            sp.wait_ge(s_penfree, -(-GROUPS // 3))

            def step(g, u, i, new, old):
                if not new:
                    return
                wait(sp, a_T, g - 1)
                to = attr_in[:, u % 2, :]
                for lo, hi in ((0, 112), (112, 127)):
                    sp.dma_start(to[lo:hi, :],
                                 bass.AP(tensor=edge_attr.tensor, offset=lo * TILES * ED + g * (ATTR_C * ED),
                                         ap=[[TILES * ED, hi - lo], [1, ATTR_C * ED]])).then_inc(s_attr[u % 2], 16)
                sp.dma_start(to[127:128, :], bass.AP(tensor=attr_tail.tensor, offset=g * (ATTR_C * ED),
                                                     ap=[[ATTR_C * ED, 1], [1, ATTR_C * ED]])).then_inc(s_attr[u % 2], 16)

            run_groups(sp, step)
            sp.wait_ge(s_ebfin, 1)
            sp.dma_start(bias_rows.rearrange("t c -> (t c)")[0:P * TILES * H].rearrange("(p c) -> p c", p=P),
                         eb_nat[:, 0:TILES * H]).then_inc(s_ebout, 16)
            table1_v = table1.rearrange("(b p) f -> p b f", p=BN)
            for n, (b0, nb) in enumerate(CHUNKS):
                wait(sp, L[1]["feat_out"], b0 + nb)
                sp.dma_start(table1_v[:, b0:b0 + nb, :], kv[:, b0:b0 + nb, :]).then_inc(s_tab[1], 16)
            sp.wait_ge(s_out, 1)
            out_v = out.rearrange("(b p) f -> p b f", p=BN)
            sp.dma_start(out_v, work[:, :, :]).then_inc(s_out, 16)
            sp.wait_ge(s_out, 17)
            sp.wait_ge(s_tab[0], 16 * len(CHUNKS))
            sp.wait_ge(s_tab[1], 16 * len(CHUNKS))
            sp.wait_ge(s_ebout, 16)
            sp.wait_ge(s_er, 160)
            sp.wait_ge(s_bz, 16)

        @block.gpsimd
        def _(pool):
            n = [0]
            Rep4 = Rep.rearrange("p r (v h) -> p r v h", h=H)

            def then(ins):
                n[0] += 1
                ins.then_inc(s_pool, 1)
                pool.wait_ge(s_pool, n[0])

            pool.memset(pad_i[0:1, 0, 0:P], 0).then_inc(s_pool, 1)
            pool.memset(pad_i[0:1, 0, P:P + 2], -1).then_inc(s_pool, 1)
            pool.memset(pad_i[0:1, 1, :], PAD_DST).then_inc(s_pool, 1)
            pool.memset(ones[:, :], 1.0).then_inc(s_pool, 1)
            n[0] = 4
            then(pool.memset(dst_nat, NODES - 1))
            pool.sem_inc(s_const, 1)
            pool.memset(ident[:, :], 0.0).then_inc(s_pool, 1)
            pool.memset(HselT[:, :, :], 0.0).then_inc(s_pool, 1)
            pool.memset(Rep, 0.0).then_inc(s_pool, 1)
            n[0] += 3
            then(pool.memset(E0[:, :], 0.0))
            pool.iota(iota_i[:, :], pattern=[[1, P]], base=0, channel_multiplier=0).then_inc(s_pool, 1)
            pool.iota(thr_i[:, :], pattern=[[BN, BLOCKS - 1]], base=BN, channel_multiplier=0).then_inc(s_pool, 1)
            pool.iota(vcol_i[:, 0:VK], pattern=[[VP, VK]], base=0, channel_multiplier=1).then_inc(s_pool, 1)
            pool.iota(vcol_i[:, VK:VK + 1], pattern=[[0, 1]], base=BN, channel_multiplier=BN).then_inc(s_pool, 1)
            n[0] += 4
            then(pool.affine_select(out=ident[:, :], in_=ident[:, :], compare_op=ALU.not_equal, fill=1.0,
                                    base=0, pattern=[[-1, P]], channel_multiplier=1))
            then(pool.affine_select(out=E0[:, :], in_=E0[:, :], compare_op=ALU.not_equal, fill=1.0,
                                    base=0, pattern=[[0, H]], channel_multiplier=1))
            pool.sem_inc(s_const, 1)
            then(pool.affine_select(out=HselT[:, :, :], in_=HselT[:, :, :], compare_op=ALU.not_equal, fill=1.0,
                                    base=0, pattern=[[0, GV], [-1, H]], channel_multiplier=1))
            then(pool.affine_select(out=Rep4, in_=Rep4, compare_op=ALU.not_equal, fill=1.0,
                                    base=0, pattern=[[-GV, GK], [-1, GV], [0, H]], channel_multiplier=1))
            for t, w, k in ((headmask, H, DH), (Vsel, GV, H)):
                then(pool.affine_select(out=t[:, :], in_=ones[:, 0:w], compare_op=ALU.is_ge, fill=0.0,
                                        base=0, pattern=[[-k, w]], channel_multiplier=1))
                then(pool.affine_select(out=t[:, :], in_=t[:, :], compare_op=ALU.is_ge, fill=0.0,
                                        base=k - 1, pattern=[[k, w]], channel_multiplier=-1))
            pool.sem_inc(s_const, 1)

            pool.wait_ge(s_er, 160)
            pool.wait_ge(s_tidx, 1)
            for k in range(VK):
                pool.indirect_dma_start(rows_i[:, k, :], None, edge_rows,
                                        bass.IndirectOffsetOnAxis(ap=tidx[:, k:k + 1], axis=0)).then_inc(s_rows, 16)

            def gathers(layer, table, w):
                s = L[layer]
                base = layer * (GROUPS // UNROLL)

                def step(g, u, i):
                    wait(pool, s["idx_staged"], g - (UNROLL - 1))
                    for j in range(GV // QV):
                        wait(pool, s["pv_ready"], 4 * (g - UNROLL) + j + 1)
                        pool.sem_inc(s_go, 1)
                        for v in range(QV * j, QV * j + QV):
                            pool.indirect_dma_start(
                                G[:, u, v, 0:w], None, table,
                                bass.IndirectOffsetOnAxis(ap=idx_stage[:, u, v:v + 1], axis=0)
                            ).then_inc(s_gath[0][u][j], 16)

                for u in range(UNROLL):
                    step(u, u, 0)
                with pool.Fori(1, GROUPS // UNROLL) as i:
                    for u in range(UNROLL):
                        step(UNROLL * i + u, u, i)

            pool.wait_ge(s_idx0, 1)
            pool.wait_ge(s_tab[0], 16 * len(CHUNKS))
            gathers(0, table0, W0)
            pool.wait_ge(s_ebout, 16)
            pool.wait_ge(s_bz, 16)
            wait(pool, L[0]["pv_ready"], 4 * GROUPS)
            for k in range(VK):
                pool.indirect_dma_start(bias_v[:, k, :, :].rearrange("p e h -> p (e h)"), None, bias_rows,
                                        bass.IndirectOffsetOnAxis(ap=tidx[:, k:k + 1], axis=0)).then_inc(s_ebin, 16)
            pool.wait_ge(s_tab[1], 16 * len(CHUNKS))
            pool.wait_ge(s_ebt, VK * H)
            pool.wait_ge(s_idx0, 2)
            gathers(1, table1, W1)

        @block.scalar
        def _(act):
            act.dma_start(w0n[:, :], w0).then_inc(s_w, 16)
            for k in range(2):
                act.dma_start(attc[:, k:k + 1], att.rearrange("(t p a) -> t p a", p=P, a=1)[k]).then_inc(s_w, 16)
            for k, w in enumerate((wq, wk, wv)):
                act.dma_start(Wqkv[:, F * k:F * k + F], w).then_inc(s_w, 16)
            act.dma_start(Wo[:, :], wo).then_inc(s_w, 16)
            act.wait_ge(s_v, 5)
            for c in range(QV):
                act.dma_start(WeBD[ED * c:ED * c + ED, c, :], we).then_inc(s_w, 16)
            for k, b in enumerate((bias0, bq, bk, bv, bo, gamma, beta)):
                act.dma_start(rowv[:, k, :], b.rearrange("(a f) -> a f", a=1).to_broadcast([BN, F])).then_inc(s_w, 16)
            act.dma_start(be_r[:, :], be.rearrange("(a f) -> a f", a=1).to_broadcast([P, H])).then_inc(s_w, 16)

            act.wait_ge(s_vt, 2)
            act.activation(idx_all[:, 0:VISITS], tp[0][:, 0:VISITS], ACT.Copy).then_inc(s_vte, 1)
            act.activation(lid[:, :], tp[1][:, 0:VISITS], ACT.Copy).then_inc(s_vte, 1)
            act.wait_ge(s_vte, 2)
            act.activation(idx_stage[:, :, :].rearrange("p u v -> p (u v)"), idx_all[:, 0:UNROLL * GV], ACT.Copy).then_inc(s_idx0, 1)
            act.wait_ge(s_vt, 3)
            for k, w in enumerate((H * SLOT, F, 2 * H)):
                act.activation(offs[k], ex[0][0:1, 0:VISITS], ACT.Copy, scale=float(w)).then_inc(s_vte, 1)
            act.wait_ge(s_vt, 4)
            for k in range(2):
                to = chain_pen[:, k, :].rearrange("p (g v) -> p g v", v=GV)
                act.activation(to[:, :, ::-1] if k else to, bank[4 + k][0:H, 0:VISITS].rearrange("p (g v) -> p g v", v=GV),
                               ACT.Copy, scale=BIG).then_inc(s_vte, 1)
            act.wait_ge(s_vt, 5)
            act.activation(first_lid[:, :], sm[0:H, 256:256 + GROUPS], ACT.Copy).then_inc(s_vte, 1)

            def square(s, source):
                for c in range(BLOCKS // LN_CHUNK):
                    b = slice(LN_CHUNK * c, LN_CHUNK * c + LN_CHUNK)
                    wait(act, s["xc"], c + 1)
                    act.activation(work2[:, b, :], source[:, b, :], ACT.Square).then_inc(s.sem["sq"], 1)
                wait(act, s["var"], 1)
                act.activation(st[:, 3, :], st[:, 2, :], ACT.Sqrt).then_inc(s.sem["std"], 1)

            square(L[0], hn)
            act.wait_ge(s_wps, 2)
            act.activation(WA[:, 0:F], sm[:, 0:F], ACT.Copy).then_inc(s_wc, 1)
            act.activation(WA[:, F:F + 2 * H], sm[:, F:F + 2 * H], ACT.Copy).then_inc(s_wc, 1)

            def transposed(s, n, nb, used, count):
                wait(act, s["hT_ps"], n + 1)
                wait(act, used, count)
                act.activation(HT[:, n % 2, 0:nb * BN], tp[n % 2][:, 0:nb * BN], ACT.Copy).then_inc(s.sem["hT"], 1)

            for n, (b0, nb) in enumerate(CHUNKS):
                transposed(L[0], n, nb, L[0]["feat"], n - 1)
                wait(act, L[0]["feat"], n + 1)
                act.activation(h0[:, b0:b0 + nb, :],
                               ex[n % 2][0:BN, 0:nb * (F + 2 * H)].rearrange("p (b f) -> p b f", b=nb)[:, :, 0:W0],
                               ACT.Copy).then_inc(L[0].sem["feat_out"], 1)
                act.activation(nd[:, b0:b0 + nb, 0:H],
                               ex[n % 2][0:BN, 0:nb * (F + 2 * H)].rearrange("p (b f) -> p b f", b=nb)[:, :, W0:W0 + H],
                               ACT.Copy).then_inc(L[0].sem["feat_done"], 1)
            for c in range(-(-GROUPS // 3)):
                ng = min(3, GROUPS - 3 * c)
                act.wait_ge(s_pent, c + 1)
                wait(act, s_penfree, c - 1)
                act.activation(prod[:, c % 2, 0:ng * (P + 2)], ms[c % 2][:, 0:ng * (P + 2)], ACT.Copy,
                               scale=BIG).then_inc(s_pene, 1)

            def layer(n):
                s = L[n]

                pen_f = pen[:, :, :].rearrange("p g e -> p (g e)")

                def evac(g, j):
                    wait(act, s["t_done"], 4 * g + j + 1)
                    wait(act, s["expanded"], 4 * (g - 1) + j + 1)
                    act.activation(ST[:, QV * j:QV * j + QV, :],
                                   tp[j % 2][0:BN, :].rearrange("p (v e) -> p v e", v=QV), ACT.Copy).then_inc(s.sem["st_ready"], 1)

                def step(g, u, i, new, old):
                    q = g - 1
                    if old and n == 0:
                        wait(act, s["scoreT"], q + 1)
                        wait(act, s["dd_ready"], 2 * q)
                        act.activation(esT[:, :], sT[:, P:2 * P], ACT.Copy).then_inc(s.sem["esT_ready"], 1)
                    if new:
                        for j in range(3):
                            evac(g, j)
                    if old:
                        wait(act, s["dd_ready"], (2 - n) * (q + 1))
                        wait(act, s["pT"], q)
                        k = 2 - n
                        act.activation(EP[:, 0:k, :], DD[:, 0:k, :], ACT.Exp).then_inc(s.sem["p_ready"], 1)
                        wait(act, s["pT"], q + 1)
                        wait(act, s["mm_done"], GV * q)
                        act.activation(PV[:, :, :, DH:DH + k].rearrange("p v h k -> p (v h) k"),
                                       sT[:, 2 * P:(2 + k) * P].rearrange("p (k c) -> p c k", k=k), ACT.Copy).then_inc(s.sem["pcols"], 1)
                        wait(act, s["al_mm"], q + 1)
                        wait(act, s["rescaled"], q)
                        act.activation(AL[:, :], sm[0:BN, 128:128 + H], ACT.Exp).then_inc(s.sem["al_ready"], 1)
                    if new:
                        evac(g, 3)
                        if n == 0:
                            wait(act, s["expanded"], 4 * g + 4)
                            wait(act, s["scoreT"], g)
                            wait(act, s["score_parts"], g)
                            act.activation(es[:, :, :, :], ex[0][:, 0:GV * 2 * H].rearrange("p (v k h) -> p k v h", k=2, h=H), ACT.Copy).then_inc(s.sem["es_ready"], 1)
                            wait(act, a_T, g + 1)
                            wait(act, a_mm, g)
                            act.activation(attrT[:, :], ex[1][:, :], ACT.Copy).then_inc(a_Te, 1)
                            wait(act, a_mm, g + 1)
                            act.activation(eb_nat[:, bass.ds(g * (ATTR_C * H), ATTR_C * H)], sm[:, 256:256 + ATTR_C * H],
                                           ACT.Copy).then_inc(a_out, 1)
                        wait(act, s["m_done"], g - 1)
                        if n == 0:
                            wait(act, s["ps_ready"], g - 1)
                        act.activation(pcur[:, u % 2, :], pen_f[:, bass.ds(g * (P + 1), P + 1)], ACT.Copy).then_inc(s.sem["pcur_ready"], 1)
                        for j in range(GV // QV):
                            act.wait_ge(s_gath[0][u][j], 64 * (i + 1 + n * (GROUPS // UNROLL)))
                        act.activation(idx_stage[:, u, :], idx_all[:, bass.ds((g + UNROLL) * GV, GV)], ACT.Copy).then_inc(s.sem["idx_staged"], 1)

                run_groups(act, step)

            act.wait_ge(s_penfree, -(-GROUPS // 3))
            layer(0)
            wait(act, L[0]["idx_staged"], GROUPS)
            act.activation(idx_stage[:, :, :].rearrange("p u v -> p (u v)"), idx_all[:, 0:UNROLL * GV], ACT.Copy).then_inc(s_idx0, 1)
            square(L[1], hn)
            for n, (b0, nb) in enumerate(CHUNKS):
                transposed(L[1], n, nb, L[1]["feat_done"], CHUNKS[n - 1][0] if n else 0)
            for h in range(H):
                act.wait_ge(s_ebt, VK * (h + 1))
                act.activation(ebias[:, :, h], ms[h % 2][:, 0:VISITS], ACT.Copy).then_inc(s_ebe, 1)
            layer(1)
            for n, (b0, nb) in enumerate(CHUNKS):
                act.wait_ge(s_fT, n + 1)
                wait(act, s_fo, n - 1)
                act.activation(HT[:, n % 2, 0:nb * BN], tp[n % 2][:, 0:nb * BN], ACT.Copy).then_inc(s_fTe, 1)
            square(F_, work)

        @block.tensor
        def _(pe):
            regs = [pe.alloc_register(f"pe_off{k}") for k in range(GV)]
            t4 = TILES // QV
            pe.wait_ge(s_const, 2)
            pe.wait_ge(s_fl, 1)
            for w in range(2):
                for k in range(QV):
                    last = pe.matmul(bank[w][0:BLOCKS - 1, k:TILES:QV], FLB_[:, w * QV + k, :], ident[0:t4, 0:t4], start=True, stop=True)
            last.then_inc(s_flT, 1)
            pe.wait_ge(s_ge, 1)
            pe.matmul(bank[2][0:VP, 0:TILES], ones[0:BLOCKS - 1, 0:VP], ge[:, 1, :], start=True, stop=True).then_inc(s_diff, 1)
            pe.wait_ge(s_watt, 1)
            pe.transpose(sm[:, 0:F], w0n[:, :], ident[:, :]).then_inc(s_wps, 1)
            pe.matmul(sm[:, F:F + 2 * H], w0n[:, :], attblk[:, :], start=True, stop=True).then_inc(s_wps, 1)
            pe.wait_ge(s_rowsf, 1)
            iv = ident[0:VP, 0:VP]
            for k in range(VK):
                last = pe.transpose(tp[0][:, VP * k:VP * k + VP], rows_f[:, k, 0:P], iv)
            last.then_inc(s_vt, 1)
            pe.wait_ge(s_vlid, 1)
            for k in range(VK):
                last = pe.transpose(tp[1][:, VP * k:VP * k + VP], lid_v[:, k, :], iv)
            last.then_inc(s_vt, 1)
            for k in range(VK):
                last = pe.matmul(ex[0][0:1, VP * k:VP * k + VP], vstat[:, 5, k:k + 1], iv, start=True, stop=True)
            last.then_inc(s_vt, 1)
            for m in range(2):
                for k in range(VK):
                    last = pe.matmul(bank[4 + m][0:H, VP * k:VP * k + VP],
                                     chain_b[:, m, k, :], iv, start=True, stop=True)
            last.then_inc(s_vt, 1)
            pe.wait_ge(s_vte, 2)
            pe.matmul(sm[0:H, 256:256 + GROUPS], E0[:, :], lid[:, 0:VISITS:GV], start=True, stop=True).then_inc(s_vt, 1)

            def transposes(s, n, b0, nb):
                wait(pe, s["hn"], (b0 + nb - 1) // LN_CHUNK + 1)
                wait(pe, s["hT"], n - 1)
                for k in range(nb):
                    last = pe.transpose(tp[n % 2][:, k * BN:k * BN + BN], hn[:, b0 + k, :], ident[0:BN, 0:BN])
                last.then_inc(s.sem["hT_ps"], 1)

            pe.wait_ge(s_vte, 5)
            for n, (b0, nb) in enumerate(CHUNKS):
                transposes(L[0], n, b0, nb)
                wait(pe, L[0]["hT"], n + 1)
                wait(pe, L[0]["feat_out"], n - 1)
                wait(pe, L[0]["feat_done"], n - 1)
                for k in range(nb):
                    last = pe.matmul(ex[n % 2][0:BN, k * (F + 2 * H):(k + 1) * (F + 2 * H)], HT[:, n % 2, k * BN:k * BN + BN],
                                     WA[:, :], start=True, stop=True)
                last.then_inc(L[0].sem["feat"], 1)
            pe.wait_ge(s_const, 3)
            pe.wait_ge(s_vte, 7)
            for c in range(-(-GROUPS // 3)):
                wait(pe, s_pene, c - 1)
                for g in range(3 * c, min(3 * c + 3, GROUPS)):
                    last = pe.matmul(ms[c % 2][:, (g % 3) * (P + 2):(g % 3 + 1) * (P + 2)],
                                     Rep[:, g % GK, :], rows_f[:, g // GK, P:ROW],
                                     start=True, stop=True)
                last.then_inc(s_pent, 1)

            def layer(n):
                s = L[n]
                width = F if n else 2 * H
                nodes = (q_sb if n else nd[:, :, :]).rearrange("p b f -> p (b f)")

                def one_hot_T(g, u, j):
                    wait(pe, s["S_ready"], 4 * g + j + 1)
                    wait(pe, s["st_ready"], 4 * g + j - 1)
                    for k in range(QV):
                        last = pe.transpose(tp[j % 2][0:BN, k * P:k * P + P], S[:, u % 2, QV * j + k, :], ident[:, :])
                    last.then_inc(s.sem["t_done"], 1)

                def expand(g, j):
                    wait(pe, s["st_ready"], 4 * g + j + 1)
                    if n:
                        wait(pe, s["qk_done"], 4 * g + j - 1)
                    elif j == 0:
                        wait(pe, s["es_ready"], g)
                    for k in range(QV):
                        v = QV * j + k
                        o = ex[j % 2][:, k * F:k * F + F] if n else ex[0][:, v * 2 * H:(v + 1) * 2 * H]
                        off = pe.snap(regs[v], min_val=0, max_val=(BLOCKS - 1) * width)
                        last = pe.matmul(o, ST[:, v, :], nodes[:, bass.ds(off, width)], start=True, stop=True)
                    last.then_inc(s.sem["expanded"], 1)

                def step(g, u, i, new, old):
                    q = g - 1
                    if old:
                        wait(pe, s["scores_ready"], q + 1)
                        wait(pe, s["pcols"], q)
                        wait(pe, s["dd_ready"], (2 - n) * q)
                        if n == 0:
                            wait(pe, s["es_ready"], q + 1)
                            wait(pe, s["esT_ready"], q)
                            pe.transpose(sT[:, P:2 * P], es[:, 1, :, :].rearrange("p v h -> p (v h)"), ident[:, :])
                        pe.transpose(sT[:, 0:P], sc[:, :, :].rearrange("p v h -> p (v h)"), ident[:, :]).then_inc(s.sem["scoreT"], 1)
                    if new:
                        pe.load(regs, offs[1 if n else 2][:, bass.ds(g * GV, GV)])
                        one_hot_T(g, u, 0)
                    if old:
                        wait(pe, s["rh_ready"], q + 1)
                        wait(pe, s["x_done"], q)
                        wait(pe, s["al_ready"], q)
                        if n == 0:
                            wait(pe, a_out, q + 1)
                        wait(pe, s["u_done"], q)
                        pe.matmul(sm[0:H, 0:2 * GV], Hsel[:, :], RH[:, :, :].rearrange("p k v -> p (k v)"),
                                  start=True, stop=True).then_inc(s.sem["hop1"], 1)
                    if new:
                        one_hot_T(g, u, 1)
                        expand(g, 0)
                    if old:
                        wait(pe, s["x_done"], q + 1)
                        wait(pe, s["u_done"], q + 1)
                        wait(pe, s["carry"], q + 1)
                        wait(pe, s["cc_mul"], q)
                        d = D[:, (u + 1) % 2, :, :]
                        for k in range(2):
                            last = pe.matmul(sm[:, 64 + GV * k:64 + GV * k + GV], HselT[:, :, :].rearrange("p v h -> p (v h)"),
                                             d[:, k, k:k + GV], start=True, stop=True)
                        last.then_inc(s.sem["hop2"], 1)
                    if new:
                        one_hot_T(g, u, 2)
                        expand(g, 1)
                    if old:
                        if n == 0:
                            wait(pe, s["ps_ready"], q + 1)
                        else:
                            wait(pe, s["p_ready"], q + 1)
                        wait(pe, s["pv_ready"], 4 * q)
                        wait(pe, s["pcols"], q)
                        if n == 0:
                            pe.transpose(sT[:, 3 * P:4 * P], PS[:, :], ident[:, :])
                        pe.transpose(sT[:, 2 * P:3 * P], EP[:, 0, :], ident[:, :]).then_inc(s.sem["pT"], 1)
                        wait(pe, s["r8_ready"], q + 1)
                        wait(pe, s["ohf_ready"], q + 1)
                        wait(pe, s["al_ready"], q)
                        pe.matmul(sm[0:BN, 128:128 + H], OHF[:, :], R8[:, :], start=True, stop=True).then_inc(s.sem["al_mm"], 1)
                    if new:
                        one_hot_T(g, u, 3)
                    if old:
                        wait(pe, s["pcols"], q + 1)
                        for v in range(GV):
                            if v % QV == 0:
                                wait(pe, s["pv_ready"], 4 * q + v // QV + 1)
                            if v % 2 == 0:
                                wait(pe, s["acc_added"], GV * q + v - 2)
                            o = ms[v % 4 // 2][0:BN, (v % 2) * 256:(v % 2) * 256 + H * SLOT]
                            pe.matmul(o, S[:, (u + 1) % 2, v, :], PV[:, v, :, :].rearrange("p h k -> p (h k)"),
                                      start=True, stop=True).then_inc(s.sem["mm_done"], 1)
                    if new:
                        expand(g, 2)
                        expand(g, 3)
                        if n == 0:
                            pe.wait_ge(s_attr[u % 2], 48 * (2 * i + u // 2 + 1))
                            wait(pe, a_Te, g)
                            for k in range(QV):
                                last = pe.transpose(ex[1][:, k * P:k * P + P], attr_in[:, u % 2, k * P:k * P + P], ident[:, :])
                            last.then_inc(a_T, 1)
                            wait(pe, a_Te, g + 1)
                            wait(pe, a_out, g)
                            wait(pe, s["al_ready"], g)
                            for k in range(QV):
                                last = pe.matmul(sm[:, 256 + 32 * k:256 + 32 * k + 32], attrT[:, k * P:k * P + P],
                                                 WeBD[:, :, :].rearrange("p c h -> p (c h)"), start=True, stop=True)
                            last.then_inc(a_mm, 1)

                run_groups(pe, step)

            pe.wait_ge(s_w, 19 * 16)
            wait(pe, L[0]["feat_done"], len(CHUNKS) + 1)
            layer(0)
            m = 0
            for n, (b0, nb) in enumerate(CHUNKS):
                transposes(L[1], n, b0, nb)
                wait(pe, L[1]["hT"], n + 1)
                for k in range(nb):
                    wait(pe, L[1]["feat_out"], m - 1)
                    pe.matmul(ex[m % 2][0:BN, 0:3 * F], HT[:, n % 2, k * BN:k * BN + BN], Wqkv[:, :],
                              start=True, stop=True).then_inc(L[1].sem["feat_done"], 1)
                    m += 1
            pe.wait_ge(s_ebin, 16 * VK)
            for h in range(H):
                wait(pe, s_ebe, h - 1)
                for k in range(VK):
                    pe.transpose(ms[h % 2][:, VP * k:VP * k + VP], bias_v[:, k, :, h], ident[0:VP, 0:VP]).then_inc(s_ebt, 1)
            wait(pe, L[1]["feat_out"], BLOCKS)
            layer(1)
            for n, (b0, nb) in enumerate(CHUNKS):
                pe.wait_ge(s_fin_on, 1)
                wait(pe, s_fTe, n - 1)
                for k in range(nb):
                    last = pe.transpose(tp[n % 2][:, k * BN:k * BN + BN], work2[:, b0 + k, :], ident[0:BN, 0:BN])
                last.then_inc(s_fT, 1)
                pe.wait_ge(s_fTe, n + 1)
                wait(pe, s_fh, n - 1)
                for k in range(nb):
                    last = pe.matmul(ex[n % 2][0:BN, k * F:k * F + F], HT[:, n % 2, k * BN:k * BN + BN], Wo[:, :],
                                     start=True, stop=True)
                last.then_inc(s_fo, 1)

        @block.vector
        def _(ve):
            n_v = [0]

            def then(ins):
                n_v[0] += 1
                ins.then_inc(s_v, 1)
                ve.wait_ge(s_v, n_v[0])

            regs = [ve.alloc_register(f"ve_off{k}") for k in range(GV)]
            then(ve.memset(WeBD[:, :, :], 0.0))
            ve.memset(idx_all[:, VISITS:], 0).then_inc(s_v, 1)
            ve.memset(D[:, :, :, :], LOW).then_inc(s_v, 1)
            ve.memset(PV[:, :, :, :], 0.0).then_inc(s_v, 1)
            n_v[0] += 3
            then(ve.memset(acc[:, :, :], 0.0))
            ve.wait_ge(s_const, 2)
            ve.tensor_copy(iota_n[:, :], iota_i[:, :]).then_inc(s_v, 1)
            ve.tensor_copy(thr_row[:, :], thr_i[:, :]).then_inc(s_v, 1)
            ve.tensor_copy(vcol[:, :], vcol_i[:, 0:VK]).then_inc(s_v, 1)
            n_v[0] += 3
            then(ve.tensor_copy(thr_col[0:BLOCKS - 1, :], vcol_i[0:BLOCKS - 1, VK:VK + 1]))
            ve.wait_ge(s_dst, 48)
            then(ve.tensor_copy(FL[:, :, :], dst_nat[:, :].rearrange("p (k c) -> p c k", k=QV)[:, ::P - 1, :]))
            t4 = TILES // QV
            ve.tensor_copy(FLB_,
                           FL[:, :, :].rearrange("p w k -> p (w k)").unsqueeze(2).to_broadcast([t4, 2 * QV, BLOCKS - 1])
                           ).then_inc(s_fl, 1)
            ve.wait_ge(s_flT, 1)
            then(ve.tensor_scalar(ge[:, 0, :], bank[1][0:BLOCKS - 1, 0:TILES], thr_col[0:BLOCKS - 1, :], None, op0=ALU.is_ge))
            ve.scalar_tensor_tensor(ge[:, 1, :], bank[0][0:BLOCKS - 1, 0:TILES], thr_col[0:BLOCKS - 1, :], ge[:, 0, :],
                                    op0=ALU.is_lt, op1=ALU.mult).then_inc(s_ge, 1)
            ve.memset(vtmp[:, 0, :], 1.0).then_inc(s_v, 1)
            n_v[0] += 1
            ve.wait_ge(s_v, n_v[0])
            ve.wait_ge(s_diff, 1)
            then(ve.tensor_tensor_scan(vend[:, :], vtmp[:, 0, :], bank[2][0:VP, 0:TILES], 0.0, ALU.add, ALU.add))
            for k in range(VK):
                then(ve.scalar_tensor_tensor(vtmp[:, 1, :], vend[:, :], vcol[:, k:k + 1], vend[:, :], op0=ALU.is_le, op1=ALU.mult))
                ve.tensor_reduce(vstat[:, 1, k:k + 1], vtmp[:, 1, :], AX.X, ALU.max).then_inc(s_v, 1)
                n_v[0] += 1
                then(ve.tensor_scalar(vtmp[:, 0, :], vend[:, :], vcol[:, k:k + 1], None, op0=ALU.is_le))
                then(ve.tensor_reduce(vstat[:, 0, k:k + 1], vtmp[:, 0, :], AX.X, ALU.add))
            ve.tensor_copy(tidx[:, :], vstat[:, 0, :]).then_inc(s_tidx, 1)

            ve.wait_ge(s_w, 19 * 16)
            ve.wait_ge(s_const, 3)
            for k in range(2):
                ve.tensor_scalar(attblk[:, k * H:k * H + H], headmask[:, :], attc[:, k:k + 1], None, op0=ALU.mult).then_inc(s_v, 1)
            n_v[0] += 2
            ve.wait_ge(s_v, n_v[0])
            ve.sem_inc(s_watt, 1)
            then(ve.tensor_reduce(Hsel[:, :], ident[:, :].rearrange("p (v h) -> p h v", h=H), AX.X, ALU.add))
            then(ve.tensor_scalar(Wqkv[:, 0:F], Wqkv[:, 0:F], DH ** -0.5, None, op0=ALU.mult))
            then(ve.tensor_scalar(rowv[:, 1, :], rowv[:, 1, :], DH ** -0.5, None, op0=ALU.mult))

            def layernorm(s, source, to, relu):
                for c in range(BLOCKS // LN_CHUNK):
                    b = slice(LN_CHUNK * c, LN_CHUNK * c + LN_CHUNK)
                    then(ve.tensor_reduce(st[:, 0, b], source[:, b, :], AX.X, ALU.add))
                    then(ve.tensor_scalar(st[:, 1, b], st[:, 0, b], 1.0 / F, None, op0=ALU.mult))
                    ve.tensor_tensor(to[:, b, :], source[:, b, :], st[:, 1, b].unsqueeze(2).to_broadcast([BN, LN_CHUNK, F]),
                                     ALU.subtract).then_inc(s.sem["xc"], 1)
                for c in range(BLOCKS // LN_CHUNK):
                    b = slice(LN_CHUNK * c, LN_CHUNK * c + LN_CHUNK)
                    wait(ve, s["sq"], c + 1)
                    then(ve.tensor_reduce(st[:, 0, b], work2[:, b, :], AX.X, ALU.add))
                ve.tensor_scalar(st[:, 2, :], st[:, 0, :], 1.0 / F, 1e-5, op0=ALU.mult, op1=ALU.add).then_inc(s.sem["var"], 1)
                wait(ve, s["std"], 1)
                then(ve.reciprocal(st[:, 4, :], st[:, 3, :]))
                for c in range(BLOCKS // LN_CHUNK):
                    b = slice(LN_CHUNK * c, LN_CHUNK * c + LN_CHUNK)
                    r = st[:, 4, b].unsqueeze(2).to_broadcast([BN, LN_CHUNK, F])
                    if relu:
                        ve.scalar_tensor_tensor(to[:, b, :], to[:, b, :], 0.0, r, op0=ALU.max, op1=ALU.mult).then_inc(s.sem["hn"], 1)
                    else:
                        ve.tensor_tensor(to[:, b, :], to[:, b, :], r, ALU.mult).then_inc(s.sem["hn"], 1)
                wait(ve, s["hn"], BLOCKS // LN_CHUNK)

            ve.wait_ge(s_rows, 16 * VK)
            ve.tensor_copy(rows_f[:, :, :], rows_i[:, :, :]).then_inc(s_rowsf, 1)
            ve.wait_ge(s_rowsf, 1)
            then(ve.tensor_tensor(cmpb[:, :, :], rows_f[:, :, P + 1:P + 2].to_broadcast([VP, VK, BLOCKS - 1]),
                                  thr_row[0:VP, :].unsqueeze(1).to_broadcast([VP, VK, BLOCKS - 1]), ALU.is_ge))
            then(ve.tensor_reduce(vstat[:, 2, :], cmpb[:, :, :], AX.X, ALU.add))
            then(ve.tensor_tensor(vstat[:, 3, :], vcol[:, :], vstat[:, 1, :], ALU.subtract))
            then(ve.tensor_tensor(vstat[:, 4, :], vstat[:, 3, :], vstat[:, 2, :], ALU.add))
            then(ve.tensor_scalar(vstat[:, 5, :], vstat[:, 4, :], float(BLOCKS - 1), None, op0=ALU.min))
            then(ve.tensor_scalar(vstat[:, 6, :], vstat[:, 5, :], float(BN), None, op0=ALU.mult))
            then(ve.tensor_tensor(vstat[:, 7, :], rows_f[:, :, P], rows_f[:, :, 2 * P], ALU.subtract))
            then(ve.tensor_tensor(vstat[:, 8, :], rows_f[:, :, P + 1], rows_f[:, :, 2 * P + 1], ALU.subtract))
            ve.tensor_copy(chain_b[:, :, :, :].rearrange("p m k h -> p (m k) h"),
                           vstat[:, 7:9, :].rearrange("p m k -> p (m k)").unsqueeze(2).to_broadcast([VP, 2 * VK, H])
                           ).then_inc(s_v, 1)
            n_v[0] += 1
            then(ve.tensor_tensor(lid_v[:, :, :], rows_f[:, :, P + 1:2 * P + 1],
                                  vstat[:, 6, :].unsqueeze(2).to_broadcast([VP, VK, P]), ALU.subtract))
            ve.sem_inc(s_vlid, 1)
            ve.wait_ge(s_x, 16)
            layernorm(L[0], xs, hn, True)
            wait(ve, L[0]["feat_out"], len(CHUNKS))
            wait(ve, L[0]["feat_done"], len(CHUNKS))
            then(ve.tensor_tensor(nst[:, 0, :, :], h0[:, :, F:W0], nd[:, :, 0:H], ALU.add))
            ve.scalar_tensor_tensor(nd[:, :, H:2 * H], nst[:, 0, :, :], SLOPE, nst[:, 0, :, :], op0=ALU.mult,
                                    op1=ALU.max).then_inc(L[0].sem["feat_done"], 1)
            for c in range(-(-GROUPS // 3)):
                ng = min(3, GROUPS - 3 * c)
                ve.wait_ge(s_pene, c + 1)
                d = prod[:, c % 2, 0:ng * (P + 2)].rearrange("p (g e) -> p g e", g=ng)
                ve.tensor_tensor(pen[:, 3 * c:3 * c + ng, :], d[:, :, 0:P + 1], d[:, :, 1:P + 2], ALU.subtract).then_inc(s_penfree, 1)
            ve.wait_ge(s_penfree, -(-GROUPS // 3))
            ve.wait_ge(s_vte, 8)
            ve.wait_ge(s_bz, 16)

            def layer(n):
                s = L[n]
                k = 2 - n
                acc_f = acc[:, :, :].rearrange("p b f -> p (b f)")

                def one_hot(g, u, j):
                    wait(ve, s["mm_done"], GV * (g - 1))
                    ve.tensor_tensor(S[:, u % 2, QV * j:QV * j + QV, :],
                                     iota_n[:, 0:BN].unsqueeze(1).to_broadcast([P, QV, BN]),
                                     lid[:, bass.ds(g * GV + QV * j, QV)].unsqueeze(2).to_broadcast([P, QV, BN]),
                                     ALU.is_equal).then_inc(s.sem["S_ready"], 1)

                def step(g, u, i, new, old):
                    q = g - 1
                    uq = (u - 1) % UNROLL
                    gi = n * (GROUPS // UNROLL)
                    if new:
                        one_hot(g, u, 0)
                    if old:
                        score = sT[:, 0:P] if n else smax[:, :]
                        p0 = pcur[:, (u + 1) % 2, 0:P]
                        p1 = pcur[:, (u + 1) % 2, 1:P + 1]
                        wait(ve, s["pcur_ready"], q + 1)
                        wait(ve, s["scoreT"], q + 1)
                        if n == 0:
                            wait(ve, s["esT_ready"], q + 1)
                            wait(ve, s["f_done"], q)
                            ve.tensor_tensor(smax[:, :], sT[:, 0:P], esT[:, :], ALU.max).then_inc(s.sem["smax_ready"], 1)
                            wait(ve, s["smax_ready"], q + 1)
                        wait(ve, s["rh_ready"], q)
                        ve.tensor_tensor_scan(FR[:, 0, :], p0, score, LOW, ALU.add, ALU.max).then_inc(s.sem["edge_scans"], 1)
                        ve.tensor_tensor_scan(FR[:, 1, :], p1[:, ::-1], score[:, ::-1], LOW, ALU.add, ALU.max).then_inc(s.sem["edge_scans"], 1)
                        wait(ve, s["edge_scans"], 2 * q + 2)
                        wait(ve, s["hop1"], q)
                        ve.tensor_tensor(RH[:, :, :], Vsel[:, :].unsqueeze(1).to_broadcast([P, 2, GV]),
                                         FR[:, :, P - 1:P].to_broadcast([P, 2, GV]), ALU.mult).then_inc(s.sem["rh_ready"], 1)
                    if new:
                        one_hot(g, u, 1)
                    if old:
                        d = D[:, (u + 1) % 2, :, :]
                        e = D[:, u % 2, :, :]
                        wait(ve, s["hop1"], q + 1)
                        wait(ve, s["carry"], q)
                        wait(ve, s["hop2"], q)
                        ve.tensor_tensor_scan(d[:, 0, 1:GV + 1], chain_pen[:, 0, bass.ds(q * GV, GV)], sm[0:H, 0:GV],
                                              d[:, 0, 0:1], ALU.add, ALU.max).then_inc(s.sem["x_done"], 1)
                        ve.tensor_tensor_scan(d[:, 1, GV - 1::-1], chain_pen[:, 1, bass.ds(q * GV, GV)],
                                              sm[0:H, GV:2 * GV][:, ::-1], LOW, ALU.add, ALU.max).then_inc(s.sem["u_done"], 1)
                        wait(ve, s["x_done"], q + 1)
                        ve.tensor_copy(e[:, 0, 0:1], d[:, 0, GV:GV + 1]).then_inc(s.sem["carry"], 1)
                    if new:
                        one_hot(g, u, 2)
                    if old:
                        wait(ve, s["hop2"], q + 1)
                        ve.tensor_tensor(CCM[:, :, :], sm[:, 64:64 + 2 * GV].rearrange("p (k v) -> p k v", k=2),
                                         Vsel[:, :].unsqueeze(1).to_broadcast([P, 2, GV]), ALU.mult).then_inc(s.sem["cc_mul"], 1)
                        wait(ve, s["cc_mul"], q + 1)
                        wait(ve, s["df"], 2 * q)
                        ve.tensor_reduce(CC[:, :], CCM[:, :, :], AX.X, ALU.add).then_inc(s.sem["cc_done"], 1)
                        wait(ve, s["cc_done"], q + 1)
                        wait(ve, s["m_done"], q)
                        ve.tensor_tensor_scan(FF[:, :], p0, score, CC[:, 0:1], ALU.add, ALU.max).then_inc(s.sem["f_done"], 1)
                        wait(ve, s["f_done"], q + 1)
                        ve.tensor_tensor_scan(MM[:, ::-1], p1[:, ::-1], FF[:, ::-1], CC[:, 1:2], ALU.add, ALU.max).then_inc(s.sem["m_done"], 1)
                        wait(ve, s["m_done"], q + 1)
                        wait(ve, s["p_ready"], q)
                        if n == 0:
                            ve.tensor_tensor(DD[:, 1, :], esT[:, :], MM[:, :], ALU.subtract).then_inc(s.sem["dd_ready"], 1)
                        ve.tensor_tensor(DD[:, 0, :], sT[:, 0:P], MM[:, :], ALU.subtract).then_inc(s.sem["dd_ready"], 1)
                        wait(ve, s["al_mm"], q)
                        wait(ve, s["r8_ready"], q)
                        ve.tensor_tensor(DF[:, 0:1], CC[0:H, 0:1], MM[0:H, 0:1], ALU.subtract).then_inc(s.sem["df"], 1)
                        ve.tensor_scalar(OHF[:, :], iota_n[0:H, 0:BN], first_lid[:, bass.ds(q, 1)], None, op0=ALU.is_equal).then_inc(s.sem["ohf_ready"], 1)
                        wait(ve, s["df"], 2 * q + 1)
                        ve.tensor_scalar(DF[:, 1:2], DF[:, 0:1], 0.0, -200.0, op0=ALU.min, op1=ALU.max).then_inc(s.sem["df"], 1)
                        wait(ve, s["df"], 2 * q + 2)
                        ve.tensor_scalar(R8[:, :], ident[0:H, 0:H], DF[:, 1:2], None, op0=ALU.mult).then_inc(s.sem["r8_ready"], 1)
                        if n == 0:
                            wait(ve, s["p_ready"], q + 1)
                            wait(ve, s["pT"], q)
                            ve.scalar_tensor_tensor(PS[:, :], p0, 0.0, EP[:, 1, :], op0=ALU.is_lt, op1=ALU.mult).then_inc(s.sem["ps_ready"], 1)
                    if new:
                        one_hot(g, u, 3)
                    if old:
                        ve.load(regs, offs[0][:, bass.ds(q * GV, GV)])
                        off = [ve.snap(r, min_val=0, max_val=(BLOCKS - 1) * H * SLOT) for r in regs]
                        c0 = F if n else 0

                        def weigh(j):
                            wait(ve, s["mm_done"], GV * q)
                            rows = G[:, uq, QV * j:QV * j + QV, c0:c0 + F].rearrange("p v (h d) -> p v h d", h=H)
                            ve.tensor_tensor(PV[:, QV * j:QV * j + QV, :, 0:DH], rows,
                                             PV[:, QV * j:QV * j + QV, :, DH:DH + 1].to_broadcast([P, QV, H, DH]), ALU.mult).then_inc(s.sem["pv_ready"], 1)

                        wait(ve, s["pcols"], q + 1)
                        weigh(0)
                        weigh(1)
                        wait(ve, s["al_ready"], q + 1)
                        wait(ve, s["acc_added"], GV * q)
                        a = acc_f[:, bass.ds(off[0], H * SLOT)].rearrange("p (h k) -> p h k", h=H)
                        ve.tensor_tensor(a, a, AL[:, :].unsqueeze(2).to_broadcast([BN, H, SLOT]), ALU.mult).then_inc(s.sem["rescaled"], 1)
                        wait(ve, s["rescaled"], q + 1)
                        for v in range(GV):
                            if v in (2, 6):
                                weigh(2 + v // 4)
                            if v % 2 == 0:
                                wait(ve, s["mm_done"], GV * q + v + 2)
                            wait(ve, s["acc_added"], GV * q + v)
                            a = acc_f[:, bass.ds(off[v], H * SLOT)]
                            o = ms[v % 4 // 2][0:BN, (v % 2) * 256:(v % 2) * 256 + H * SLOT]
                            ve.tensor_tensor(a, a, o, ALU.add).then_inc(s.sem["acc_added"], 1)
                    if new:
                        for j in range(GV // QV):
                            ve.wait_ge(s_gath[0][u][j], 64 * (i + 1 + gi))
                        if n == 0:
                            wait(ve, s["es_ready"], g + 1)
                            wait(ve, s["scores_ready"], g)
                            ve.tensor_tensor(raw[:, :, :], es[:, 0, :, :],
                                             G[:, u, :, F:W0], ALU.add).then_inc(s.sem["score_parts"], 1)
                            wait(ve, s["score_parts"], g + 1)
                            wait(ve, s["scoreT"], g)
                            ve.scalar_tensor_tensor(sc[:, :, :], raw[:, :, :], SLOPE, raw[:, :, :], op0=ALU.mult,
                                                    op1=ALU.max).then_inc(s.sem["scores_ready"], 1)
                        else:
                            for j in range(GV // QV):
                                wait(ve, s["expanded"], 4 * g + j + 1)
                                wait(ve, s["score_parts"], 4 * g + j - 1)
                                ve.tensor_tensor(prod[:, j % 2, :].rearrange("p (v f) -> p v f", v=QV),
                                                 ex[j % 2][:, :].rearrange("p (v f) -> p v f", v=QV),
                                                 G[:, u, QV * j:QV * j + QV, 0:F], ALU.mult).then_inc(s.sem["qk_done"], 1)
                                wait(ve, s["qk_done"], 4 * g + j + 1)
                                wait(ve, s["scores_ready"], g)
                                ve.tensor_reduce(raw[:, QV * j:QV * j + QV, :].rearrange("p v h -> p (v h)"),
                                                 prod[:, j % 2, :].rearrange("p (c d) -> p c d", d=DH), AX.X,
                                                 ALU.add).then_inc(s.sem["score_parts"], 1)
                            wait(ve, s["score_parts"], 4 * g + 4)
                            wait(ve, s["scoreT"], g)
                            ve.tensor_tensor(sc[:, :, :].rearrange("p v h -> p (v h)"), raw[:, :, :].rearrange("p v h -> p (v h)"),
                                             ebias[:, :, :].rearrange("p v h -> p (v h)")[:, bass.ds(g * P, P)],
                                             ALU.add).then_inc(s.sem["scores_ready"], 1)

                run_groups(ve, step)
                wait(ve, s["acc_added"], GV * GROUPS)

            layer(0)
            ve.wait_ge(a_out, GROUPS)
            v3 = eb_nat[:, 0:TILES * H].rearrange("p (c h) -> p c h", h=H)
            ve.tensor_tensor(v3, v3, be_r[:, :].unsqueeze(1).to_broadcast([P, TILES, H]), ALU.add).then_inc(s_ebfin, 1)
            accs = acc[:, :, :].rearrange("p b (h k) -> p b h k", h=H)
            lsum, pself = accs[:, :, :, DH], accs[:, :, :, DH + 1]

            def bh(t):
                return t.unsqueeze(3).to_broadcast([BN, BLOCKS, H, DH])

            def flat(t):
                return t.rearrange("p b (h d) -> p b h d", d=DH)

            accm = accs[:, :, :, 0:DH]
            then(ve.tensor_tensor(nst[:, 0, :, :], lsum, pself, ALU.add))
            then(ve.tensor_scalar(nst[:, 1, :, :], nst[:, 0, :, :], 0.0, None, op0=ALU.is_equal))
            then(ve.tensor_tensor(nst[:, 2, :, :], nst[:, 1, :, :], pself, ALU.add))
            then(ve.tensor_tensor(nst[:, 3, :, :], nst[:, 1, :, :], nst[:, 0, :, :], ALU.add))
            then(ve.reciprocal(nst[:, 4, :, :], nst[:, 3, :, :]))
            then(ve.tensor_tensor(flat(work), flat(h0[:, :, 0:F]), bh(nst[:, 2, :, :]), ALU.mult))
            then(ve.tensor_tensor(flat(work), flat(work), accm, ALU.add))
            then(ve.tensor_tensor(flat(work), flat(work), bh(nst[:, 4, :, :]), ALU.mult))
            then(ve.tensor_tensor(work, work, xs[:, :, :], ALU.add))
            then(ve.tensor_tensor(xs[:, :, :], work, rowv[:, 0, :].unsqueeze(1).to_broadcast([BN, BLOCKS, F]), ALU.add))
            then(ve.memset(acc[:, :, :], 0.0))
            then(ve.memset(D[:, :, :, :], LOW))
            layernorm(L[1], xs, hn, True)
            ve.wait_ge(s_ebout, 16)
            for b in range(BLOCKS):
                wait(ve, L[1]["feat_done"], b + 1)
                then(ve.tensor_tensor(q_sb[:, b, :], ex[b % 2][0:BN, 0:F], rowv[:, 1, :], ALU.add))
                ve.tensor_tensor(kv[:, b, :], ex[b % 2][0:BN, F:3 * F], rowv[:, 2:4, :].rearrange("p k f -> p (k f)"),
                                 ALU.add).then_inc(L[1].sem["feat_out"], 1)
            ve.wait_ge(s_ebe, H)
            layer(1)
            then(ve.tensor_scalar(nst[:, 0, :, :], lsum, 1e-8, None, op0=ALU.add))
            then(ve.reciprocal(nst[:, 1, :, :], nst[:, 0, :, :]))
            ve.tensor_tensor(flat(work2), accm, bh(nst[:, 1, :, :]), ALU.mult).then_inc(s_fin_on, 1)
            then(ve.tensor_tensor(hn[:, :, :], hn[:, :, :], rowv[:, 4, :].unsqueeze(1).to_broadcast([BN, BLOCKS, F]), ALU.add))
            for n, (b0, nb) in enumerate(CHUNKS):
                ve.wait_ge(s_fo, n + 1)
                ve.tensor_tensor(hn[:, b0:b0 + nb, :], ex[n % 2][0:BN, 0:nb * F].rearrange("p (b f) -> p b f", b=nb),
                                 hn[:, b0:b0 + nb, :], ALU.add).then_inc(s_fh, 1)
            ve.wait_ge(s_fh, len(CHUNKS))
            layernorm(F_, hn, work, False)
            then(ve.tensor_tensor(work, work, rowv[:, 5, :].unsqueeze(1).to_broadcast([BN, BLOCKS, F]), ALU.mult))
            then(ve.tensor_tensor(work, work, rowv[:, 6, :].unsqueeze(1).to_broadcast([BN, BLOCKS, F]), ALU.add))
            ve.tensor_tensor(work, work, xs[:, :, :], ALU.add).then_inc(s_out, 1)


_INS = ['x', 'src', 'dst', 'edge_attr_32', 'L0_gnn_W', 'L0_gnn_att', 'L0_gnn_bias', 'L1_gnn_Wq', 'L1_gnn_bq',
        'L1_gnn_Wk', 'L1_gnn_bk', 'L1_gnn_Wv', 'L1_gnn_bv', 'L1_gnn_We', 'L1_gnn_be', 'L1_gnn_Wo', 'L1_gnn_bo',
        'L1_gnn_gamma', 'L1_gnn_beta']
_OUTS = [((3125, 128), 'float32')]


def kernel(**inputs):
    import numpy as _np
    import concourse.bacc as _bacc
    from concourse import mybir as _mybir
    from concourse.bass_utils import run_bass_kernel_spmd as _run

    nc = _bacc.Bacc("TRN2", target_bir_lowering=False, num_devices=1)
    arrays, args = {}, []
    for name in _INS:
        a = _np.ascontiguousarray(inputs[name])
        arrays[f"in_{name}_dram"] = a
        args.append(nc.dram_tensor(f"in_{name}_dram", a.shape, _mybir.dt.from_np(a.dtype), kind="ExternalInput").ap())
    for i, (shape, dtype) in enumerate(_OUTS):
        dt = _mybir.dt.from_np(_np.dtype(dtype))
        args.append(nc.dram_tensor(f"out_{i}_dram", shape, dt, kind="ExternalOutput").ap())
    gnn_kernel(nc, *args)
    r = _run(nc, [arrays], core_ids=[0])
    got = tuple(r.results[0][f"out_{i}_dram"] for i in range(len(_OUTS)))
    return got[0]
```

```python
from contextlib import ExitStack

import concourse.bass as bass
from concourse import mybir

F32 = mybir.dt.float32
BF16 = mybir.dt.bfloat16
I32 = mybir.dt.int32
ALU = mybir.AluOpType
ACT = mybir.ActivationFunctionType
AX = mybir.AxisListType

NODES, EDGES, F, ED, H = 3125, 53125, 128, 32, 8
DH = F // H
P = 128
BN = 125
BLOCKS = NODES // BN
TILES = -(-EDGES // P)
FULL = EDGES // P
REST = EDGES - FULL * P
GV = P // H
GROUPS = -(-(TILES + BLOCKS - 1) // GV)
VISITS = GROUPS * GV
UNROLL = 3
QV = 4
VP = 112
VK = VISITS // VP
GK = VP // GV
SLOT = DH + 2
W0 = F + H
W1 = 2 * F
ROW = 2 * P + 2
ATTR_C = 16
PAD_DST = 4000
BIG = float(2 ** 100)
LOW = -BIG
SLOPE = 0.2
CHUNKS = [(s, min(3, BLOCKS - s)) for s in range(0, BLOCKS, 3)]
LN_CHUNK = 5


class Signal:

    def __init__(self, s, base):
        self.s, self.base = s, base


def gnn_kernel(nc, x, src, dst, edge_attr, w0, att, bias0, wq, bq, wk, bk, wv, bv, we, be, wo, bo, gamma,
               beta, out):
    ctx = ExitStack()

    def sb(name, shape, dt=F32):
        return ctx.enter_context(nc.sbuf_tensor(name, shape, dt))

    def sem(name):
        return ctx.enter_context(nc.semaphore(name))

    def wait(eng, s, value):
        if not isinstance(value, int) or value > 0:
            if isinstance(s, Signal):
                eng.wait_ge(s.s, s.base + value)
            else:
                eng.wait_ge(s, value)

    with ctx:
        edge_rows = nc.dram_tensor("edge_rows", (TILES + 1, ROW), I32, kind="Internal").ap()
        bias_rows = nc.dram_tensor("bias_rows", (TILES + 1, P * H), F32, kind="Internal").ap()
        attr_tail = nc.dram_tensor("attr_tail", (GROUPS * ATTR_C, ED), F32, kind="Internal").ap()
        table0 = nc.dram_tensor("table0", (NODES, W0), F32, kind="Internal").ap()
        table1 = nc.dram_tensor("table1", (NODES, W1), F32, kind="Internal").ap()

        xs = sb("xs", [BN, BLOCKS, F])
        hn = sb("hn", [BN, BLOCKS, F])
        h0b = sb("h0b", [P, VISITS * H])
        h0 = h0b[0:BN, 0:BLOCKS * W0].rearrange("p (b f) -> p b f", f=W0)
        ebias = h0b[:, 0:VISITS * H].rearrange("p (v h) -> p v h", h=H)
        nd = sb("nd", [BN, BLOCKS, 2 * H])
        nd3 = sb("nd3", [BN, BLOCKS, 3, 2 * H], BF16)
        acc = sb("acc", [BN, BLOCKS, H * SLOT])
        qe = sb("qe", [P, VISITS * H])
        eb_nat = qe[:, 0:VISITS * H]
        q_sb = qe[0:BN, 0:BLOCKS * F].rearrange("p (b f) -> p b f", f=F)
        G = sb("G", [P, UNROLL, GV, W1])
        kv = G[0:BN, :, :, :].rearrange("p u v f -> p (u v f)")[:, 0:BLOCKS * W1].rearrange(
            "p (b f) -> p b f", f=W1)
        work = G[0:BN, :, :, :].rearrange("p u v f -> p (u v f)")[:, 0:BLOCKS * F].rearrange(
            "p (b f) -> p b f", f=F)
        work2 = G[0:BN, :, :, :].rearrange("p u v f -> p (u v f)")[:, BLOCKS * F:2 * BLOCKS * F].rearrange(
            "p (b f) -> p b f", f=F)
        bias_v = G[0:VP, :, :, :].rearrange("p u v f -> p (u v f)")[:, 8192:8192 + VK * P * H].rearrange(
            "p (k e h) -> p k e h", k=VK, h=H)
        rows_i = G[0:VP, :, :, :].rearrange("p u v f -> p (u v f)")[:, 0:VK * ROW].bitcast(I32).rearrange(
            "p (k r) -> p k r", k=VK)
        S = sb("S", [P, UNROLL, GV, BN])
        ST_ = sb("ST", [P, GV, P])
        ST = ST_[0:BN, :, :]
        ST_b = ST_[0:BN, :, :].rearrange("p v e -> p (v e)").bitcast(BF16)[:, 0:GV * P].rearrange("p (v e) -> p v e", v=GV)
        PV = sb("PV", [P, GV, H, SLOT])
        prod = sb("prod", [P, UNROLL, QV * F])
        attr_in = prod
        rows = sb("rows", [P, 2, VISITS])
        chain_pen = rows[0:H, :, :]
        offs = [rows[32 * k + 32:32 * k + 33, 0, :].bitcast(I32) for k in range(3)]

        def views(tensor, start, shapes):
            made, at = [], start
            for parts, shape, dt in shapes:
                size = 1
                for d in shape:
                    size *= d
                v = tensor[0:parts, at:at + size]
                if dt is not F32:
                    v = v.bitcast(dt)
                names = "abc"[:len(shape)]
                made.append(v.rearrange(f"p ({' '.join(names)}) -> p {' '.join(names)}", **dict(zip(names, shape)))
                            if len(shape) > 1 else v)
                at += size
            return made

        S_flat = S[:, :, :, :].rearrange("p k v n -> p (k v n)")
        dst_nat, ge, vend, vtmp, lid_v, FLB_, cmpb, iota_i = views(S_flat, 0, (
            (TILES // QV, (QV * P,), I32), (BLOCKS - 1, (2, TILES), F32), (VP, (TILES,), F32), (VP, (2, TILES), F32),
            (VP, (VK, P), F32), (TILES // QV, (2 * QV, BLOCKS - 1), F32), (VP, (VK, BLOCKS - 1), F32), (P, (P,), I32)))
        HT, Rep = views(ST_[:, :, :].rearrange("p v e -> p (v e)"), 0, (
            (P, (2, 3 * BN), F32), (VP, (GK, GV * H), F32)))
        nst_, rows_f = views(PV[:, :, :, :].rearrange("p v h k -> p (v h k)"), 0, (
            (BN, (6, BLOCKS * H), F32), (VP, (VK, ROW), F32)))
        nst = nst_.rearrange("p k (b h) -> p k b h", h=H)
        pen = sb("pen", [P, GROUPS, P + 1], BF16)
        pcur = sb("pcur", [P, UNROLL, P + 1], BF16)
        idx_all = sb("idx_all", [P, VISITS + UNROLL * GV], I32)
        idx_stage = sb("idx_stage", [P, UNROLL, GV], I32)
        lid = sb("lid", [P, VISITS])
        first_lid = sb("first_lid", [H, GROUPS])
        raw = sb("raw", [P, GV, H])
        sc = sb("sc", [P, GV, H])
        es = sb("es", [P, 2, GV, H])
        esT = sb("esT", [P, P])
        smax = sb("smax", [P, P])
        FR = sb("FR", [P, 2, P])
        RH = sb("RH", [P, 2, GV])
        D = sb("D", [H, UNROLL, 2, GV + 1])
        CCM = sb("CCM", [P, 2, GV])
        CC = sb("CC", [P, 2])
        FF = sb("FF", [P, P])
        MM = sb("MM", [P, P])
        DD = sb("DD", [P, 2, P])
        EP = sb("EP", [P, 2, P])
        PS = sb("PS", [P, P])
        DF = sb("DF", [H, 2])
        R8 = sb("R8", [H, H])
        OHF = sb("OHF", [H, BN])
        AL = sb("AL", [BN, H])
        attrT = sb("attrT", [P, QV * P])
        ident = sb("ident", [P, P])
        ones = sb("ones", [P, P])
        iota_n = sb("iota_n", [P, P])
        thr_row = sb("thr_row", [P, BLOCKS - 1])
        thr_i = sb("thr_i", [P, BLOCKS - 1], I32)
        thr_col = sb("thr_col", [P, 1])
        vcol = sb("vcol", [VP, VK])
        vcol_i = sb("vcol_i", [VP, VK + 1], I32)
        headmask = sb("headmask", [P, H])
        Vsel = sb("Vsel", [P, GV])
        HselT = sb("HselT", [H, GV, H])
        Hsel = sb("Hsel", [P, H])
        E0 = sb("E0", [P, H])
        pad_i = sb("pad_i", [1, 2, P + 2], I32)
        FL = sb("FL", [TILES // QV, 2, QV])
        vstat = sb("vstat", [VP, 10, VK])
        tidx = sb("tidx", [VP, VK], I32)
        chain_b = sb("chain_b", [VP, 2, VK, H])
        w0n = sb("w0n", [F, F])
        attc = sb("attc", [P, 2])
        attblk = sb("attblk", [P, 2 * H])
        WA = sb("WA", [P, F + 2 * H])
        Wqkv = sb("Wqkv", [P, 3 * F])
        Wo = sb("Wo", [P, F])
        WeBD = sb("WeBD", [P, QV, H])
        rowv = sb("rowv", [BN, 7, F])
        be_r = sb("be_r", [P, H])
        st = sb("st", [BN, 6, BLOCKS])

        bank = [ctx.enter_context(nc.psum_tensor(f"bank{i}", [P, 512], F32)) for i in range(8)]
        tp = bank[0:2]
        ex = bank[2:4]
        ms = bank[4:6]
        sT = bank[6]
        sm = bank[7]

        s_dst, s_x, s_w, s_pad, s_er, s_bz = (sem(n) for n in (
            "dst_in", "x_in", "weights_in", "pads_out", "edge_rows_out", "bias_pad_out"))
        s_tail = sem("attr_tail_out")
        s_attr = [sem(f"attr_in{k}") for k in range(UNROLL)]
        s_rows = sem("rows_in")
        s_const = sem("constants")
        s_pool = sem("pool_done")
        s_v = sem("vector_done")
        s_fl, s_flT, s_ge, s_diff = sem("firsts_lasts"), sem("firsts_lasts_rows"), sem("block_steps"), sem("steps_summed")
        s_tidx, s_rowsf, s_vlid = sem("tile_index"), sem("rows_as_float"), sem("visit_ids")
        s_vt, s_vte = sem("visit_transposes"), sem("visit_copies")
        s_pent, s_pene = sem("pen_spread"), sem("pen_copied")
        s_penfree = sem("pen_bank_free")
        s_idx0 = sem("first_indices")
        s_watt, s_wps, s_wc = sem("att_blocks"), sem("weights_products"), sem("weights_ready")
        s_tab = [sem("table0_out"), sem("table1_out")]
        s_ebout, s_ebin, s_ebt, s_ebe = sem("bias_rows_out"), sem("bias_rows_in"), sem("bias_transposed"), sem("bias_copied")
        s_ebfin = sem("bias_complete")
        s_out = sem("out_written")
        s_go = sem("quarters_gathered")

        NODE_SEMS = ("xc", "sq", "var", "std", "hn", "hT_ps", "hT", "feat", "feat_out", "feat_done")
        LOOP_SEMS = dict(S_ready=4, t_done=4, st_ready=4, expanded=4, qk_done=0, score_parts=1, scores_ready=1,
                         es_ready=1, scoreT=1, esT_ready=1, smax_ready=1, edge_scans=2, rh_ready=1, hop1=1, x_done=1,
                         carry=1, u_done=1, hop2=1, cc_mul=1, cc_done=1, f_done=1, m_done=1, dd_ready=2, p_ready=1,
                         ps_ready=1, pT=1, pcols=1, pv_ready=4, mm_done=GV, acc_added=GV, df=2, r8_ready=1,
                         ohf_ready=1, al_mm=1, al_ready=1, rescaled=1, idx_staged=1, pcur_ready=1)
        loop_sem = {k: sem(k) for k in LOOP_SEMS}

        class Layer:
            def __init__(self, n):
                self.sem = {k: sem(f"{k}_{n}") for k in NODE_SEMS} | loop_sem
                self.base = {k: (n == 1) * GROUPS * v for k, v in LOOP_SEMS.items()}

            def __getitem__(self, k):
                return Signal(self.sem[k], self.base.get(k, 0))

        L = [Layer(0), Layer(1)]
        s_gath = [[sem(f"gathered_{u}_{j}") for j in range(GV // QV)] for u in range(UNROLL)]
        a_T, a_Te, a_mm, a_out = sem("attrT_ps"), sem("attrT"), sem("bias_mm"), sem("bias_sb")
        s_fin_on, s_fT, s_fTe, s_fo, s_fh = (sem(n) for n in ("mean_msgs", "msgsT_ps", "msgsT", "projected", "projected_used"))
        X1 = sem("x1_ready")
        NODE_SEMS = NODE_SEMS[:5]
        F_ = Layer("f")

        NPOOL = 16
        block = ctx.enter_context(nc.Block())

        def gathered(n, u, i):
            return 16 * QV * (i + 1 + n * len(range(u, GROUPS, UNROLL)))

        def run_groups(eng, step, behind=2):
            for g in range(UNROLL + 1):
                step(g, g % UNROLL, g // UNROLL, True, g > 0, g > 1)
            with eng.Fori(1, (GROUPS - 1) // UNROLL) as i:
                for k in range(UNROLL):
                    step(UNROLL * i + (1 + k), (1 + k) % UNROLL, i + (1 + k) // UNROLL, True, True, True)
            for g in range(GROUPS, GROUPS + behind):
                step(g, g % UNROLL, g // UNROLL, False, g == GROUPS, True)

        @block.sync
        def _(sp):
            sp.wait_ge(s_const, 1)
            a = 96 * QV * P
            sp.dma_start(dst_nat[0:96, :], dst[0:a].rearrange("(p c) -> p c", p=96)).then_inc(s_dst, 16)
            b = 103 * QV * P
            sp.dma_start(dst_nat[96:103, :], dst[a:b].rearrange("(p c) -> p c", c=QV * P)).then_inc(s_dst, 16)
            sp.dma_start(dst_nat[103:104, 0:EDGES - b], dst[b:EDGES].rearrange("(a c) -> a c", a=1)).then_inc(s_dst, 16)
            sp.dma_start(edge_rows[0:FULL, 0:P], src[0:FULL * P].rearrange("(t c) -> t c", c=P)).then_inc(s_er, 16)
            sp.dma_start(edge_rows[1:FULL, P:ROW],
                         bass.AP(tensor=dst.tensor, offset=P - 1, ap=[[P, FULL - 1], [1, P + 2]])).then_inc(s_er, 16)
            sp.dma_start(edge_rows[0:1, P + 1:ROW], dst[0:P + 1].rearrange("(a c) -> a c", a=1)).then_inc(s_er, 16)
            sp.dma_start(edge_rows[FULL:FULL + 1, 0:REST], src[FULL * P:EDGES].rearrange("(a c) -> a c", a=1)).then_inc(s_er, 16)
            sp.dma_start(edge_rows[FULL:FULL + 1, P:P + 1 + REST],
                         dst[FULL * P - 1:EDGES].rearrange("(a c) -> a c", a=1)).then_inc(s_er, 16)
            sp.dma_start(edge_rows[0:1, P:P + 1], pad_i[0:1, 0, P:P + 1]).then_inc(s_er, 16)
            sp.dma_start(edge_rows[FULL:FULL + 1, REST:P], pad_i[0:1, 0, 0:P - REST]).then_inc(s_er, 16)
            sp.dma_start(edge_rows[FULL + 1:FULL + 2, 0:P], pad_i[0:1, 0, 0:P]).then_inc(s_er, 16)
            sp.dma_start(edge_rows[FULL:FULL + 1, P + 1 + REST:ROW], pad_i[0:1, 1, 0:P + 1 - REST]).then_inc(s_er, 16)
            sp.dma_start(edge_rows[FULL + 1:FULL + 2, P:ROW], pad_i[0:1, 1, :]).then_inc(s_er, 16)
            sp.dma_start(xs[:, :, :], x.rearrange("(b p) f -> p b f", p=BN)).then_inc(s_x, 16)
            m = EDGES - 127 * TILES
            sp.dma_start(attr_tail[0:m, :], edge_attr[127 * TILES:EDGES, :]).then_inc(s_tail, 16)
            sp.dma_start(attr_tail[m:m + P, :], ones[:, 0:ED]).then_inc(s_tail, 16)
            rest = GROUPS * ATTR_C - m - P
            sp.dma_start(attr_tail[m + P:m + P + rest, :], ones[0:rest, 0:ED]).then_inc(s_tail, 16)
            sp.wait_ge(s_v, 5)
            sp.dma_start(bias_rows[TILES:TILES + 1, :], acc[0:1, :, :].rearrange("p b f -> p (b f)")[:, 0:P * H]).then_inc(s_bz, 16)
            table0_v = table0.rearrange("(b p) f -> p b f", p=BN)
            for n, (b0, nb) in enumerate(CHUNKS):
                wait(sp, L[0]["feat_out"], n + 1)
                sp.dma_start(table0_v[:, b0:b0 + nb, :], h0[:, b0:b0 + nb, :]).then_inc(s_tab[0], 16)
            sp.wait_ge(s_tail, 48)
            sp.wait_ge(s_penfree, -(-GROUPS // 3))

            def step(g, u, i, new, mid, old):
                wait(sp, a_T, g - UNROLL + 1)
                to = attr_in[:, u, :]
                for lo, hi in ((0, 112), (112, 127)):
                    sp.dma_start(to[lo:hi, :],
                                 bass.AP(tensor=edge_attr.tensor, offset=lo * TILES * ED + g * (ATTR_C * ED),
                                         ap=[[TILES * ED, hi - lo], [1, ATTR_C * ED]])).then_inc(s_attr[u], 16)
                sp.dma_start(to[127:128, :], bass.AP(tensor=attr_tail.tensor, offset=g * (ATTR_C * ED),
                                                     ap=[[ATTR_C * ED, 1], [1, ATTR_C * ED]])).then_inc(s_attr[u], 16)

            run_groups(sp, step, behind=0)
            sp.wait_ge(s_ebfin, 1)
            sp.dma_start(bias_rows.rearrange("t c -> (t c)")[0:P * TILES * H].rearrange("(p c) -> p c", p=P),
                         eb_nat[:, 0:TILES * H]).then_inc(s_ebout, 16)
            table1_v = table1.rearrange("(b p) f -> p b f", p=BN)
            for n, (b0, nb) in enumerate(CHUNKS):
                wait(sp, L[1]["feat_out"], b0 + nb)
                sp.dma_start(table1_v[:, b0:b0 + nb, :], kv[:, b0:b0 + nb, :]).then_inc(s_tab[1], 16)
            sp.wait_ge(s_out, 1)
            out_v = out.rearrange("(b p) f -> p b f", p=BN)
            sp.dma_start(out_v, work[:, :, :]).then_inc(s_out, 16)
            sp.wait_ge(s_out, 17)
            sp.wait_ge(s_tab[0], 16 * len(CHUNKS))
            sp.wait_ge(s_tab[1], 16 * len(CHUNKS))
            sp.wait_ge(s_ebout, 16)
            sp.wait_ge(s_er, 160)
            sp.wait_ge(s_bz, 16)

        @block.gpsimd
        def _(pool):
            n = [0]
            Rep4 = Rep.rearrange("p r (v h) -> p r v h", h=H)

            def then(ins):
                n[0] += 1
                ins.then_inc(s_pool, 1)
                pool.wait_ge(s_pool, n[0])

            pool.memset(pad_i[0:1, 0, 0:P], 0).then_inc(s_pool, 1)
            pool.memset(pad_i[0:1, 0, P:P + 2], -1).then_inc(s_pool, 1)
            pool.memset(pad_i[0:1, 1, :], PAD_DST).then_inc(s_pool, 1)
            pool.memset(ones[:, :], 1.0).then_inc(s_pool, 1)
            n[0] = 4
            then(pool.memset(dst_nat, NODES - 1))
            pool.sem_inc(s_const, 1)
            pool.memset(ident[:, :], 0.0).then_inc(s_pool, 1)
            pool.memset(HselT[:, :, :], 0.0).then_inc(s_pool, 1)
            pool.memset(Rep, 0.0).then_inc(s_pool, 1)
            n[0] += 3
            then(pool.memset(E0[:, :], 0.0))
            pool.iota(iota_i[:, :], pattern=[[1, P]], base=0, channel_multiplier=0).then_inc(s_pool, 1)
            pool.iota(thr_i[:, :], pattern=[[BN, BLOCKS - 1]], base=BN, channel_multiplier=0).then_inc(s_pool, 1)
            pool.iota(vcol_i[:, 0:VK], pattern=[[VP, VK]], base=0, channel_multiplier=1).then_inc(s_pool, 1)
            pool.iota(vcol_i[:, VK:VK + 1], pattern=[[0, 1]], base=BN, channel_multiplier=BN).then_inc(s_pool, 1)
            n[0] += 4
            then(pool.affine_select(out=ident[:, :], in_=ident[:, :], compare_op=ALU.not_equal, fill=1.0,
                                    base=0, pattern=[[-1, P]], channel_multiplier=1))
            then(pool.affine_select(out=E0[:, :], in_=E0[:, :], compare_op=ALU.not_equal, fill=1.0,
                                    base=0, pattern=[[0, H]], channel_multiplier=1))
            pool.sem_inc(s_const, 1)
            then(pool.affine_select(out=HselT[:, :, :], in_=HselT[:, :, :], compare_op=ALU.not_equal, fill=1.0,
                                    base=0, pattern=[[0, GV], [-1, H]], channel_multiplier=1))
            then(pool.affine_select(out=Rep4, in_=Rep4, compare_op=ALU.not_equal, fill=1.0,
                                    base=0, pattern=[[-GV, GK], [-1, GV], [0, H]], channel_multiplier=1))
            for t, w, k in ((headmask, H, DH), (Vsel, GV, H)):
                then(pool.affine_select(out=t[:, :], in_=ones[:, 0:w], compare_op=ALU.is_ge, fill=0.0,
                                        base=0, pattern=[[-k, w]], channel_multiplier=1))
                then(pool.affine_select(out=t[:, :], in_=t[:, :], compare_op=ALU.is_ge, fill=0.0,
                                        base=k - 1, pattern=[[k, w]], channel_multiplier=-1))
            pool.sem_inc(s_const, 1)

            pool.wait_ge(s_er, 160)
            pool.wait_ge(s_tidx, 1)
            for k in range(VK):
                pool.indirect_dma_start(rows_i[:, k, :], None, edge_rows,
                                        bass.IndirectOffsetOnAxis(ap=tidx[:, k:k + 1], axis=0)).then_inc(s_rows, 16)

            def gathers(n, table, w):
                s = L[n]

                def step(g, u, i, new, mid, old):
                    wait(pool, s["idx_staged"], g - (UNROLL - 1))
                    for j in range(GV // QV):
                        wait(pool, s["pv_ready"], 4 * (g - UNROLL) + j + 1)
                        pool.sem_inc(s_go, 1)
                        for v in range(QV * j, QV * j + QV):
                            pool.indirect_dma_start(
                                G[:, u, v, 0:w], None, table,
                                bass.IndirectOffsetOnAxis(ap=idx_stage[:, u, v:v + 1], axis=0)
                            ).then_inc(s_gath[u][j], 16)

                run_groups(pool, step, behind=0)

            pool.wait_ge(s_idx0, 1)
            pool.wait_ge(s_tab[0], 16 * len(CHUNKS))
            gathers(0, table0, W0)
            pool.wait_ge(s_ebout, 16)
            pool.wait_ge(s_bz, 16)
            wait(pool, L[0]["pv_ready"], 4 * GROUPS)
            for k in range(VK):
                pool.indirect_dma_start(bias_v[:, k, :, :].rearrange("p e h -> p (e h)"), None, bias_rows,
                                        bass.IndirectOffsetOnAxis(ap=tidx[:, k:k + 1], axis=0)).then_inc(s_ebin, 16)
            pool.wait_ge(s_tab[1], 16 * len(CHUNKS))
            pool.wait_ge(s_ebt, VK * H)
            pool.wait_ge(s_idx0, 2)
            gathers(1, table1, W1)

        @block.scalar
        def _(act):
            act.dma_start(w0n[:, :], w0).then_inc(s_w, 16)
            for k in range(2):
                act.dma_start(attc[:, k:k + 1], att.rearrange("(t p a) -> t p a", p=P, a=1)[k]).then_inc(s_w, 16)
            for k, w in enumerate((wq, wk, wv)):
                act.dma_start(Wqkv[:, F * k:F * k + F], w).then_inc(s_w, 16)
            act.dma_start(Wo[:, :], wo).then_inc(s_w, 16)
            act.wait_ge(s_v, 5)
            for c in range(QV):
                act.dma_start(WeBD[ED * c:ED * c + ED, c, :], we).then_inc(s_w, 16)
            for k, b in enumerate((bias0, bq, bk, bv, bo, gamma, beta)):
                act.dma_start(rowv[:, k, :], b.rearrange("(a f) -> a f", a=1).to_broadcast([BN, F])).then_inc(s_w, 16)
            act.dma_start(be_r[:, :], be.rearrange("(a f) -> a f", a=1).to_broadcast([P, H])).then_inc(s_w, 16)

            act.wait_ge(s_vt, 2)
            act.activation(idx_all[:, 0:VISITS], tp[0][:, 0:VISITS], ACT.Copy).then_inc(s_vte, 1)
            act.activation(lid[:, :], tp[1][:, 0:VISITS], ACT.Copy).then_inc(s_vte, 1)
            act.wait_ge(s_vte, 2)
            act.activation(idx_stage[:, :, :].rearrange("p u v -> p (u v)"), idx_all[:, 0:UNROLL * GV], ACT.Copy).then_inc(s_idx0, 1)
            act.wait_ge(s_vt, 3)
            for k, w in enumerate((H * SLOT, F, 3 * 2 * H)):
                act.activation(offs[k], ex[0][0:1, 0:VISITS], ACT.Copy, scale=float(w)).then_inc(s_vte, 1)
            act.wait_ge(s_vt, 4)
            for k in range(2):
                to = chain_pen[:, k, :].rearrange("p (g v) -> p g v", v=GV)
                act.activation(to[:, :, ::-1] if k else to, bank[4 + k][0:H, 0:VISITS].rearrange("p (g v) -> p g v", v=GV),
                               ACT.Copy, scale=BIG).then_inc(s_vte, 1)
            act.wait_ge(s_vt, 5)
            act.activation(first_lid[:, :], sm[0:H, 256:256 + GROUPS], ACT.Copy).then_inc(s_vte, 1)

            def square(s, source):
                for c in range(BLOCKS // LN_CHUNK):
                    b = slice(LN_CHUNK * c, LN_CHUNK * c + LN_CHUNK)
                    wait(act, s["xc"], c + 1)
                    act.activation(work2[:, b, :], source[:, b, :], ACT.Square).then_inc(s.sem["sq"], 1)
                wait(act, s["var"], 1)
                act.activation(st[:, 3, :], st[:, 2, :], ACT.Sqrt).then_inc(s.sem["std"], 1)

            square(L[0], hn)
            act.wait_ge(s_wps, 2)
            act.activation(WA[:, 0:F], sm[:, 0:F], ACT.Copy).then_inc(s_wc, 1)
            act.activation(WA[:, F:F + 2 * H], sm[:, F:F + 2 * H], ACT.Copy).then_inc(s_wc, 1)

            def transposed(s, n, nb, used, count):
                wait(act, s["hT_ps"], n + 1)
                wait(act, used, count)
                act.activation(HT[:, n % 2, 0:nb * BN], tp[n % 2][:, 0:nb * BN], ACT.Copy).then_inc(s.sem["hT"], 1)

            for n, (b0, nb) in enumerate(CHUNKS):
                transposed(L[0], n, nb, L[0]["feat"], n - 1)
                wait(act, L[0]["feat"], n + 1)
                act.activation(h0[:, b0:b0 + nb, :],
                               ex[n % 2][0:BN, 0:nb * (F + 2 * H)].rearrange("p (b f) -> p b f", b=nb)[:, :, 0:W0],
                               ACT.Copy).then_inc(L[0].sem["feat_out"], 1)
                act.activation(nd[:, b0:b0 + nb, 0:H],
                               ex[n % 2][0:BN, 0:nb * (F + 2 * H)].rearrange("p (b f) -> p b f", b=nb)[:, :, W0:W0 + H],
                               ACT.Copy).then_inc(L[0].sem["feat_done"], 1)
            for c in range(-(-GROUPS // 3)):
                ng = min(3, GROUPS - 3 * c)
                act.wait_ge(s_pent, c + 1)
                wait(act, s_penfree, c - 1)
                act.activation(prod[:, c % 2, 0:ng * (P + 2)], ms[c % 2][:, 0:ng * (P + 2)], ACT.Copy,
                               scale=BIG).then_inc(s_pene, 1)

            def layer(n):
                s = L[n]

                pen_f = pen[:, :, :].rearrange("p g e -> p (g e)")

                def evac(g, j):
                    wait(act, s["t_done"], 4 * g + j + 1)
                    wait(act, s["expanded"], 4 * (g - 1) + j + 1)
                    act.activation((ST if n else ST_b)[:, QV * j:QV * j + QV, :],
                                   tp[j % 2][0:BN, :].rearrange("p (v e) -> p v e", v=QV), ACT.Copy).then_inc(s.sem["st_ready"], 1)

                def step(g, u, i, new, mid, old):
                    q = g - 1
                    k = 2 - n
                    if mid and n == 0:
                        wait(act, s["scoreT"], q + 1)
                        wait(act, s["dd_ready"], 2 * q)
                        act.activation(esT[:, :], sT[:, P:2 * P], ACT.Copy).then_inc(s.sem["esT_ready"], 1)
                    if new:
                        for j in range(4):
                            evac(g, j)
                    if mid:
                        wait(act, s["dd_ready"], k * (q + 1))
                        wait(act, s["pT"], q)
                        act.activation(EP[:, 0:k, :], DD[:, 0:k, :], ACT.Exp).then_inc(s.sem["p_ready"], 1)
                    if new:
                        if n == 0:
                            wait(act, s["expanded"], 4 * g + 4)
                            wait(act, s["scoreT"], g)
                            wait(act, s["score_parts"], g)
                            act.activation(es[:, :, :, :], ex[0][:, 0:GV * 2 * H].rearrange("p (v k h) -> p k v h", k=2, h=H), ACT.Copy).then_inc(s.sem["es_ready"], 1)
                            wait(act, a_T, g + 1)
                            wait(act, a_mm, g)
                            act.activation(attrT[:, :], ex[1][:, :], ACT.Copy).then_inc(a_Te, 1)
                    if mid:
                        wait(act, s["al_mm"], q + 1)
                        wait(act, s["rescaled"], q)
                        act.activation(AL[:, :], sm[0:BN, 128:128 + H], ACT.Exp).then_inc(s.sem["al_ready"], 1)
                    if new:
                        wait(act, s["m_done"], g - UNROLL + 1)
                        if n == 0:
                            wait(act, s["ps_ready"], g - UNROLL + 1)
                        act.activation(pcur[:, u, :], pen_f[:, bass.ds(g * (P + 1), P + 1)], ACT.Copy).then_inc(s.sem["pcur_ready"], 1)
                        for j in range(GV // QV):
                            act.wait_ge(s_gath[u][j], gathered(n, u, i))
                        act.activation(idx_stage[:, u, :], idx_all[:, bass.ds((g + UNROLL) * GV, GV)], ACT.Copy).then_inc(s.sem["idx_staged"], 1)
                    if mid:
                        wait(act, s["pT"], q + 1)
                        wait(act, s["mm_done"], GV * q)
                        act.activation(PV[:, :, :, DH:DH + k].rearrange("p v h k -> p (v h) k"),
                                       sT[:, 2 * P:(2 + k) * P].rearrange("p (k c) -> p c k", k=k), ACT.Copy).then_inc(s.sem["pcols"], 1)
                    if new and n == 0:
                        wait(act, a_mm, g + 1)
                        act.activation(eb_nat[:, bass.ds(g * (ATTR_C * H), ATTR_C * H)], sm[:, 256:256 + ATTR_C * H],
                                       ACT.Copy).then_inc(a_out, 1)

                run_groups(act, step)

            act.wait_ge(s_penfree, -(-GROUPS // 3))
            layer(0)
            wait(act, L[0]["idx_staged"], GROUPS)
            act.activation(idx_stage[:, :, :].rearrange("p u v -> p (u v)"), idx_all[:, 0:UNROLL * GV], ACT.Copy).then_inc(s_idx0, 1)
            square(L[1], hn)
            for n, (b0, nb) in enumerate(CHUNKS):
                transposed(L[1], n, nb, L[1]["feat_done"], CHUNKS[n - 1][0] if n else 0)
            for h in range(H):
                act.wait_ge(s_ebt, VK * (h + 1))
                act.activation(ebias[:, :, h], ms[h % 2][:, 0:VISITS], ACT.Copy).then_inc(s_ebe, 1)
            layer(1)
            for n, (b0, nb) in enumerate(CHUNKS):
                act.wait_ge(s_fT, n + 1)
                wait(act, s_fo, n - 1)
                act.activation(HT[:, n % 2, 0:nb * BN], tp[n % 2][:, 0:nb * BN], ACT.Copy).then_inc(s_fTe, 1)
            square(F_, work)

        @block.tensor
        def _(pe):
            regs = [pe.alloc_register(f"pe_off{k}") for k in range(GV)]
            t4 = TILES // QV
            pe.wait_ge(s_const, 2)
            pe.wait_ge(s_fl, 1)
            for w in range(2):
                for k in range(QV):
                    last = pe.matmul(bank[w][0:BLOCKS - 1, k:TILES:QV], FLB_[:, w * QV + k, :], ident[0:t4, 0:t4], start=True, stop=True)
            last.then_inc(s_flT, 1)
            pe.wait_ge(s_ge, 1)
            pe.matmul(bank[2][0:VP, 0:TILES], ones[0:BLOCKS - 1, 0:VP], ge[:, 1, :], start=True, stop=True).then_inc(s_diff, 1)
            pe.wait_ge(s_watt, 1)
            pe.transpose(sm[:, 0:F], w0n[:, :], ident[:, :]).then_inc(s_wps, 1)
            pe.matmul(sm[:, F:F + 2 * H], w0n[:, :], attblk[:, :], start=True, stop=True).then_inc(s_wps, 1)
            pe.wait_ge(s_rowsf, 1)
            iv = ident[0:VP, 0:VP]
            for k in range(VK):
                last = pe.transpose(tp[0][:, VP * k:VP * k + VP], rows_f[:, k, 0:P], iv)
            last.then_inc(s_vt, 1)
            pe.wait_ge(s_vlid, 1)
            for k in range(VK):
                last = pe.transpose(tp[1][:, VP * k:VP * k + VP], lid_v[:, k, :], iv)
            last.then_inc(s_vt, 1)
            for k in range(VK):
                last = pe.matmul(ex[0][0:1, VP * k:VP * k + VP], vstat[:, 5, k:k + 1], iv, start=True, stop=True)
            last.then_inc(s_vt, 1)
            for m in range(2):
                for k in range(VK):
                    last = pe.matmul(bank[4 + m][0:H, VP * k:VP * k + VP],
                                     chain_b[:, m, k, :], iv, start=True, stop=True)
            last.then_inc(s_vt, 1)
            pe.wait_ge(s_vte, 2)
            pe.matmul(sm[0:H, 256:256 + GROUPS], E0[:, :], lid[:, 0:VISITS:GV], start=True, stop=True).then_inc(s_vt, 1)

            def transposes(s, n, b0, nb):
                wait(pe, s["hn"], (b0 + nb - 1) // LN_CHUNK + 1)
                wait(pe, s["hT"], n - 1)
                for k in range(nb):
                    last = pe.transpose(tp[n % 2][:, k * BN:k * BN + BN], hn[:, b0 + k, :], ident[0:BN, 0:BN])
                last.then_inc(s.sem["hT_ps"], 1)

            pe.wait_ge(s_vte, 5)
            for n, (b0, nb) in enumerate(CHUNKS):
                transposes(L[0], n, b0, nb)
                wait(pe, L[0]["hT"], n + 1)
                wait(pe, L[0]["feat_out"], n - 1)
                wait(pe, L[0]["feat_done"], n - 1)
                for k in range(nb):
                    last = pe.matmul(ex[n % 2][0:BN, k * (F + 2 * H):(k + 1) * (F + 2 * H)], HT[:, n % 2, k * BN:k * BN + BN],
                                     WA[:, :], start=True, stop=True)
                last.then_inc(L[0].sem["feat"], 1)
            pe.wait_ge(s_const, 3)
            pe.wait_ge(s_vte, 7)
            for c in range(-(-GROUPS // 3)):
                wait(pe, s_pene, c - 1)
                for g in range(3 * c, min(3 * c + 3, GROUPS)):
                    last = pe.matmul(ms[c % 2][:, (g % 3) * (P + 2):(g % 3 + 1) * (P + 2)],
                                     Rep[:, g % GK, :], rows_f[:, g // GK, P:ROW],
                                     start=True, stop=True)
                last.then_inc(s_pent, 1)

            def layer(n):
                s = L[n]
                width = F if n else 3 * 2 * H
                nodes = q_sb.rearrange("p b f -> p (b f)") if n else nd3[:, :, :, :].rearrange("p b k f -> p (b k f)")

                def one_hot_T(g, u, j):
                    wait(pe, s["S_ready"], 4 * g + j + 1)
                    wait(pe, s["st_ready"], 4 * g + j - 1)
                    for k in range(QV):
                        last = pe.transpose(tp[j % 2][0:BN, k * P:k * P + P], S[:, u, QV * j + k, :], ident[:, :])
                    last.then_inc(s.sem["t_done"], 1)

                def expand(g, j):
                    wait(pe, s["st_ready"], 4 * g + j + 1)
                    if n:
                        wait(pe, s["qk_done"], 4 * g + j - 1)
                    elif j == 0:
                        wait(pe, s["es_ready"], g)
                    for k in range(QV):
                        v = QV * j + k
                        off = pe.snap(regs[v], min_val=0, max_val=(BLOCKS - 1) * width)
                        if n:
                            last = pe.matmul(ex[j % 2][:, k * F:k * F + F], ST[:, v, :], nodes[:, bass.ds(off, F)], start=True, stop=True)
                            continue
                        for part in range(3):
                            last = pe.matmul(ex[0][:, v * 2 * H:(v + 1) * 2 * H], ST_b[:, v, :],
                                             nodes[:, bass.ds(off + part * 2 * H, 2 * H)], start=part == 0, stop=part == 2)
                    last.then_inc(s.sem["expanded"], 1)

                def sums(g, u, p):
                    r, ur = g - 2, (u + 1) % UNROLL
                    if p == 0:
                        wait(pe, s["pcols"], r + 1)
                    if p % 2 == 0:
                        wait(pe, s["pv_ready"], 4 * r + p // 2 + 1)
                    wait(pe, s["acc_added"], GV * r + 2 * p - 2)
                    for k in range(2):
                        pe.matmul(ms[p % 2][0:BN, k * 256:k * 256 + H * SLOT], S[:, ur, 2 * p + k, :],
                                  PV[:, 2 * p + k, :, :].rearrange("p h k -> p (h k)"),
                                  start=True, stop=True).then_inc(s.sem["mm_done"], 1)

                def step(g, u, i, new, mid, old):
                    q = g - 1
                    if mid:
                        wait(pe, s["scores_ready"], q + 1)
                        wait(pe, s["pcols"], q)
                        wait(pe, s["dd_ready"], (2 - n) * q)
                        if n == 0:
                            wait(pe, s["es_ready"], q + 1)
                            wait(pe, s["esT_ready"], q)
                            pe.transpose(sT[:, P:2 * P], es[:, 1, :, :].rearrange("p v h -> p (v h)"), ident[:, :])
                        pe.transpose(sT[:, 0:P], sc[:, :, :].rearrange("p v h -> p (v h)"), ident[:, :]).then_inc(s.sem["scoreT"], 1)
                    if new:
                        pe.load(regs, offs[1 if n else 2][:, bass.ds(g * GV, GV)])
                        one_hot_T(g, u, 0)
                    if old:
                        sums(g, u, 0)
                    if mid:
                        wait(pe, s["rh_ready"], q + 1)
                        wait(pe, s["x_done"], q)
                        wait(pe, s["u_done"], q)
                        wait(pe, s["al_ready"], q)
                        if n == 0:
                            wait(pe, a_out, q + 1)
                        pe.matmul(sm[0:H, 0:2 * GV], Hsel[:, :], RH[:, :, :].rearrange("p k v -> p (k v)"),
                                  start=True, stop=True).then_inc(s.sem["hop1"], 1)
                    if old:
                        sums(g, u, 1)
                    if new:
                        one_hot_T(g, u, 1)
                    if mid:
                        wait(pe, s["x_done"], q + 1)
                        wait(pe, s["u_done"], q + 1)
                        wait(pe, s["carry"], q + 1)
                        wait(pe, s["cc_mul"], q)
                        d = D[:, (u + 2) % UNROLL, :, :]
                        for k in range(2):
                            last = pe.matmul(sm[:, 64 + GV * k:64 + GV * k + GV], HselT[:, :, :].rearrange("p v h -> p (v h)"),
                                             d[:, k, k:k + GV], start=True, stop=True)
                        last.then_inc(s.sem["hop2"], 1)
                    if old:
                        sums(g, u, 2)
                    if new:
                        one_hot_T(g, u, 2)
                    if old:
                        sums(g, u, 3)
                    if new:
                        expand(g, 0)
                        expand(g, 1)
                        one_hot_T(g, u, 3)
                    if old:
                        sums(g, u, 4)
                    if new:
                        expand(g, 2)
                    if old:
                        sums(g, u, 5)
                    if new:
                        expand(g, 3)
                    if old:
                        sums(g, u, 6)
                    if new and n == 0:
                        pe.wait_ge(s_attr[u], 48 * (i + 1))
                        wait(pe, a_Te, g)
                        for k in range(QV):
                            last = pe.transpose(ex[1][:, k * P:k * P + P], attr_in[:, u, k * P:k * P + P], ident[:, :])
                        last.then_inc(a_T, 1)
                    if mid:
                        wait(pe, s["p_ready"], q + 1)
                        if n == 0:
                            wait(pe, s["ps_ready"], q + 1)
                            pe.transpose(sT[:, 3 * P:4 * P], PS[:, :], ident[:, :])
                        pe.transpose(sT[:, 2 * P:3 * P], EP[:, 0, :], ident[:, :]).then_inc(s.sem["pT"], 1)
                        wait(pe, s["r8_ready"], q + 1)
                        wait(pe, s["ohf_ready"], q + 1)
                        pe.matmul(sm[0:BN, 128:128 + H], OHF[:, :], R8[:, :], start=True, stop=True).then_inc(s.sem["al_mm"], 1)
                    if old:
                        sums(g, u, 7)
                    if new and n == 0:
                        wait(pe, a_Te, g + 1)
                        wait(pe, a_out, g)
                        wait(pe, s["al_ready"], g)
                        for k in range(QV):
                            last = pe.matmul(sm[:, 256 + 32 * k:256 + 32 * k + 32], attrT[:, k * P:k * P + P],
                                             WeBD[:, :, :].rearrange("p c h -> p (c h)"), start=True, stop=True)
                        last.then_inc(a_mm, 1)

                run_groups(pe, step)

            pe.wait_ge(s_w, 19 * 16)
            wait(pe, L[0]["feat_done"], len(CHUNKS) + 1)
            layer(0)
            m = 0
            for n, (b0, nb) in enumerate(CHUNKS):
                transposes(L[1], n, b0, nb)
                wait(pe, L[1]["hT"], n + 1)
                for k in range(nb):
                    wait(pe, L[1]["feat_out"], m - 1)
                    pe.matmul(ex[m % 2][0:BN, 0:3 * F], HT[:, n % 2, k * BN:k * BN + BN], Wqkv[:, :],
                              start=True, stop=True).then_inc(L[1].sem["feat_done"], 1)
                    m += 1
            pe.wait_ge(s_ebin, 16 * VK)
            for h in range(H):
                wait(pe, s_ebe, h - 1)
                for k in range(VK):
                    pe.transpose(ms[h % 2][:, VP * k:VP * k + VP], bias_v[:, k, :, h], ident[0:VP, 0:VP]).then_inc(s_ebt, 1)
            wait(pe, L[1]["feat_out"], BLOCKS)
            layer(1)
            for n, (b0, nb) in enumerate(CHUNKS):
                pe.wait_ge(s_fin_on, 1)
                wait(pe, s_fTe, n - 1)
                for k in range(nb):
                    last = pe.transpose(tp[n % 2][:, k * BN:k * BN + BN], work2[:, b0 + k, :], ident[0:BN, 0:BN])
                last.then_inc(s_fT, 1)
                pe.wait_ge(s_fTe, n + 1)
                wait(pe, s_fh, n - 1)
                for k in range(nb):
                    last = pe.matmul(ex[n % 2][0:BN, k * F:k * F + F], HT[:, n % 2, k * BN:k * BN + BN], Wo[:, :],
                                     start=True, stop=True)
                last.then_inc(s_fo, 1)

        @block.vector
        def _(ve):
            n_v = [0]

            def then(ins):
                n_v[0] += 1
                ins.then_inc(s_v, 1)
                ve.wait_ge(s_v, n_v[0])

            regs = [ve.alloc_register(f"ve_off{k}") for k in range(GV)]
            then(ve.memset(WeBD[:, :, :], 0.0))
            ve.memset(idx_all[:, VISITS:], 0).then_inc(s_v, 1)
            ve.memset(D[:, :, :, :], LOW).then_inc(s_v, 1)
            ve.memset(PV[:, :, :, :], 0.0).then_inc(s_v, 1)
            n_v[0] += 3
            then(ve.memset(acc[:, :, :], 0.0))
            ve.wait_ge(s_const, 2)
            ve.tensor_copy(iota_n[:, :], iota_i[:, :]).then_inc(s_v, 1)
            ve.tensor_copy(thr_row[:, :], thr_i[:, :]).then_inc(s_v, 1)
            ve.tensor_copy(vcol[:, :], vcol_i[:, 0:VK]).then_inc(s_v, 1)
            n_v[0] += 3
            then(ve.tensor_copy(thr_col[0:BLOCKS - 1, :], vcol_i[0:BLOCKS - 1, VK:VK + 1]))
            ve.wait_ge(s_dst, 48)
            then(ve.tensor_copy(FL[:, :, :], dst_nat[:, :].rearrange("p (k c) -> p c k", k=QV)[:, ::P - 1, :]))
            t4 = TILES // QV
            ve.tensor_copy(FLB_,
                           FL[:, :, :].rearrange("p w k -> p (w k)").unsqueeze(2).to_broadcast([t4, 2 * QV, BLOCKS - 1])
                           ).then_inc(s_fl, 1)
            ve.wait_ge(s_flT, 1)
            then(ve.tensor_scalar(ge[:, 0, :], bank[1][0:BLOCKS - 1, 0:TILES], thr_col[0:BLOCKS - 1, :], None, op0=ALU.is_ge))
            ve.scalar_tensor_tensor(ge[:, 1, :], bank[0][0:BLOCKS - 1, 0:TILES], thr_col[0:BLOCKS - 1, :], ge[:, 0, :],
                                    op0=ALU.is_lt, op1=ALU.mult).then_inc(s_ge, 1)
            ve.memset(vtmp[:, 0, :], 1.0).then_inc(s_v, 1)
            n_v[0] += 1
            ve.wait_ge(s_v, n_v[0])
            ve.wait_ge(s_diff, 1)
            then(ve.tensor_tensor_scan(vend[:, :], vtmp[:, 0, :], bank[2][0:VP, 0:TILES], 0.0, ALU.add, ALU.add))
            for k in range(VK):
                then(ve.scalar_tensor_tensor(vtmp[:, 1, :], vend[:, :], vcol[:, k:k + 1], vend[:, :], op0=ALU.is_le, op1=ALU.mult))
                ve.tensor_reduce(vstat[:, 1, k:k + 1], vtmp[:, 1, :], AX.X, ALU.max).then_inc(s_v, 1)
                n_v[0] += 1
                then(ve.tensor_scalar(vtmp[:, 0, :], vend[:, :], vcol[:, k:k + 1], None, op0=ALU.is_le))
                then(ve.tensor_reduce(vstat[:, 0, k:k + 1], vtmp[:, 0, :], AX.X, ALU.add))
            ve.tensor_copy(tidx[:, :], vstat[:, 0, :]).then_inc(s_tidx, 1)

            ve.wait_ge(s_w, 19 * 16)
            ve.wait_ge(s_const, 3)
            for k in range(2):
                ve.tensor_scalar(attblk[:, k * H:k * H + H], headmask[:, :], attc[:, k:k + 1], None, op0=ALU.mult).then_inc(s_v, 1)
            n_v[0] += 2
            ve.wait_ge(s_v, n_v[0])
            ve.sem_inc(s_watt, 1)
            then(ve.tensor_reduce(Hsel[:, :], ident[:, :].rearrange("p (v h) -> p h v", h=H), AX.X, ALU.add))
            then(ve.tensor_scalar(Wqkv[:, 0:F], Wqkv[:, 0:F], DH ** -0.5, None, op0=ALU.mult))
            then(ve.tensor_scalar(rowv[:, 1, :], rowv[:, 1, :], DH ** -0.5, None, op0=ALU.mult))

            def layernorm(s, source, to, relu):
                for c in range(BLOCKS // LN_CHUNK):
                    b = slice(LN_CHUNK * c, LN_CHUNK * c + LN_CHUNK)
                    then(ve.tensor_reduce(st[:, 0, b], source[:, b, :], AX.X, ALU.add))
                    then(ve.tensor_scalar(st[:, 1, b], st[:, 0, b], 1.0 / F, None, op0=ALU.mult))
                    ve.tensor_tensor(to[:, b, :], source[:, b, :], st[:, 1, b].unsqueeze(2).to_broadcast([BN, LN_CHUNK, F]),
                                     ALU.subtract).then_inc(s.sem["xc"], 1)
                for c in range(BLOCKS // LN_CHUNK):
                    b = slice(LN_CHUNK * c, LN_CHUNK * c + LN_CHUNK)
                    wait(ve, s["sq"], c + 1)
                    then(ve.tensor_reduce(st[:, 0, b], work2[:, b, :], AX.X, ALU.add))
                ve.tensor_scalar(st[:, 2, :], st[:, 0, :], 1.0 / F, 1e-5, op0=ALU.mult, op1=ALU.add).then_inc(s.sem["var"], 1)
                wait(ve, s["std"], 1)
                then(ve.reciprocal(st[:, 4, :], st[:, 3, :]))
                for c in range(BLOCKS // LN_CHUNK):
                    b = slice(LN_CHUNK * c, LN_CHUNK * c + LN_CHUNK)
                    r = st[:, 4, b].unsqueeze(2).to_broadcast([BN, LN_CHUNK, F])
                    if relu:
                        ve.scalar_tensor_tensor(to[:, b, :], to[:, b, :], 0.0, r, op0=ALU.max, op1=ALU.mult).then_inc(s.sem["hn"], 1)
                    else:
                        ve.tensor_tensor(to[:, b, :], to[:, b, :], r, ALU.mult).then_inc(s.sem["hn"], 1)
                wait(ve, s["hn"], BLOCKS // LN_CHUNK)

            ve.wait_ge(s_rows, 16 * VK)
            ve.tensor_copy(rows_f[:, :, :], rows_i[:, :, :]).then_inc(s_rowsf, 1)
            ve.wait_ge(s_rowsf, 1)
            then(ve.tensor_tensor(cmpb[:, :, :], rows_f[:, :, P + 1:P + 2].to_broadcast([VP, VK, BLOCKS - 1]),
                                  thr_row[0:VP, :].unsqueeze(1).to_broadcast([VP, VK, BLOCKS - 1]), ALU.is_ge))
            then(ve.tensor_reduce(vstat[:, 2, :], cmpb[:, :, :], AX.X, ALU.add))
            then(ve.tensor_tensor(vstat[:, 3, :], vcol[:, :], vstat[:, 1, :], ALU.subtract))
            then(ve.tensor_tensor(vstat[:, 4, :], vstat[:, 3, :], vstat[:, 2, :], ALU.add))
            then(ve.tensor_scalar(vstat[:, 5, :], vstat[:, 4, :], float(BLOCKS - 1), None, op0=ALU.min))
            then(ve.tensor_scalar(vstat[:, 6, :], vstat[:, 5, :], float(BN), None, op0=ALU.mult))
            then(ve.tensor_tensor(vstat[:, 7, :], rows_f[:, :, P], rows_f[:, :, 2 * P], ALU.subtract))
            then(ve.tensor_tensor(vstat[:, 8, :], rows_f[:, :, P + 1], rows_f[:, :, 2 * P + 1], ALU.subtract))
            ve.tensor_copy(chain_b[:, :, :, :].rearrange("p m k h -> p (m k) h"),
                           vstat[:, 7:9, :].rearrange("p m k -> p (m k)").unsqueeze(2).to_broadcast([VP, 2 * VK, H])
                           ).then_inc(s_v, 1)
            n_v[0] += 1
            then(ve.tensor_tensor(lid_v[:, :, :], rows_f[:, :, P + 1:2 * P + 1],
                                  vstat[:, 6, :].unsqueeze(2).to_broadcast([VP, VK, P]), ALU.subtract))
            ve.sem_inc(s_vlid, 1)
            ve.wait_ge(s_x, 16)
            layernorm(L[0], xs, hn, True)
            wait(ve, L[0]["feat_out"], len(CHUNKS))
            wait(ve, L[0]["feat_done"], len(CHUNKS))
            then(ve.tensor_tensor(nst[:, 0, :, :], h0[:, :, F:W0], nd[:, :, 0:H], ALU.add))
            ve.scalar_tensor_tensor(nd[:, :, H:2 * H], nst[:, 0, :, :], SLOPE, nst[:, 0, :, :], op0=ALU.mult,
                                    op1=ALU.max).then_inc(s_v, 1)
            n_v[0] += 1
            ve.wait_ge(s_v, n_v[0])
            then(ve.tensor_copy(nd3[:, :, 0, :], nd[:, :, :]))
            then(ve.tensor_tensor(nd[:, :, :], nd[:, :, :], nd3[:, :, 0, :], ALU.subtract))
            then(ve.tensor_copy(nd3[:, :, 1, :], nd[:, :, :]))
            then(ve.tensor_tensor(nd[:, :, :], nd[:, :, :], nd3[:, :, 1, :], ALU.subtract))
            ve.tensor_copy(nd3[:, :, 2, :], nd[:, :, :]).then_inc(L[0].sem["feat_done"], 1)
            for c in range(-(-GROUPS // 3)):
                ng = min(3, GROUPS - 3 * c)
                ve.wait_ge(s_pene, c + 1)
                d = prod[:, c % 2, 0:ng * (P + 2)].rearrange("p (g e) -> p g e", g=ng)
                ve.tensor_tensor(pen[:, 3 * c:3 * c + ng, :], d[:, :, 0:P + 1], d[:, :, 1:P + 2], ALU.subtract).then_inc(s_penfree, 1)
            ve.wait_ge(s_penfree, -(-GROUPS // 3))
            ve.wait_ge(s_vte, 8)
            ve.wait_ge(s_bz, 16)

            def layer(n):
                s = L[n]
                k = 2 - n
                acc_f = acc[:, :, :].rearrange("p b f -> p (b f)")

                def step(g, u, i, new, mid, old):
                    q, r = g - 1, g - 2
                    uq, ur = (u + 2) % UNROLL, (u + 1) % UNROLL
                    score = sT[:, 0:P] if n else smax[:, :]
                    p0 = pcur[:, uq, 0:P]
                    p1 = pcur[:, uq, 1:P + 1]
                    d, e = D[:, uq, :, :], D[:, u, :, :]
                    off = []

                    def load_offsets(k):
                        if old:
                            half = regs[k * GV // 2:(k + 1) * GV // 2]
                            ve.load(half, offs[0][:, bass.ds(r * GV + k * (GV // 2), GV // 2)])
                            off.extend(ve.snap(x, min_val=0, max_val=(BLOCKS - 1) * H * SLOT) for x in half)

                    def one_hot(j):
                        if not new:
                            return
                        wait(ve, s["mm_done"], GV * (g - UNROLL + 1))
                        ve.tensor_tensor(S[:, u, QV * j:QV * j + QV, :],
                                         iota_n[:, 0:BN].unsqueeze(1).to_broadcast([P, QV, BN]),
                                         lid[:, bass.ds(g * GV + QV * j, QV)].unsqueeze(2).to_broadcast([P, QV, BN]),
                                         ALU.is_equal).then_inc(s.sem["S_ready"], 1)

                    def qk_product(j):
                        if not new or n == 0:
                            return
                        ve.wait_ge(s_gath[u][j], gathered(n, u, i))
                        wait(ve, s["expanded"], 4 * g + j + 1)
                        wait(ve, s["score_parts"], 4 * g + j - 1)
                        ve.tensor_tensor(prod[:, j % 2, :].rearrange("p (v f) -> p v f", v=QV),
                                         ex[j % 2][:, :].rearrange("p (v f) -> p v f", v=QV),
                                         G[:, u, QV * j:QV * j + QV, 0:F], ALU.mult).then_inc(s.sem["qk_done"], 1)

                    def qk_sum(j):
                        if not new or n == 0:
                            return
                        wait(ve, s["qk_done"], 4 * g + j + 1)
                        wait(ve, s["scores_ready"], g)
                        ve.tensor_reduce(raw[:, QV * j:QV * j + QV, :].rearrange("p v h -> p (v h)"),
                                         prod[:, j % 2, :].rearrange("p (c d) -> p c d", d=DH), AX.X,
                                         ALU.add).then_inc(s.sem["score_parts"], 1)

                    def score_sum():
                        if not new or n == 1:
                            return
                        for j in range(GV // QV):
                            ve.wait_ge(s_gath[u][j], gathered(n, u, i))
                        wait(ve, s["es_ready"], g + 1)
                        wait(ve, s["scores_ready"], g)
                        ve.tensor_tensor(raw[:, :, :], es[:, 0, :, :],
                                         G[:, u, :, F:W0], ALU.add).then_inc(s.sem["score_parts"], 1)

                    def scores():
                        if not new:
                            return
                        wait(ve, s["score_parts"], (4 if n else 1) * (g + 1))
                        wait(ve, s["scoreT"], g)
                        if n == 0:
                            ve.scalar_tensor_tensor(sc[:, :, :], raw[:, :, :], SLOPE, raw[:, :, :], op0=ALU.mult,
                                                    op1=ALU.max).then_inc(s.sem["scores_ready"], 1)
                        else:
                            ve.tensor_tensor(sc[:, :, :].rearrange("p v h -> p (v h)"), raw[:, :, :].rearrange("p v h -> p (v h)"),
                                             ebias[:, :, :].rearrange("p v h -> p (v h)")[:, bass.ds(g * P, P)],
                                             ALU.add).then_inc(s.sem["scores_ready"], 1)

                    def loop_max():
                        if not mid or n == 1:
                            return
                        wait(ve, s["scoreT"], q + 1)
                        wait(ve, s["esT_ready"], q + 1)
                        wait(ve, s["f_done"], q)
                        ve.tensor_tensor(smax[:, :], sT[:, 0:P], esT[:, :], ALU.max).then_inc(s.sem["smax_ready"], 1)

                    def edge_scans():
                        if not mid:
                            return
                        wait(ve, s["pcur_ready"], q + 1)
                        if n == 0:
                            wait(ve, s["smax_ready"], q + 1)
                        else:
                            wait(ve, s["scoreT"], q + 1)
                        wait(ve, s["rh_ready"], q)
                        ve.tensor_tensor_scan(FR[:, 0, :], p0, score, LOW, ALU.add, ALU.max).then_inc(s.sem["edge_scans"], 1)
                        ve.tensor_tensor_scan(FR[:, 1, :], p1[:, ::-1], score[:, ::-1], LOW, ALU.add, ALU.max).then_inc(s.sem["edge_scans"], 1)

                    def edge_maxima():
                        if not mid:
                            return
                        wait(ve, s["edge_scans"], 2 * q + 2)
                        wait(ve, s["hop1"], q)
                        ve.tensor_tensor(RH[:, :, :], Vsel[:, :].unsqueeze(1).to_broadcast([P, 2, GV]),
                                         FR[:, :, P - 1:P].to_broadcast([P, 2, GV]), ALU.mult).then_inc(s.sem["rh_ready"], 1)

                    def visit_scans():
                        if not mid:
                            return
                        wait(ve, s["hop1"], q + 1)
                        wait(ve, s["carry"], q)
                        wait(ve, s["hop2"], q)
                        ve.tensor_tensor_scan(d[:, 0, 1:GV + 1], chain_pen[:, 0, bass.ds(q * GV, GV)], sm[0:H, 0:GV],
                                              d[:, 0, 0:1], ALU.add, ALU.max).then_inc(s.sem["x_done"], 1)
                        ve.tensor_tensor_scan(d[:, 1, GV - 1::-1], chain_pen[:, 1, bass.ds(q * GV, GV)],
                                              sm[0:H, GV:2 * GV][:, ::-1], LOW, ALU.add, ALU.max).then_inc(s.sem["u_done"], 1)

                    def carry():
                        if not mid:
                            return
                        wait(ve, s["x_done"], q + 1)
                        ve.tensor_copy(e[:, 0, 0:1], d[:, 0, GV:GV + 1]).then_inc(s.sem["carry"], 1)

                    def outer_maxima():
                        if not mid:
                            return
                        wait(ve, s["hop2"], q + 1)
                        wait(ve, s["cc_done"], q)
                        ve.tensor_tensor(CCM[:, :, :], sm[:, 64:64 + 2 * GV].rearrange("p (k v) -> p k v", k=2),
                                         Vsel[:, :].unsqueeze(1).to_broadcast([P, 2, GV]), ALU.mult).then_inc(s.sem["cc_mul"], 1)

                    def outer_columns():
                        if not mid:
                            return
                        wait(ve, s["cc_mul"], q + 1)
                        wait(ve, s["df"], 2 * q)
                        wait(ve, s["m_done"], q)
                        ve.tensor_reduce(CC[:, :], CCM[:, :, :], AX.X, ALU.add).then_inc(s.sem["cc_done"], 1)

                    def forward_maxima():
                        if not mid:
                            return
                        wait(ve, s["cc_done"], q + 1)
                        wait(ve, s["m_done"], q)
                        ve.tensor_tensor_scan(FF[:, :], p0, score, CC[:, 0:1], ALU.add, ALU.max).then_inc(s.sem["f_done"], 1)

                    def node_maxima():
                        if not mid:
                            return
                        wait(ve, s["f_done"], q + 1)
                        wait(ve, s["dd_ready"], (2 - n) * q)
                        wait(ve, s["df"], 2 * q)
                        ve.tensor_tensor_scan(MM[:, ::-1], p1[:, ::-1], FF[:, ::-1], CC[:, 1:2], ALU.add, ALU.max).then_inc(s.sem["m_done"], 1)

                    def differences():
                        if not mid:
                            return
                        wait(ve, s["m_done"], q + 1)
                        wait(ve, s["p_ready"], q)
                        if n == 0:
                            ve.tensor_tensor(DD[:, 1, :], esT[:, :], MM[:, :], ALU.subtract).then_inc(s.sem["dd_ready"], 1)
                        ve.tensor_tensor(DD[:, 0, :], sT[:, 0:P], MM[:, :], ALU.subtract).then_inc(s.sem["dd_ready"], 1)
                        wait(ve, s["al_mm"], q)
                        wait(ve, s["r8_ready"], q)
                        ve.tensor_tensor(DF[:, 0:1], CC[0:H, 0:1], MM[0:H, 0:1], ALU.subtract).then_inc(s.sem["df"], 1)
                        ve.tensor_scalar(OHF[:, :], iota_n[0:H, 0:BN], first_lid[:, bass.ds(q, 1)], None, op0=ALU.is_equal).then_inc(s.sem["ohf_ready"], 1)

                    def shrink():
                        if not mid:
                            return
                        wait(ve, s["df"], 2 * q + 1)
                        ve.tensor_scalar(DF[:, 1:2], DF[:, 0:1], 0.0, -200.0, op0=ALU.min, op1=ALU.max).then_inc(s.sem["df"], 1)

                    def shrink_heads():
                        if not mid:
                            return
                        wait(ve, s["df"], 2 * q + 2)
                        wait(ve, s["al_mm"], q)
                        ve.tensor_scalar(R8[:, :], ident[0:H, 0:H], DF[:, 1:2], None, op0=ALU.mult).then_inc(s.sem["r8_ready"], 1)

                    def loop_weights():
                        if not mid or n == 1:
                            return
                        wait(ve, s["p_ready"], q + 1)
                        wait(ve, s["pT"], q)
                        ve.scalar_tensor_tensor(PS[:, :], p0, 0.0, EP[:, 1, :], op0=ALU.is_lt, op1=ALU.mult).then_inc(s.sem["ps_ready"], 1)

                    def weigh(j):
                        if not old:
                            return
                        wait(ve, s["pcols"], r + 1)
                        wait(ve, s["mm_done"], GV * r)
                        c0 = F if n else 0
                        rows = G[:, ur, QV * j:QV * j + QV, c0:c0 + F].rearrange("p v (h d) -> p v h d", h=H)
                        ve.tensor_tensor(PV[:, QV * j:QV * j + QV, :, 0:DH], rows,
                                         PV[:, QV * j:QV * j + QV, :, DH:DH + 1].to_broadcast([P, QV, H, DH]), ALU.mult).then_inc(s.sem["pv_ready"], 1)

                    def rescale():
                        if not old:
                            return
                        wait(ve, s["al_ready"], r + 1)
                        wait(ve, s["acc_added"], GV * r)
                        a = acc_f[:, bass.ds(off[0], H * SLOT)].rearrange("p (h k) -> p h k", h=H)
                        ve.tensor_tensor(a, a, AL[:, :].unsqueeze(2).to_broadcast([BN, H, SLOT]), ALU.mult).then_inc(s.sem["rescaled"], 1)

                    def add(v):
                        if not old:
                            return
                        if v == 0:
                            wait(ve, s["rescaled"], r + 1)
                        if v % 2 == 0:
                            wait(ve, s["mm_done"], GV * r + v + 2)
                        wait(ve, s["acc_added"], GV * r + v)
                        a = acc_f[:, bass.ds(off[v], H * SLOT)]
                        o = ms[v % 4 // 2][0:BN, (v % 2) * 256:(v % 2) * 256 + H * SLOT]
                        ve.tensor_tensor(a, a, o, ALU.add).then_inc(s.sem["acc_added"], 1)

                    one_hot(0)
                    load_offsets(0)
                    weigh(0)
                    load_offsets(1)
                    loop_max()
                    weigh(1)
                    edge_scans()
                    rescale()
                    edge_maxima()
                    one_hot(1)
                    add(0)
                    visit_scans()
                    add(1)
                    carry()
                    one_hot(2)
                    add(2)
                    weigh(2)
                    outer_maxima()
                    add(3)
                    outer_columns()
                    add(4)
                    forward_maxima()
                    add(5)
                    node_maxima()
                    one_hot(3)
                    add(6)
                    differences()
                    weigh(3)
                    add(7)
                    shrink()
                    qk_product(0)
                    add(8)
                    shrink_heads()
                    qk_sum(0)
                    add(9)
                    qk_product(1)
                    add(10)
                    loop_weights()
                    qk_sum(1)
                    add(11)
                    qk_product(2)
                    add(12)
                    qk_sum(2)
                    add(13)
                    qk_product(3)
                    score_sum()
                    add(14)
                    qk_sum(3)
                    add(15)
                    scores()

                run_groups(ve, step)
                wait(ve, s["acc_added"], GV * GROUPS)

            layer(0)
            ve.wait_ge(a_out, GROUPS)
            v3 = eb_nat[:, 0:TILES * H].rearrange("p (c h) -> p c h", h=H)
            ve.tensor_tensor(v3, v3, be_r[:, :].unsqueeze(1).to_broadcast([P, TILES, H]), ALU.add).then_inc(s_ebfin, 1)
            accs = acc[:, :, :].rearrange("p b (h k) -> p b h k", h=H)
            lsum, pself = accs[:, :, :, DH], accs[:, :, :, DH + 1]

            def bh(t):
                return t.unsqueeze(3).to_broadcast([BN, BLOCKS, H, DH])

            def flat(t):
                return t.rearrange("p b (h d) -> p b h d", d=DH)

            accm = accs[:, :, :, 0:DH]
            then(ve.tensor_tensor(nst[:, 0, :, :], lsum, pself, ALU.add))
            then(ve.tensor_scalar(nst[:, 1, :, :], nst[:, 0, :, :], 0.0, None, op0=ALU.is_equal))
            then(ve.tensor_tensor(nst[:, 2, :, :], nst[:, 1, :, :], pself, ALU.add))
            then(ve.tensor_tensor(nst[:, 3, :, :], nst[:, 1, :, :], nst[:, 0, :, :], ALU.add))
            then(ve.reciprocal(nst[:, 4, :, :], nst[:, 3, :, :]))
            then(ve.tensor_tensor(flat(work), flat(h0[:, :, 0:F]), bh(nst[:, 2, :, :]), ALU.mult))
            then(ve.tensor_tensor(flat(work), flat(work), accm, ALU.add))
            then(ve.tensor_tensor(flat(work), flat(work), bh(nst[:, 4, :, :]), ALU.mult))
            then(ve.tensor_tensor(work, work, xs[:, :, :], ALU.add))
            then(ve.tensor_tensor(xs[:, :, :], work, rowv[:, 0, :].unsqueeze(1).to_broadcast([BN, BLOCKS, F]), ALU.add))
            then(ve.memset(acc[:, :, :], 0.0))
            then(ve.memset(D[:, :, :, :], LOW))
            layernorm(L[1], xs, hn, True)
            ve.wait_ge(s_ebout, 16)
            for b in range(BLOCKS):
                wait(ve, L[1]["feat_done"], b + 1)
                then(ve.tensor_tensor(q_sb[:, b, :], ex[b % 2][0:BN, 0:F], rowv[:, 1, :], ALU.add))
                ve.tensor_tensor(kv[:, b, :], ex[b % 2][0:BN, F:3 * F], rowv[:, 2:4, :].rearrange("p k f -> p (k f)"),
                                 ALU.add).then_inc(L[1].sem["feat_out"], 1)
            ve.wait_ge(s_ebe, H)
            layer(1)
            then(ve.tensor_scalar(nst[:, 0, :, :], lsum, 1e-8, None, op0=ALU.add))
            then(ve.reciprocal(nst[:, 1, :, :], nst[:, 0, :, :]))
            ve.tensor_tensor(flat(work2), accm, bh(nst[:, 1, :, :]), ALU.mult).then_inc(s_fin_on, 1)
            then(ve.tensor_tensor(hn[:, :, :], hn[:, :, :], rowv[:, 4, :].unsqueeze(1).to_broadcast([BN, BLOCKS, F]), ALU.add))
            for n, (b0, nb) in enumerate(CHUNKS):
                ve.wait_ge(s_fo, n + 1)
                ve.tensor_tensor(hn[:, b0:b0 + nb, :], ex[n % 2][0:BN, 0:nb * F].rearrange("p (b f) -> p b f", b=nb),
                                 hn[:, b0:b0 + nb, :], ALU.add).then_inc(s_fh, 1)
            ve.wait_ge(s_fh, len(CHUNKS))
            layernorm(F_, hn, work, False)
            then(ve.tensor_tensor(work, work, rowv[:, 5, :].unsqueeze(1).to_broadcast([BN, BLOCKS, F]), ALU.mult))
            then(ve.tensor_tensor(work, work, rowv[:, 6, :].unsqueeze(1).to_broadcast([BN, BLOCKS, F]), ALU.add))
            ve.tensor_tensor(work, work, xs[:, :, :], ALU.add).then_inc(s_out, 1)


_INS = ['x', 'src', 'dst', 'edge_attr_32', 'L0_gnn_W', 'L0_gnn_att', 'L0_gnn_bias', 'L1_gnn_Wq', 'L1_gnn_bq',
        'L1_gnn_Wk', 'L1_gnn_bk', 'L1_gnn_Wv', 'L1_gnn_bv', 'L1_gnn_We', 'L1_gnn_be', 'L1_gnn_Wo', 'L1_gnn_bo',
        'L1_gnn_gamma', 'L1_gnn_beta']
_OUTS = [((3125, 128), 'float32')]


def kernel(**inputs):
    import numpy as _np
    import concourse.bacc as _bacc
    from concourse import mybir as _mybir
    from concourse.bass_utils import run_bass_kernel_spmd as _run

    nc = _bacc.Bacc("TRN2", target_bir_lowering=False, num_devices=1)
    arrays, args = {}, []
    for name in _INS:
        a = _np.ascontiguousarray(inputs[name])
        arrays[f"in_{name}_dram"] = a
        args.append(nc.dram_tensor(f"in_{name}_dram", a.shape, _mybir.dt.from_np(a.dtype), kind="ExternalInput").ap())
    for i, (shape, dtype) in enumerate(_OUTS):
        dt = _mybir.dt.from_np(_np.dtype(dtype))
        args.append(nc.dram_tensor(f"out_{i}_dram", shape, dt, kind="ExternalOutput").ap())
    gnn_kernel(nc, *args)
    r = _run(nc, [arrays], core_ids=[0])
    got = tuple(r.results[0][f"out_{i}_dram"] for i in range(len(_OUTS)))
    return got[0]
```

```python
from contextlib import ExitStack

import concourse.bass as bass
from concourse import mybir

F32 = mybir.dt.float32
BF16 = mybir.dt.bfloat16
I32 = mybir.dt.int32
ALU = mybir.AluOpType
ACT = mybir.ActivationFunctionType
AX = mybir.AxisListType

NODES, EDGES, F, ED, H = 3125, 53125, 128, 32, 8
DH = F // H
P = 128
BN = 125
BLOCKS = NODES // BN
TILES = -(-EDGES // P)
FULL = EDGES // P
REST = EDGES - FULL * P
GV = P // H
GROUPS = -(-(TILES + BLOCKS - 1) // GV)
VISITS = GROUPS * GV
UNROLL = 3
QV = 4
VP = 112
VK = VISITS // VP
GK = VP // GV
SLOT = DH + 2
W0 = F + H
W1 = 2 * F
ROW = 2 * P + 2
ATTR_C = 16
PAD_DST = 4000
BIG = float(2 ** 100)
LOW = -BIG
SLOPE = 0.2
CHUNKS = [(s, min(3, BLOCKS - s)) for s in range(0, BLOCKS, 3)]
FEAT_BANKS = 4


class Signal:

    def __init__(self, s, base):
        self.s, self.base = s, base


def gnn_kernel(nc, x, src, dst, edge_attr, w0, att, bias0, wq, bq, wk, bk, wv, bv, we, be, wo, bo, gamma,
               beta, out):
    ctx = ExitStack()

    def sb(name, shape, dt=F32):
        return ctx.enter_context(nc.sbuf_tensor(name, shape, dt))

    def sem(name):
        return ctx.enter_context(nc.semaphore(name))

    def wait(eng, s, value):
        if not isinstance(value, int) or value > 0:
            if isinstance(s, Signal):
                eng.wait_ge(s.s, s.base + value)
            else:
                eng.wait_ge(s, value)

    with ctx:
        edge_rows = nc.dram_tensor("edge_rows", (TILES + 1, ROW), I32, kind="Internal").ap()
        bias_rows = nc.dram_tensor("bias_rows", (TILES + 1, P * H), F32, kind="Internal").ap()
        attr_tail = nc.dram_tensor("attr_tail", (GROUPS * ATTR_C, ED), F32, kind="Internal").ap()
        table0 = nc.dram_tensor("table0", (NODES, W0), F32, kind="Internal").ap()
        table1 = nc.dram_tensor("table1", (NODES, W1), F32, kind="Internal").ap()

        xs = sb("xs", [BN, BLOCKS, F])
        hn = sb("hn", [BN, BLOCKS, F])
        h0b = sb("h0b", [P, VISITS * H])
        h0 = h0b[0:BN, 0:BLOCKS * W0].rearrange("p (b f) -> p b f", f=W0)
        ebias = h0b[:, 0:VISITS * H].rearrange("p (v h) -> p v h", h=H)
        nd = sb("nd", [BN, BLOCKS, 2 * H])
        nd3 = sb("nd3", [BN, BLOCKS, 3, 2 * H], BF16)
        acc = sb("acc", [BN, BLOCKS, H * SLOT])
        qe = sb("qe", [P, VISITS * H])
        eb_nat = qe[:, 0:VISITS * H]
        q_sb = qe[0:BN, 0:BLOCKS * F].rearrange("p (b f) -> p b f", f=F)
        G = sb("G", [P, UNROLL, GV, W1])
        kv = G[0:BN, :, :, :].rearrange("p u v f -> p (u v f)")[:, 0:BLOCKS * W1].rearrange(
            "p (b f) -> p b f", f=W1)
        work = G[0:BN, :, :, :].rearrange("p u v f -> p (u v f)")[:, 0:BLOCKS * F].rearrange(
            "p (b f) -> p b f", f=F)
        work2 = G[0:BN, :, :, :].rearrange("p u v f -> p (u v f)")[:, BLOCKS * F:2 * BLOCKS * F].rearrange(
            "p (b f) -> p b f", f=F)
        bias_v = G[0:VP, :, :, :].rearrange("p u v f -> p (u v f)")[:, 8192:8192 + VK * P * H].rearrange(
            "p (k e h) -> p k e h", k=VK, h=H)
        rows_i = G[0:VP, :, :, :].rearrange("p u v f -> p (u v f)")[:, 0:VK * ROW].bitcast(I32).rearrange(
            "p (k r) -> p k r", k=VK)
        S = sb("S", [P, UNROLL, GV, BN])
        ST_ = sb("ST", [P, GV, P])
        ST = ST_[0:BN, :, :]
        ST_b = ST_[0:BN, :, :].rearrange("p v e -> p (v e)").bitcast(BF16)[:, 0:GV * P].rearrange("p (v e) -> p v e", v=GV)
        PV = sb("PV", [P, GV, H, SLOT])
        prod = sb("prod", [P, UNROLL, QV * F])
        attr_in = prod
        rows = sb("rows", [P, 2, VISITS])
        chain_pen = rows[0:H, :, :]
        offs = [rows[32 * k + 32:32 * k + 33, 0, :].bitcast(I32) for k in range(3)]

        def views(tensor, start, shapes):
            made, at = [], start
            for parts, shape, dt in shapes:
                size = 1
                for d in shape:
                    size *= d
                v = tensor[0:parts, at:at + size]
                if dt is not F32:
                    v = v.bitcast(dt)
                names = "abc"[:len(shape)]
                made.append(v.rearrange(f"p ({' '.join(names)}) -> p {' '.join(names)}", **dict(zip(names, shape)))
                            if len(shape) > 1 else v)
                at += size
            return made

        S_flat = S[:, :, :, :].rearrange("p k v n -> p (k v n)")
        work3 = S_flat[0:BN, 0:BLOCKS * F].rearrange("p (b f) -> p b f", f=F)
        dst_nat, ge, vend, vtmp, lid_v, FLB_, cmpb, iota_i = views(S_flat, 0, (
            (TILES // QV, (QV * P,), I32), (BLOCKS - 1, (2, TILES), F32), (VP, (TILES,), F32), (VP, (2, TILES), F32),
            (VP, (VK, P), F32), (TILES // QV, (2 * QV, BLOCKS - 1), F32), (VP, (VK, BLOCKS - 1), F32), (P, (P,), I32)))
        HT, Rep = views(ST_[:, :, :].rearrange("p v e -> p (v e)"), 0, (
            (P, (2, 3 * BN), F32), (VP, (GK, GV * H), F32)))
        nst_, rows_f = views(PV[:, :, :, :].rearrange("p v h k -> p (v h k)"), 0, (
            (BN, (6, BLOCKS * H), F32), (VP, (VK, ROW), F32)))
        nst = nst_.rearrange("p k (b h) -> p k b h", h=H)
        pen = sb("pen", [P, GROUPS, P + 1], BF16)
        pcur = sb("pcur", [P, UNROLL, P + 1], BF16)
        idx_all = sb("idx_all", [P, VISITS + UNROLL * GV], I32)
        idx_stage = sb("idx_stage", [P, UNROLL, GV], I32)
        lid = sb("lid", [P, VISITS])
        first_lid = sb("first_lid", [H, GROUPS])
        raw = sb("raw", [P, GV, H])
        sc = sb("sc", [P, GV, H])
        es = sb("es", [P, 2, GV, H])
        esT = sb("esT", [P, P])
        smax = sb("smax", [P, P])
        FR = sb("FR", [P, 2, P])
        RH = sb("RH", [P, 2, GV])
        D = sb("D", [H, UNROLL, 2, GV + 1])
        CCM = sb("CCM", [P, 2, GV])
        CC = sb("CC", [P, 2])
        FF = sb("FF", [P, P])
        MM = sb("MM", [P, P])
        DD = sb("DD", [P, 2, P])
        EP = sb("EP", [P, 2, P])
        PS = sb("PS", [P, P])
        DF = sb("DF", [H, 2])
        R8 = sb("R8", [H, H])
        OHF = sb("OHF", [H, BN])
        AL = sb("AL", [BN, H])
        attrT = sb("attrT", [P, QV * P])
        ident = sb("ident", [P, P])
        ones = sb("ones", [P, P])
        iota_n = sb("iota_n", [P, P])
        thr_row = sb("thr_row", [P, BLOCKS - 1])
        thr_i = sb("thr_i", [P, BLOCKS - 1], I32)
        thr_col = sb("thr_col", [P, 1])
        vcol = sb("vcol", [VP, VK])
        vcol_i = sb("vcol_i", [VP, VK + 1], I32)
        headmask = sb("headmask", [P, H])
        Vsel = sb("Vsel", [P, GV])
        HselT = sb("HselT", [H, GV, H])
        Hsel = sb("Hsel", [P, H])
        E0 = sb("E0", [P, H])
        pad_i = sb("pad_i", [1, 2, P + 2], I32)
        FL = sb("FL", [TILES // QV, 2, QV])
        vstat = sb("vstat", [VP, 10, VK])
        tidx = sb("tidx", [VP, VK], I32)
        chain_b = sb("chain_b", [VP, 2, VK, H])
        w0n = sb("w0n", [F, F])
        attc = sb("attc", [P, 2])
        attblk = sb("attblk", [P, 2 * H])
        WA = sb("WA", [P, F + 2 * H])
        Wqkv = sb("Wqkv", [P, 3 * F])
        Wo = sb("Wo", [P, F])
        WeBD = sb("WeBD", [P, QV, H])
        rowv = sb("rowv", [BN, 7, F])
        be_r = sb("be_r", [P, H])
        st = sb("st", [BN, 6, BLOCKS])

        bank = [ctx.enter_context(nc.psum_tensor(f"bank{i}", [P, 512], F32)) for i in range(8)]
        tp = bank[0:2]
        ex = bank[2:4]
        ms = bank[4:6]
        sT = bank[6]
        sm = bank[7]

        s_dst, s_x, s_w, s_pad, s_er, s_bz = (sem(n) for n in (
            "dst_in", "x_in", "weights_in", "pads_out", "edge_rows_out", "bias_pad_out"))
        s_tail = sem("attr_tail_out")
        s_attr = [sem(f"attr_in{k}") for k in range(UNROLL)]
        s_rows = sem("rows_in")
        s_const = sem("constants")
        s_pool = sem("pool_done")
        s_v = sem("vector_done")
        s_fl, s_flT, s_ge, s_diff = sem("firsts_lasts"), sem("firsts_lasts_rows"), sem("block_steps"), sem("steps_summed")
        s_tidx, s_rowsf, s_vlid = sem("tile_index"), sem("rows_as_float"), sem("visit_ids")
        s_vt, s_vte = sem("visit_transposes"), sem("visit_copies")
        s_pent, s_pene = sem("pen_spread"), sem("pen_copied")
        s_penfree = sem("pen_bank_free")
        s_idx0 = sem("first_indices")
        s_watt, s_wps, s_wc = sem("att_blocks"), sem("weights_products"), sem("weights_ready")
        s_tab = [sem("table0_out"), sem("table1_out")]
        s_ebout, s_ebin, s_ebt, s_ebe = sem("bias_rows_out"), sem("bias_rows_in"), sem("bias_transposed"), sem("bias_copied")
        s_ebfin = sem("bias_complete")
        s_out = sem("out_written")
        s_xb, s_self, s_hp, s_kvb, s_hrelu, s_xbeta, s_hbo, s_norm, s_res = (sem(n) for n in (
            "x_plus_bias0", "loop_sums", "loop_messages", "keys_values_complete", "h_rectified", "x_plus_beta", "h_plus_bo",
            "normalised", "result"))
        s_go = sem("quarters_gathered")

        NODE_SEMS = ("xc", "sq", "var", "std", "hn", "hT_ps", "hT", "feat", "feat_out", "feat_done", "kv_copied")
        LOOP_SEMS = dict(S_ready=4, t_done=4, st_ready=4, expanded=4, qk_done=0, score_parts=1, scores_ready=1,
                         es_ready=1, scoreT=1, esT_ready=1, smax_ready=1, edge_scans=2, rh_ready=1, hop1=1, x_done=1,
                         carry=1, u_done=1, hop2=1, cc_mul=1, cc_done=1, f_done=1, m_done=1, dd_ready=2, p_ready=1,
                         ps_ready=1, pT=1, pcols=1, pv_ready=4, mm_done=GV, acc_added=GV, df=2, r8_ready=1,
                         ohf_ready=1, al_mm=1, al_ready=1, rescaled=1, idx_staged=1, pcur_ready=1)
        loop_sem = {k: sem(k) for k in LOOP_SEMS}

        class Layer:
            def __init__(self, n):
                self.sem = {k: sem(f"{k}_{n}") for k in NODE_SEMS} | loop_sem
                self.base = {k: (n == 1) * GROUPS * v for k, v in LOOP_SEMS.items()}

            def __getitem__(self, k):
                return Signal(self.sem[k], self.base.get(k, 0))

        L = [Layer(0), Layer(1)]
        s_gath = [[sem(f"gathered_{u}_{j}") for j in range(GV // QV)] for u in range(UNROLL)]
        a_T, a_Te, a_mm, a_out = sem("attrT_ps"), sem("attrT"), sem("bias_mm"), sem("bias_sb")
        s_fin_on, s_fT, s_fTe, s_fo, s_fh = (sem(n) for n in ("mean_msgs", "msgsT_ps", "msgsT", "projected", "projected_used"))
        X1 = sem("x1_ready")
        NODE_SEMS = NODE_SEMS[:5]
        F_ = Layer("f")

        NPOOL = 16
        block = ctx.enter_context(nc.Block())

        def gathered(n, u, i):
            return 16 * QV * (i + 1 + n * len(range(u, GROUPS, UNROLL)))

        def feat_bank(b):
            return (ex + ms)[b % FEAT_BANKS]

        def run_groups(eng, step, behind=2):
            for g in range(UNROLL + 1):
                step(g, g % UNROLL, g // UNROLL, True, g > 0, g > 1)
            with eng.Fori(1, (GROUPS - 1) // UNROLL) as i:
                for k in range(UNROLL):
                    step(UNROLL * i + (1 + k), (1 + k) % UNROLL, i + (1 + k) // UNROLL, True, True, True)
            for g in range(GROUPS, GROUPS + behind):
                step(g, g % UNROLL, g // UNROLL, False, g == GROUPS, True)

        @block.sync
        def _(sp):
            sp.wait_ge(s_const, 1)
            a = 96 * QV * P
            sp.dma_start(dst_nat[0:96, :], dst[0:a].rearrange("(p c) -> p c", p=96)).then_inc(s_dst, 16)
            b = 103 * QV * P
            sp.dma_start(dst_nat[96:103, :], dst[a:b].rearrange("(p c) -> p c", c=QV * P)).then_inc(s_dst, 16)
            sp.dma_start(dst_nat[103:104, 0:EDGES - b], dst[b:EDGES].rearrange("(a c) -> a c", a=1)).then_inc(s_dst, 16)
            sp.dma_start(edge_rows[0:FULL, 0:P], src[0:FULL * P].rearrange("(t c) -> t c", c=P)).then_inc(s_er, 16)
            sp.dma_start(edge_rows[1:FULL, P:ROW],
                         bass.AP(tensor=dst.tensor, offset=P - 1, ap=[[P, FULL - 1], [1, P + 2]])).then_inc(s_er, 16)
            sp.dma_start(edge_rows[0:1, P + 1:ROW], dst[0:P + 1].rearrange("(a c) -> a c", a=1)).then_inc(s_er, 16)
            sp.dma_start(edge_rows[FULL:FULL + 1, 0:REST], src[FULL * P:EDGES].rearrange("(a c) -> a c", a=1)).then_inc(s_er, 16)
            sp.dma_start(edge_rows[FULL:FULL + 1, P:P + 1 + REST],
                         dst[FULL * P - 1:EDGES].rearrange("(a c) -> a c", a=1)).then_inc(s_er, 16)
            sp.dma_start(edge_rows[0:1, P:P + 1], pad_i[0:1, 0, P:P + 1]).then_inc(s_er, 16)
            sp.dma_start(edge_rows[FULL:FULL + 1, REST:P], pad_i[0:1, 0, 0:P - REST]).then_inc(s_er, 16)
            sp.dma_start(edge_rows[FULL + 1:FULL + 2, 0:P], pad_i[0:1, 0, 0:P]).then_inc(s_er, 16)
            sp.dma_start(edge_rows[FULL:FULL + 1, P + 1 + REST:ROW], pad_i[0:1, 1, 0:P + 1 - REST]).then_inc(s_er, 16)
            sp.dma_start(edge_rows[FULL + 1:FULL + 2, P:ROW], pad_i[0:1, 1, :]).then_inc(s_er, 16)
            sp.dma_start(xs[:, :, :], x.rearrange("(b p) f -> p b f", p=BN)).then_inc(s_x, 16)
            m = EDGES - 127 * TILES
            sp.dma_start(attr_tail[0:m, :], edge_attr[127 * TILES:EDGES, :]).then_inc(s_tail, 16)
            sp.dma_start(attr_tail[m:m + P, :], ones[:, 0:ED]).then_inc(s_tail, 16)
            rest = GROUPS * ATTR_C - m - P
            sp.dma_start(attr_tail[m + P:m + P + rest, :], ones[0:rest, 0:ED]).then_inc(s_tail, 16)
            sp.wait_ge(s_v, 5)
            sp.dma_start(bias_rows[TILES:TILES + 1, :], acc[0:1, :, :].rearrange("p b f -> p (b f)")[:, 0:P * H]).then_inc(s_bz, 16)
            table0_v = table0.rearrange("(b p) f -> p b f", p=BN)
            for n, (b0, nb) in enumerate(CHUNKS):
                wait(sp, L[0]["feat_out"], n + 1)
                sp.dma_start(table0_v[:, b0:b0 + nb, :], h0[:, b0:b0 + nb, :]).then_inc(s_tab[0], 16)
            sp.wait_ge(s_tail, 48)
            sp.wait_ge(s_penfree, -(-GROUPS // 3))

            def step(g, u, i, new, mid, old):
                wait(sp, a_T, g - UNROLL + 1)
                to = attr_in[:, u, :]
                for lo, hi in ((0, 112), (112, 127)):
                    sp.dma_start(to[lo:hi, :],
                                 bass.AP(tensor=edge_attr.tensor, offset=lo * TILES * ED + g * (ATTR_C * ED),
                                         ap=[[TILES * ED, hi - lo], [1, ATTR_C * ED]])).then_inc(s_attr[u], 16)
                sp.dma_start(to[127:128, :], bass.AP(tensor=attr_tail.tensor, offset=g * (ATTR_C * ED),
                                                     ap=[[ATTR_C * ED, 1], [1, ATTR_C * ED]])).then_inc(s_attr[u], 16)

            run_groups(sp, step, behind=0)
            sp.wait_ge(a_out, GROUPS)
            sp.dma_start(bias_rows.rearrange("t c -> (t c)")[0:P * TILES * H].rearrange("(p c) -> p c", p=P),
                         eb_nat[:, 0:TILES * H]).then_inc(s_ebout, 16)
            table1_v = table1.rearrange("(b p) f -> p b f", p=BN)
            for n, (b0, nb) in enumerate(CHUNKS):
                wait(sp, s_kvb, n + 1)
                sp.dma_start(table1_v[:, b0:b0 + nb, :], kv[:, b0:b0 + nb, :]).then_inc(s_tab[1], 16)
            out_v = out.rearrange("(b p) f -> p b f", p=BN)
            for n, (b0, nb) in enumerate(CHUNKS):
                sp.wait_ge(s_res, n + 1)
                sp.dma_start(out_v[:, b0:b0 + nb, :], work[:, b0:b0 + nb, :]).then_inc(s_out, 16)
            sp.wait_ge(s_out, 16 * len(CHUNKS))
            sp.wait_ge(s_tab[0], 16 * len(CHUNKS))
            sp.wait_ge(s_tab[1], 16 * len(CHUNKS))
            sp.wait_ge(s_ebout, 16)
            sp.wait_ge(s_er, 160)
            sp.wait_ge(s_bz, 16)

        @block.gpsimd
        def _(pool):
            n = [0]
            Rep4 = Rep.rearrange("p r (v h) -> p r v h", h=H)

            def then(ins):
                n[0] += 1
                ins.then_inc(s_pool, 1)
                pool.wait_ge(s_pool, n[0])

            pool.memset(pad_i[0:1, 0, 0:P], 0).then_inc(s_pool, 1)
            pool.memset(pad_i[0:1, 0, P:P + 2], -1).then_inc(s_pool, 1)
            pool.memset(pad_i[0:1, 1, :], PAD_DST).then_inc(s_pool, 1)
            pool.memset(ones[:, :], 1.0).then_inc(s_pool, 1)
            n[0] = 4
            then(pool.memset(dst_nat, NODES - 1))
            pool.sem_inc(s_const, 1)
            pool.memset(ident[:, :], 0.0).then_inc(s_pool, 1)
            pool.memset(HselT[:, :, :], 0.0).then_inc(s_pool, 1)
            pool.memset(Rep, 0.0).then_inc(s_pool, 1)
            n[0] += 3
            then(pool.memset(E0[:, :], 0.0))
            pool.iota(iota_i[:, :], pattern=[[1, P]], base=0, channel_multiplier=0).then_inc(s_pool, 1)
            pool.iota(thr_i[:, :], pattern=[[BN, BLOCKS - 1]], base=BN, channel_multiplier=0).then_inc(s_pool, 1)
            pool.iota(vcol_i[:, 0:VK], pattern=[[VP, VK]], base=0, channel_multiplier=1).then_inc(s_pool, 1)
            pool.iota(vcol_i[:, VK:VK + 1], pattern=[[0, 1]], base=BN, channel_multiplier=BN).then_inc(s_pool, 1)
            n[0] += 4
            then(pool.affine_select(out=ident[:, :], in_=ident[:, :], compare_op=ALU.not_equal, fill=1.0,
                                    base=0, pattern=[[-1, P]], channel_multiplier=1))
            then(pool.affine_select(out=E0[:, :], in_=E0[:, :], compare_op=ALU.not_equal, fill=1.0,
                                    base=0, pattern=[[0, H]], channel_multiplier=1))
            pool.sem_inc(s_const, 1)
            then(pool.affine_select(out=HselT[:, :, :], in_=HselT[:, :, :], compare_op=ALU.not_equal, fill=1.0,
                                    base=0, pattern=[[0, GV], [-1, H]], channel_multiplier=1))
            then(pool.affine_select(out=Rep4, in_=Rep4, compare_op=ALU.not_equal, fill=1.0,
                                    base=0, pattern=[[-GV, GK], [-1, GV], [0, H]], channel_multiplier=1))
            for t, w, k in ((headmask, H, DH), (Vsel, GV, H)):
                then(pool.affine_select(out=t[:, :], in_=ones[:, 0:w], compare_op=ALU.is_ge, fill=0.0,
                                        base=0, pattern=[[-k, w]], channel_multiplier=1))
                then(pool.affine_select(out=t[:, :], in_=t[:, :], compare_op=ALU.is_ge, fill=0.0,
                                        base=k - 1, pattern=[[k, w]], channel_multiplier=-1))
            pool.sem_inc(s_const, 1)

            pool.wait_ge(s_er, 160)
            pool.wait_ge(s_tidx, 1)
            for k in range(VK):
                pool.indirect_dma_start(rows_i[:, k, :], None, edge_rows,
                                        bass.IndirectOffsetOnAxis(ap=tidx[:, k:k + 1], axis=0)).then_inc(s_rows, 16)

            def gathers(n, table, w):
                s = L[n]

                def step(g, u, i, new, mid, old):
                    wait(pool, s["idx_staged"], g - (UNROLL - 1))
                    for j in range(GV // QV):
                        wait(pool, s["pv_ready"], 4 * (g - UNROLL) + j + 1)
                        pool.sem_inc(s_go, 1)
                        for v in range(QV * j, QV * j + QV):
                            pool.indirect_dma_start(
                                G[:, u, v, 0:w], None, table,
                                bass.IndirectOffsetOnAxis(ap=idx_stage[:, u, v:v + 1], axis=0)
                            ).then_inc(s_gath[u][j], 16)

                run_groups(pool, step, behind=0)

            pool.wait_ge(s_idx0, 1)
            pool.wait_ge(s_tab[0], 16 * len(CHUNKS))
            gathers(0, table0, W0)
            pool.wait_ge(s_w, 19 * 16)
            pool.tensor_tensor(xs[:, :, :], xs[:, :, :], rowv[:, 0, :].unsqueeze(1).to_broadcast([BN, BLOCKS, F]), ALU.add).then_inc(s_xb, 1)
            pool.wait_ge(s_ebout, 16)
            pool.wait_ge(s_bz, 16)
            wait(pool, L[0]["pv_ready"], 4 * GROUPS)
            for k in range(VK):
                pool.indirect_dma_start(bias_v[:, k, :, :].rearrange("p e h -> p (e h)"), None, bias_rows,
                                        bass.IndirectOffsetOnAxis(ap=tidx[:, k:k + 1], axis=0)).then_inc(s_ebin, 16)
            pool.wait_ge(s_self, 1)
            for b0, nb in CHUNKS:
                b = slice(b0, b0 + nb)
                pool.tensor_tensor(hn[:, b, :].rearrange("p b (h d) -> p b h d", d=DH),
                                   h0[:, b, 0:F].rearrange("p b (h d) -> p b h d", d=DH),
                                   nst[:, 2, b, :].unsqueeze(3).to_broadcast([BN, nb, H, DH]), ALU.mult).then_inc(s_hp, 1)
            for b0, nb in CHUNKS:
                wait(pool, L[1]["kv_copied"], b0 + nb)
                pool.tensor_tensor(kv[:, b0:b0 + nb, :], kv[:, b0:b0 + nb, :],
                                   rowv[:, 2:4, :].rearrange("p k f -> p (k f)").unsqueeze(1).to_broadcast([BN, nb, 2 * F]),
                                   ALU.add).then_inc(s_kvb, 1)
            pool.wait_ge(s_tab[1], 16 * len(CHUNKS))
            pool.wait_ge(s_ebt, VK * H)
            pool.wait_ge(s_idx0, 2)
            gathers(1, table1, W1)
            pool.wait_ge(s_hrelu, 1)
            pool.tensor_tensor(hn[:, :, :], hn[:, :, :], rowv[:, 4, :].unsqueeze(1).to_broadcast([BN, BLOCKS, F]), ALU.add).then_inc(s_hbo, 1)
            pool.tensor_tensor(xs[:, :, :], xs[:, :, :], rowv[:, 6, :].unsqueeze(1).to_broadcast([BN, BLOCKS, F]), ALU.add).then_inc(s_xbeta, 1)
            pool.wait_ge(s_xbeta, 1)
            for n, (b0, nb) in enumerate(CHUNKS):
                b = slice(b0, b0 + nb)
                pool.wait_ge(s_norm, n + 1)
                pool.tensor_tensor(work[:, b, :], work[:, b, :], xs[:, b, :], ALU.add).then_inc(s_res, 1)

        @block.scalar
        def _(act):
            act.dma_start(w0n[:, :], w0).then_inc(s_w, 16)
            for k in range(2):
                act.dma_start(attc[:, k:k + 1], att.rearrange("(t p a) -> t p a", p=P, a=1)[k]).then_inc(s_w, 16)
            for k, w in enumerate((wq, wk, wv)):
                act.dma_start(Wqkv[:, F * k:F * k + F], w).then_inc(s_w, 16)
            act.dma_start(Wo[:, :], wo).then_inc(s_w, 16)
            act.wait_ge(s_v, 5)
            for c in range(QV):
                act.dma_start(WeBD[ED * c:ED * c + ED, c, :], we).then_inc(s_w, 16)
            for k, b in enumerate((bias0, bq, bk, bv, bo, gamma, beta)):
                act.dma_start(rowv[:, k, :], b.rearrange("(a f) -> a f", a=1).to_broadcast([BN, F])).then_inc(s_w, 16)
            act.dma_start(be_r[:, :], be.rearrange("(a f) -> a f", a=1).to_broadcast([P, H])).then_inc(s_w, 16)

            act.wait_ge(s_vt, 2)
            act.activation(idx_all[:, 0:VISITS], tp[0][:, 0:VISITS], ACT.Copy).then_inc(s_vte, 1)
            act.activation(lid[:, :], tp[1][:, 0:VISITS], ACT.Copy).then_inc(s_vte, 1)
            act.wait_ge(s_vte, 2)
            act.activation(idx_stage[:, :, :].rearrange("p u v -> p (u v)"), idx_all[:, 0:UNROLL * GV], ACT.Copy).then_inc(s_idx0, 1)
            act.wait_ge(s_vt, 3)
            for k, w in enumerate((H * SLOT, F, 3 * 2 * H)):
                act.activation(offs[k], ex[0][0:1, 0:VISITS], ACT.Copy, scale=float(w)).then_inc(s_vte, 1)
            act.wait_ge(s_vt, 4)
            for k in range(2):
                to = chain_pen[:, k, :].rearrange("p (g v) -> p g v", v=GV)
                act.activation(to[:, :, ::-1] if k else to, bank[4 + k][0:H, 0:VISITS].rearrange("p (g v) -> p g v", v=GV),
                               ACT.Copy, scale=BIG).then_inc(s_vte, 1)
            act.wait_ge(s_vt, 5)
            act.activation(first_lid[:, :], sm[0:H, 256:256 + GROUPS], ACT.Copy).then_inc(s_vte, 1)

            def deviations(s, c, source, scrap):
                wait(act, s["xc"], c + 1)
                b0, nb = CHUNKS[c]
                for b in range(b0, b0 + nb):
                    last = act.activation(scrap[:, b, :], source[:, b, :], ACT.Square, bias=st[:, 1, b:b + 1],
                                          accum_out=st[:, 2, b:b + 1])
                last.then_inc(s.sem["sq"], 1)

            def root(s, c):
                wait(act, s["var"], c + 1)
                b0, nb = CHUNKS[c]
                act.activation(st[:, 4, b0:b0 + nb], st[:, 3, b0:b0 + nb], ACT.Sqrt).then_inc(s.sem["std"], 1)

            def transposed(s, n, used, count, rectify=True):
                wait(act, s["hT_ps"], n + 1)
                wait(act, used, count)
                nb = CHUNKS[n][1]
                act.activation(HT[:, n % 2, 0:nb * BN], tp[n % 2][:, 0:nb * BN], ACT.Relu if rectify else ACT.Copy).then_inc(s.sem["hT"], 1)

            def features0(n):
                b0, nb = CHUNKS[n]
                if n == 0:
                    wait(act, s_wc, 2)
                wait(act, L[0]["feat"], n + 1)
                got = ex[n % 2][0:BN, 0:nb * (F + 2 * H)].rearrange("p (b f) -> p b f", b=nb)
                act.activation(h0[:, b0:b0 + nb, :], got[:, :, 0:W0], ACT.Copy).then_inc(L[0].sem["feat_out"], 1)
                act.activation(nd[:, b0:b0 + nb, 0:H], got[:, :, W0:W0 + H], ACT.Copy).then_inc(L[0].sem["feat_done"], 1)

            act.wait_ge(s_wps, 2)
            act.activation(WA[:, 0:F], sm[:, 0:F], ACT.Copy).then_inc(s_wc, 1)
            act.activation(WA[:, F:F + 2 * H], sm[:, F:F + 2 * H], ACT.Copy).then_inc(s_wc, 1)
            for k in range(len(CHUNKS) + 3):
                if k < len(CHUNKS):
                    deviations(L[0], k, xs, work2)
                if 0 <= k - 1 < len(CHUNKS):
                    root(L[0], k - 1)
                if 0 <= k - 2 < len(CHUNKS):
                    transposed(L[0], k - 2, L[0]["feat"], k - 3)
                if 0 <= k - 3:
                    features0(k - 3)
            for c in range(-(-GROUPS // 3)):
                ng = min(3, GROUPS - 3 * c)
                act.wait_ge(s_pent, c + 1)
                wait(act, s_penfree, c - 1)
                act.activation(prod[:, c % 2, 0:ng * (P + 2)], ms[c % 2][:, 0:ng * (P + 2)], ACT.Copy,
                               scale=BIG).then_inc(s_pene, 1)

            def layer(n):
                s = L[n]

                pen_f = pen[:, :, :].rearrange("p g e -> p (g e)")

                def evac(g, j):
                    wait(act, s["t_done"], 4 * g + j + 1)
                    wait(act, s["expanded"], 4 * (g - 1) + j + 1)
                    act.activation((ST if n else ST_b)[:, QV * j:QV * j + QV, :],
                                   tp[j % 2][0:BN, :].rearrange("p (v e) -> p v e", v=QV), ACT.Copy).then_inc(s.sem["st_ready"], 1)

                def step(g, u, i, new, mid, old):
                    q = g - 1
                    k = 2 - n
                    if mid and n == 0:
                        wait(act, s["scoreT"], q + 1)
                        wait(act, s["dd_ready"], 2 * q)
                        act.activation(esT[:, :], sT[:, P:2 * P], ACT.Copy).then_inc(s.sem["esT_ready"], 1)
                    if new:
                        for j in range(4):
                            evac(g, j)
                    if mid:
                        wait(act, s["dd_ready"], k * (q + 1))
                        wait(act, s["pT"], q)
                        act.activation(EP[:, 0:k, :], DD[:, 0:k, :], ACT.Exp).then_inc(s.sem["p_ready"], 1)
                    if new:
                        if n == 0:
                            wait(act, s["expanded"], 4 * g + 4)
                            wait(act, s["scoreT"], g)
                            wait(act, s["score_parts"], g)
                            act.activation(es[:, :, :, :], ex[0][:, 0:GV * 2 * H].rearrange("p (v k h) -> p k v h", k=2, h=H), ACT.Copy).then_inc(s.sem["es_ready"], 1)
                            wait(act, a_T, g + 1)
                            wait(act, a_mm, g)
                            act.activation(attrT[:, :], ex[1][:, :], ACT.Copy).then_inc(a_Te, 1)
                    if mid:
                        wait(act, s["al_mm"], q + 1)
                        wait(act, s["rescaled"], q)
                        act.activation(AL[:, :], sm[0:BN, 128:128 + H], ACT.Exp).then_inc(s.sem["al_ready"], 1)
                    if new:
                        wait(act, s["m_done"], g - UNROLL + 1)
                        if n == 0:
                            wait(act, s["ps_ready"], g - UNROLL + 1)
                        act.activation(pcur[:, u, :], pen_f[:, bass.ds(g * (P + 1), P + 1)], ACT.Copy).then_inc(s.sem["pcur_ready"], 1)
                        for j in range(GV // QV):
                            act.wait_ge(s_gath[u][j], gathered(n, u, i))
                        act.activation(idx_stage[:, u, :], idx_all[:, bass.ds((g + UNROLL) * GV, GV)], ACT.Copy).then_inc(s.sem["idx_staged"], 1)
                    if mid:
                        wait(act, s["pT"], q + 1)
                        wait(act, s["mm_done"], GV * q)
                        act.activation(PV[:, :, :, DH:DH + k].rearrange("p v h k -> p (v h) k"),
                                       sT[:, 2 * P:(2 + k) * P].rearrange("p (k c) -> p c k", k=k), ACT.Copy).then_inc(s.sem["pcols"], 1)
                    if new and n == 0:
                        wait(act, a_mm, g + 1)
                        act.activation(eb_nat[:, bass.ds(g * (ATTR_C * H), ATTR_C * H)], sm[:, 256:256 + ATTR_C * H],
                                       ACT.Copy).then_inc(a_out, 1)

                run_groups(act, step)

            act.wait_ge(s_penfree, -(-GROUPS // 3))
            layer(0)
            wait(act, L[0]["idx_staged"], GROUPS)
            act.activation(idx_stage[:, :, :].rearrange("p u v -> p (u v)"), idx_all[:, 0:UNROLL * GV], ACT.Copy).then_inc(s_idx0, 1)
            for k in range(len(CHUNKS) + 3):
                if k < len(CHUNKS):
                    deviations(L[1], k, xs, work3)
                if 0 <= k - 1 < len(CHUNKS):
                    root(L[1], k - 1)
                if 0 <= k - 2 < len(CHUNKS):
                    transposed(L[1], k - 2, L[1]["feat_done"], CHUNKS[k - 3][0] if k > 2 else 0)
                if 0 <= k - 3:
                    b0, nb = CHUNKS[k - 3]
                    for b in range(b0, b0 + nb):
                        wait(act, L[1]["feat_done"], b + 1)
                        act.activation(kv[:, b, :], feat_bank(b)[0:BN, F:3 * F], ACT.Copy).then_inc(L[1].sem["kv_copied"], 1)
            act.activation(hn[:, :, :], hn[:, :, :], ACT.Relu).then_inc(s_hrelu, 1)
            for h in range(H):
                act.wait_ge(s_ebt, VK * (h + 1))
                act.activation(ebias[:, :, h], ms[h % 2][:, 0:VISITS], ACT.Identity, bias=be_r[:, h:h + 1]).then_inc(s_ebe, 1)
            layer(1)
            def msgs_transposed(n):
                act.wait_ge(s_fT, n + 1)
                wait(act, s_fo, n - 1)
                nb = CHUNKS[n][1]
                act.activation(HT[:, n % 2, 0:nb * BN], tp[n % 2][:, 0:nb * BN], ACT.Copy).then_inc(s_fTe, 1)

            msgs_transposed(0)
            msgs_transposed(1)
            for k in range(len(CHUNKS) + 1):
                if k + 2 < len(CHUNKS):
                    msgs_transposed(k + 2)
                if k < len(CHUNKS):
                    deviations(F_, k, hn, work3)
                if k:
                    root(F_, k - 1)

        @block.tensor
        def _(pe):
            regs = [pe.alloc_register(f"pe_off{k}") for k in range(GV)]
            t4 = TILES // QV
            pe.wait_ge(s_const, 2)
            pe.wait_ge(s_fl, 1)
            for w in range(2):
                for k in range(QV):
                    last = pe.matmul(bank[w][0:BLOCKS - 1, k:TILES:QV], FLB_[:, w * QV + k, :], ident[0:t4, 0:t4], start=True, stop=True)
            last.then_inc(s_flT, 1)
            pe.wait_ge(s_ge, 1)
            pe.matmul(bank[2][0:VP, 0:TILES], ones[0:BLOCKS - 1, 0:VP], ge[:, 1, :], start=True, stop=True).then_inc(s_diff, 1)
            pe.wait_ge(s_watt, 1)
            pe.transpose(sm[:, 0:F], w0n[:, :], ident[:, :]).then_inc(s_wps, 1)
            pe.matmul(sm[:, F:F + 2 * H], w0n[:, :], attblk[:, :], start=True, stop=True).then_inc(s_wps, 1)
            pe.wait_ge(s_rowsf, 1)
            iv = ident[0:VP, 0:VP]
            for k in range(VK):
                last = pe.transpose(tp[0][:, VP * k:VP * k + VP], rows_f[:, k, 0:P], iv)
            last.then_inc(s_vt, 1)
            pe.wait_ge(s_vlid, 1)
            for k in range(VK):
                last = pe.transpose(tp[1][:, VP * k:VP * k + VP], lid_v[:, k, :], iv)
            last.then_inc(s_vt, 1)
            for k in range(VK):
                last = pe.matmul(ex[0][0:1, VP * k:VP * k + VP], vstat[:, 5, k:k + 1], iv, start=True, stop=True)
            last.then_inc(s_vt, 1)
            for m in range(2):
                for k in range(VK):
                    last = pe.matmul(bank[4 + m][0:H, VP * k:VP * k + VP],
                                     chain_b[:, m, k, :], iv, start=True, stop=True)
            last.then_inc(s_vt, 1)
            pe.wait_ge(s_vte, 2)
            pe.matmul(sm[0:H, 256:256 + GROUPS], E0[:, :], lid[:, 0:VISITS:GV], start=True, stop=True).then_inc(s_vt, 1)

            def transposes(s, n, b0, nb):
                wait(pe, s["hn"], n + 1)
                wait(pe, s["hT"], n - 1)
                for k in range(nb):
                    last = pe.transpose(tp[n % 2][:, k * BN:k * BN + BN], hn[:, b0 + k, :], ident[0:BN, 0:BN])
                last.then_inc(s.sem["hT_ps"], 1)

            pe.wait_ge(s_vte, 5)
            wait(pe, s_wc, 2)
            for n, (b0, nb) in enumerate(CHUNKS):
                transposes(L[0], n, b0, nb)
                wait(pe, L[0]["hT"], n + 1)
                wait(pe, L[0]["feat_out"], n - 1)
                wait(pe, L[0]["feat_done"], n - 1)
                for k in range(nb):
                    last = pe.matmul(ex[n % 2][0:BN, k * (F + 2 * H):(k + 1) * (F + 2 * H)], HT[:, n % 2, k * BN:k * BN + BN],
                                     WA[:, :], start=True, stop=True)
                last.then_inc(L[0].sem["feat"], 1)
            pe.wait_ge(s_const, 3)
            pe.wait_ge(s_vte, 7)
            for c in range(-(-GROUPS // 3)):
                wait(pe, s_pene, c - 1)
                for g in range(3 * c, min(3 * c + 3, GROUPS)):
                    last = pe.matmul(ms[c % 2][:, (g % 3) * (P + 2):(g % 3 + 1) * (P + 2)],
                                     Rep[:, g % GK, :], rows_f[:, g // GK, P:ROW],
                                     start=True, stop=True)
                last.then_inc(s_pent, 1)

            def layer(n):
                s = L[n]
                width = F if n else 3 * 2 * H
                nodes = q_sb.rearrange("p b f -> p (b f)") if n else nd3[:, :, :, :].rearrange("p b k f -> p (b k f)")

                def one_hot_T(g, u, j):
                    wait(pe, s["S_ready"], 4 * g + j + 1)
                    wait(pe, s["st_ready"], 4 * g + j - 1)
                    for k in range(QV):
                        last = pe.transpose(tp[j % 2][0:BN, k * P:k * P + P], S[:, u, QV * j + k, :], ident[:, :])
                    last.then_inc(s.sem["t_done"], 1)

                def expand(g, j):
                    wait(pe, s["st_ready"], 4 * g + j + 1)
                    if n:
                        wait(pe, s["qk_done"], 4 * g + j - 1)
                    elif j == 0:
                        wait(pe, s["es_ready"], g)
                    for k in range(QV):
                        v = QV * j + k
                        off = pe.snap(regs[v], min_val=0, max_val=(BLOCKS - 1) * width)
                        if n:
                            last = pe.matmul(ex[j % 2][:, k * F:k * F + F], ST[:, v, :], nodes[:, bass.ds(off, F)], start=True, stop=True)
                            continue
                        for part in range(3):
                            last = pe.matmul(ex[0][:, v * 2 * H:(v + 1) * 2 * H], ST_b[:, v, :],
                                             nodes[:, bass.ds(off + part * 2 * H, 2 * H)], start=part == 0, stop=part == 2)
                    last.then_inc(s.sem["expanded"], 1)

                def sums(g, u, p):
                    r, ur = g - 2, (u + 1) % UNROLL
                    if p == 0:
                        wait(pe, s["pcols"], r + 1)
                    if p % 2 == 0:
                        wait(pe, s["pv_ready"], 4 * r + p // 2 + 1)
                    wait(pe, s["acc_added"], GV * r + 2 * p - 2)
                    for k in range(2):
                        pe.matmul(ms[p % 2][0:BN, k * 256:k * 256 + H * SLOT], S[:, ur, 2 * p + k, :],
                                  PV[:, 2 * p + k, :, :].rearrange("p h k -> p (h k)"),
                                  start=True, stop=True).then_inc(s.sem["mm_done"], 1)

                def step(g, u, i, new, mid, old):
                    q = g - 1
                    if mid:
                        wait(pe, s["scores_ready"], q + 1)
                        wait(pe, s["pcols"], q)
                        wait(pe, s["dd_ready"], (2 - n) * q)
                        if n == 0:
                            wait(pe, s["es_ready"], q + 1)
                            wait(pe, s["esT_ready"], q)
                            pe.transpose(sT[:, P:2 * P], es[:, 1, :, :].rearrange("p v h -> p (v h)"), ident[:, :])
                        pe.transpose(sT[:, 0:P], sc[:, :, :].rearrange("p v h -> p (v h)"), ident[:, :]).then_inc(s.sem["scoreT"], 1)
                    if new:
                        pe.load(regs, offs[1 if n else 2][:, bass.ds(g * GV, GV)])
                        one_hot_T(g, u, 0)
                    if old:
                        sums(g, u, 0)
                    if mid:
                        wait(pe, s["rh_ready"], q + 1)
                        wait(pe, s["x_done"], q)
                        wait(pe, s["u_done"], q)
                        wait(pe, s["al_ready"], q)
                        if n == 0:
                            wait(pe, a_out, q + 1)
                        pe.matmul(sm[0:H, 0:2 * GV], Hsel[:, :], RH[:, :, :].rearrange("p k v -> p (k v)"),
                                  start=True, stop=True).then_inc(s.sem["hop1"], 1)
                    if old:
                        sums(g, u, 1)
                    if new:
                        one_hot_T(g, u, 1)
                    if mid:
                        wait(pe, s["x_done"], q + 1)
                        wait(pe, s["u_done"], q + 1)
                        wait(pe, s["carry"], q + 1)
                        wait(pe, s["cc_mul"], q)
                        d = D[:, (u + 2) % UNROLL, :, :]
                        for k in range(2):
                            last = pe.matmul(sm[:, 64 + GV * k:64 + GV * k + GV], HselT[:, :, :].rearrange("p v h -> p (v h)"),
                                             d[:, k, k:k + GV], start=True, stop=True)
                        last.then_inc(s.sem["hop2"], 1)
                    if old:
                        sums(g, u, 2)
                    if new:
                        one_hot_T(g, u, 2)
                    if old:
                        sums(g, u, 3)
                    if new:
                        expand(g, 0)
                        expand(g, 1)
                        one_hot_T(g, u, 3)
                    if old:
                        sums(g, u, 4)
                    if new:
                        expand(g, 2)
                    if old:
                        sums(g, u, 5)
                    if new:
                        expand(g, 3)
                    if old:
                        sums(g, u, 6)
                    if new and n == 0:
                        pe.wait_ge(s_attr[u], 48 * (i + 1))
                        wait(pe, a_Te, g)
                        for k in range(QV):
                            last = pe.transpose(ex[1][:, k * P:k * P + P], attr_in[:, u, k * P:k * P + P], ident[:, :])
                        last.then_inc(a_T, 1)
                    if mid:
                        wait(pe, s["p_ready"], q + 1)
                        if n == 0:
                            wait(pe, s["ps_ready"], q + 1)
                            pe.transpose(sT[:, 3 * P:4 * P], PS[:, :], ident[:, :])
                        pe.transpose(sT[:, 2 * P:3 * P], EP[:, 0, :], ident[:, :]).then_inc(s.sem["pT"], 1)
                        wait(pe, s["r8_ready"], q + 1)
                        wait(pe, s["ohf_ready"], q + 1)
                        pe.matmul(sm[0:BN, 128:128 + H], OHF[:, :], R8[:, :], start=True, stop=True).then_inc(s.sem["al_mm"], 1)
                    if old:
                        sums(g, u, 7)
                    if new and n == 0:
                        wait(pe, a_Te, g + 1)
                        wait(pe, a_out, g)
                        wait(pe, s["al_ready"], g)
                        for k in range(QV):
                            last = pe.matmul(sm[:, 256 + 32 * k:256 + 32 * k + 32], attrT[:, k * P:k * P + P],
                                             WeBD[:, :, :].rearrange("p c h -> p (c h)"), start=True, stop=True)
                        last.then_inc(a_mm, 1)

                run_groups(pe, step)

            pe.wait_ge(s_w, 19 * 16)
            wait(pe, L[0]["feat_done"], len(CHUNKS) + 1)
            layer(0)
            m = 0
            for n, (b0, nb) in enumerate(CHUNKS):
                transposes(L[1], n, b0, nb)
                wait(pe, L[1]["hT"], n + 1)
                for k in range(nb):
                    wait(pe, L[1]["feat_out"], m - FEAT_BANKS + 1)
                    pe.matmul(feat_bank(m)[0:BN, 0:3 * F], HT[:, n % 2, k * BN:k * BN + BN], Wqkv[:, :],
                              start=True, stop=True).then_inc(L[1].sem["feat_done"], 1)
                    m += 1
            wait(pe, L[1]["feat_out"], BLOCKS)
            pe.wait_ge(s_ebin, 16 * VK)
            for h in range(H):
                wait(pe, s_ebe, h - 1)
                for k in range(VK):
                    pe.transpose(ms[h % 2][:, VP * k:VP * k + VP], bias_v[:, k, :, h], ident[0:VP, 0:VP]).then_inc(s_ebt, 1)
            layer(1)
            for n, (b0, nb) in enumerate(CHUNKS):
                pe.wait_ge(s_fin_on, n + 1)
                wait(pe, s_fTe, n - 1)
                for k in range(nb):
                    last = pe.transpose(tp[n % 2][:, k * BN:k * BN + BN], work2[:, b0 + k, :], ident[0:BN, 0:BN])
                last.then_inc(s_fT, 1)
                pe.wait_ge(s_fTe, n + 1)
                wait(pe, s_fh, n - 1)
                for k in range(nb):
                    last = pe.matmul(ex[n % 2][0:BN, k * F:k * F + F], HT[:, n % 2, k * BN:k * BN + BN], Wo[:, :],
                                     start=True, stop=True)
                last.then_inc(s_fo, 1)

        @block.vector
        def _(ve):
            n_v = [0]

            def then(ins):
                n_v[0] += 1
                ins.then_inc(s_v, 1)
                ve.wait_ge(s_v, n_v[0])

            regs = [ve.alloc_register(f"ve_off{k}") for k in range(GV)]
            then(ve.memset(WeBD[:, :, :], 0.0))
            ve.memset(idx_all[:, VISITS:], 0).then_inc(s_v, 1)
            ve.memset(D[:, :, :, :], LOW).then_inc(s_v, 1)
            ve.memset(PV[:, :, :, :], 0.0).then_inc(s_v, 1)
            n_v[0] += 3
            then(ve.memset(acc[:, :, :], 0.0))
            ve.wait_ge(s_const, 2)
            ve.tensor_copy(iota_n[:, :], iota_i[:, :]).then_inc(s_v, 1)
            ve.tensor_copy(thr_row[:, :], thr_i[:, :]).then_inc(s_v, 1)
            ve.tensor_copy(vcol[:, :], vcol_i[:, 0:VK]).then_inc(s_v, 1)
            n_v[0] += 3
            then(ve.tensor_copy(thr_col[0:BLOCKS - 1, :], vcol_i[0:BLOCKS - 1, VK:VK + 1]))
            ve.wait_ge(s_dst, 48)
            then(ve.tensor_copy(FL[:, :, :], dst_nat[:, :].rearrange("p (k c) -> p c k", k=QV)[:, ::P - 1, :]))
            t4 = TILES // QV
            ve.tensor_copy(FLB_,
                           FL[:, :, :].rearrange("p w k -> p (w k)").unsqueeze(2).to_broadcast([t4, 2 * QV, BLOCKS - 1])
                           ).then_inc(s_fl, 1)
            ve.wait_ge(s_flT, 1)
            then(ve.tensor_scalar(ge[:, 0, :], bank[1][0:BLOCKS - 1, 0:TILES], thr_col[0:BLOCKS - 1, :], None, op0=ALU.is_ge))
            ve.scalar_tensor_tensor(ge[:, 1, :], bank[0][0:BLOCKS - 1, 0:TILES], thr_col[0:BLOCKS - 1, :], ge[:, 0, :],
                                    op0=ALU.is_lt, op1=ALU.mult).then_inc(s_ge, 1)
            ve.memset(vtmp[:, 0, :], 1.0).then_inc(s_v, 1)
            n_v[0] += 1
            ve.wait_ge(s_v, n_v[0])
            ve.wait_ge(s_diff, 1)
            then(ve.tensor_tensor_scan(vend[:, :], vtmp[:, 0, :], bank[2][0:VP, 0:TILES], 0.0, ALU.add, ALU.add))
            for k in range(VK):
                then(ve.scalar_tensor_tensor(vtmp[:, 1, :], vend[:, :], vcol[:, k:k + 1], vend[:, :], op0=ALU.is_le, op1=ALU.mult))
                ve.tensor_reduce(vstat[:, 1, k:k + 1], vtmp[:, 1, :], AX.X, ALU.max).then_inc(s_v, 1)
                n_v[0] += 1
                then(ve.tensor_scalar(vtmp[:, 0, :], vend[:, :], vcol[:, k:k + 1], None, op0=ALU.is_le))
                then(ve.tensor_reduce(vstat[:, 0, k:k + 1], vtmp[:, 0, :], AX.X, ALU.add))
            ve.tensor_copy(tidx[:, :], vstat[:, 0, :]).then_inc(s_tidx, 1)

            ve.wait_ge(s_w, 19 * 16)
            ve.wait_ge(s_const, 3)
            for k in range(2):
                ve.tensor_scalar(attblk[:, k * H:k * H + H], headmask[:, :], attc[:, k:k + 1], None, op0=ALU.mult).then_inc(s_v, 1)
            n_v[0] += 2
            ve.wait_ge(s_v, n_v[0])
            ve.sem_inc(s_watt, 1)
            then(ve.tensor_reduce(Hsel[:, :], ident[:, :].rearrange("p (v h) -> p h v", h=H), AX.X, ALU.add))
            then(ve.tensor_scalar(Wqkv[:, 0:F], Wqkv[:, 0:F], DH ** -0.5, None, op0=ALU.mult))
            then(ve.tensor_scalar(rowv[:, 1, :], rowv[:, 1, :], DH ** -0.5, None, op0=ALU.mult))

            def sums_of(s, c, source):
                b = slice(CHUNKS[c][0], sum(CHUNKS[c]))
                then(ve.tensor_reduce(st[:, 0, b], source[:, b, :], AX.X, ALU.add))
                ve.tensor_scalar(st[:, 1, b], st[:, 0, b], -1.0 / F, None, op0=ALU.mult).then_inc(s.sem["xc"], 1)

            def variance(s, c):
                b = slice(CHUNKS[c][0], sum(CHUNKS[c]))
                wait(ve, s["sq"], c + 1)
                ve.tensor_scalar(st[:, 3, b], st[:, 2, b], 1.0 / F, 1e-5, op0=ALU.mult, op1=ALU.add).then_inc(s.sem["var"], 1)

            def normalise(s, c, source, to):
                b0, nb = CHUNKS[c]
                wait(ve, s["std"], c + 1)
                then(ve.reciprocal(st[:, 5, b0:b0 + nb], st[:, 4, b0:b0 + nb]))
                for b in range(b0, b0 + nb):
                    last = ve.tensor_scalar(to[:, b, :], source[:, b, :], st[:, 1, b:b + 1], st[:, 5, b:b + 1],
                                            op0=ALU.add, op1=ALU.mult)
                last.then_inc(s.sem["hn"], 1)

            ve.wait_ge(s_rows, 16 * VK)
            ve.tensor_copy(rows_f[:, :, :], rows_i[:, :, :]).then_inc(s_rowsf, 1)
            ve.wait_ge(s_rowsf, 1)
            then(ve.tensor_tensor(cmpb[:, :, :], rows_f[:, :, P + 1:P + 2].to_broadcast([VP, VK, BLOCKS - 1]),
                                  thr_row[0:VP, :].unsqueeze(1).to_broadcast([VP, VK, BLOCKS - 1]), ALU.is_ge))
            then(ve.tensor_reduce(vstat[:, 2, :], cmpb[:, :, :], AX.X, ALU.add))
            then(ve.tensor_tensor(vstat[:, 3, :], vcol[:, :], vstat[:, 1, :], ALU.subtract))
            then(ve.tensor_tensor(vstat[:, 4, :], vstat[:, 3, :], vstat[:, 2, :], ALU.add))
            then(ve.tensor_scalar(vstat[:, 5, :], vstat[:, 4, :], float(BLOCKS - 1), None, op0=ALU.min))
            then(ve.tensor_scalar(vstat[:, 6, :], vstat[:, 5, :], float(BN), None, op0=ALU.mult))
            then(ve.tensor_tensor(vstat[:, 7, :], rows_f[:, :, P], rows_f[:, :, 2 * P], ALU.subtract))
            then(ve.tensor_tensor(vstat[:, 8, :], rows_f[:, :, P + 1], rows_f[:, :, 2 * P + 1], ALU.subtract))
            ve.tensor_copy(chain_b[:, :, :, :].rearrange("p m k h -> p (m k) h"),
                           vstat[:, 7:9, :].rearrange("p m k -> p (m k)").unsqueeze(2).to_broadcast([VP, 2 * VK, H])
                           ).then_inc(s_v, 1)
            n_v[0] += 1
            then(ve.tensor_tensor(lid_v[:, :, :], rows_f[:, :, P + 1:2 * P + 1],
                                  vstat[:, 6, :].unsqueeze(2).to_broadcast([VP, VK, P]), ALU.subtract))
            ve.sem_inc(s_vlid, 1)
            ve.wait_ge(s_x, 16)
            for k in range(len(CHUNKS) + 2):
                if k < len(CHUNKS):
                    sums_of(L[0], k, xs)
                if 0 <= k - 1 < len(CHUNKS):
                    variance(L[0], k - 1)
                if 0 <= k - 2:
                    normalise(L[0], k - 2, xs, hn)
            wait(ve, L[0]["feat_out"], len(CHUNKS))
            wait(ve, L[0]["feat_done"], len(CHUNKS))
            then(ve.tensor_tensor(nst[:, 0, :, :], h0[:, :, F:W0], nd[:, :, 0:H], ALU.add))
            ve.scalar_tensor_tensor(nd[:, :, H:2 * H], nst[:, 0, :, :], SLOPE, nst[:, 0, :, :], op0=ALU.mult,
                                    op1=ALU.max).then_inc(s_v, 1)
            n_v[0] += 1
            ve.wait_ge(s_v, n_v[0])
            then(ve.tensor_copy(nd3[:, :, 0, :], nd[:, :, :]))
            then(ve.tensor_tensor(nd[:, :, :], nd[:, :, :], nd3[:, :, 0, :], ALU.subtract))
            then(ve.tensor_copy(nd3[:, :, 1, :], nd[:, :, :]))
            then(ve.tensor_tensor(nd[:, :, :], nd[:, :, :], nd3[:, :, 1, :], ALU.subtract))
            ve.tensor_copy(nd3[:, :, 2, :], nd[:, :, :]).then_inc(L[0].sem["feat_done"], 1)
            for c in range(-(-GROUPS // 3)):
                ng = min(3, GROUPS - 3 * c)
                ve.wait_ge(s_pene, c + 1)
                d = prod[:, c % 2, 0:ng * (P + 2)].rearrange("p (g e) -> p g e", g=ng)
                ve.tensor_tensor(pen[:, 3 * c:3 * c + ng, :], d[:, :, 0:P + 1], d[:, :, 1:P + 2], ALU.subtract).then_inc(s_penfree, 1)
            ve.wait_ge(s_penfree, -(-GROUPS // 3))
            ve.wait_ge(s_vte, 8)
            ve.wait_ge(s_bz, 16)

            def layer(n):
                s = L[n]
                k = 2 - n
                acc_f = acc[:, :, :].rearrange("p b f -> p (b f)")

                def step(g, u, i, new, mid, old):
                    q, r = g - 1, g - 2
                    uq, ur = (u + 2) % UNROLL, (u + 1) % UNROLL
                    score = sT[:, 0:P] if n else smax[:, :]
                    p0 = pcur[:, uq, 0:P]
                    p1 = pcur[:, uq, 1:P + 1]
                    d, e = D[:, uq, :, :], D[:, u, :, :]
                    off = []

                    def load_offsets(k):
                        if old:
                            half = regs[k * GV // 2:(k + 1) * GV // 2]
                            ve.load(half, offs[0][:, bass.ds(r * GV + k * (GV // 2), GV // 2)])
                            off.extend(ve.snap(x, min_val=0, max_val=(BLOCKS - 1) * H * SLOT) for x in half)

                    def one_hot(j):
                        if not new:
                            return
                        wait(ve, s["mm_done"], GV * (g - UNROLL + 1))
                        ve.tensor_tensor(S[:, u, QV * j:QV * j + QV, :],
                                         iota_n[:, 0:BN].unsqueeze(1).to_broadcast([P, QV, BN]),
                                         lid[:, bass.ds(g * GV + QV * j, QV)].unsqueeze(2).to_broadcast([P, QV, BN]),
                                         ALU.is_equal).then_inc(s.sem["S_ready"], 1)

                    def qk_product(j):
                        if not new or n == 0:
                            return
                        ve.wait_ge(s_gath[u][j], gathered(n, u, i))
                        wait(ve, s["expanded"], 4 * g + j + 1)
                        wait(ve, s["score_parts"], 4 * g + j - 1)
                        ve.tensor_tensor(prod[:, j % 2, :].rearrange("p (v f) -> p v f", v=QV),
                                         ex[j % 2][:, :].rearrange("p (v f) -> p v f", v=QV),
                                         G[:, u, QV * j:QV * j + QV, 0:F], ALU.mult).then_inc(s.sem["qk_done"], 1)

                    def qk_sum(j):
                        if not new or n == 0:
                            return
                        wait(ve, s["qk_done"], 4 * g + j + 1)
                        wait(ve, s["scores_ready"], g)
                        ve.tensor_reduce(raw[:, QV * j:QV * j + QV, :].rearrange("p v h -> p (v h)"),
                                         prod[:, j % 2, :].rearrange("p (c d) -> p c d", d=DH), AX.X,
                                         ALU.add).then_inc(s.sem["score_parts"], 1)

                    def score_sum():
                        if not new or n == 1:
                            return
                        for j in range(GV // QV):
                            ve.wait_ge(s_gath[u][j], gathered(n, u, i))
                        wait(ve, s["es_ready"], g + 1)
                        wait(ve, s["scores_ready"], g)
                        ve.tensor_tensor(raw[:, :, :], es[:, 0, :, :],
                                         G[:, u, :, F:W0], ALU.add).then_inc(s.sem["score_parts"], 1)

                    def scores():
                        if not new:
                            return
                        wait(ve, s["score_parts"], (4 if n else 1) * (g + 1))
                        wait(ve, s["scoreT"], g)
                        if n == 0:
                            ve.scalar_tensor_tensor(sc[:, :, :], raw[:, :, :], SLOPE, raw[:, :, :], op0=ALU.mult,
                                                    op1=ALU.max).then_inc(s.sem["scores_ready"], 1)
                        else:
                            ve.tensor_tensor(sc[:, :, :].rearrange("p v h -> p (v h)"), raw[:, :, :].rearrange("p v h -> p (v h)"),
                                             ebias[:, :, :].rearrange("p v h -> p (v h)")[:, bass.ds(g * P, P)],
                                             ALU.add).then_inc(s.sem["scores_ready"], 1)

                    def loop_max():
                        if not mid or n == 1:
                            return
                        wait(ve, s["scoreT"], q + 1)
                        wait(ve, s["esT_ready"], q + 1)
                        wait(ve, s["f_done"], q)
                        ve.tensor_tensor(smax[:, :], sT[:, 0:P], esT[:, :], ALU.max).then_inc(s.sem["smax_ready"], 1)

                    def edge_scans():
                        if not mid:
                            return
                        wait(ve, s["pcur_ready"], q + 1)
                        if n == 0:
                            wait(ve, s["smax_ready"], q + 1)
                        else:
                            wait(ve, s["scoreT"], q + 1)
                        wait(ve, s["rh_ready"], q)
                        ve.tensor_tensor_scan(FR[:, 0, :], p0, score, LOW, ALU.add, ALU.max).then_inc(s.sem["edge_scans"], 1)
                        ve.tensor_tensor_scan(FR[:, 1, :], p1[:, ::-1], score[:, ::-1], LOW, ALU.add, ALU.max).then_inc(s.sem["edge_scans"], 1)

                    def edge_maxima():
                        if not mid:
                            return
                        wait(ve, s["edge_scans"], 2 * q + 2)
                        wait(ve, s["hop1"], q)
                        ve.tensor_tensor(RH[:, :, :], Vsel[:, :].unsqueeze(1).to_broadcast([P, 2, GV]),
                                         FR[:, :, P - 1:P].to_broadcast([P, 2, GV]), ALU.mult).then_inc(s.sem["rh_ready"], 1)

                    def visit_scans():
                        if not mid:
                            return
                        wait(ve, s["hop1"], q + 1)
                        wait(ve, s["carry"], q)
                        wait(ve, s["hop2"], q)
                        ve.tensor_tensor_scan(d[:, 0, 1:GV + 1], chain_pen[:, 0, bass.ds(q * GV, GV)], sm[0:H, 0:GV],
                                              d[:, 0, 0:1], ALU.add, ALU.max).then_inc(s.sem["x_done"], 1)
                        ve.tensor_tensor_scan(d[:, 1, GV - 1::-1], chain_pen[:, 1, bass.ds(q * GV, GV)],
                                              sm[0:H, GV:2 * GV][:, ::-1], LOW, ALU.add, ALU.max).then_inc(s.sem["u_done"], 1)

                    def carry():
                        if not mid:
                            return
                        wait(ve, s["x_done"], q + 1)
                        ve.tensor_copy(e[:, 0, 0:1], d[:, 0, GV:GV + 1]).then_inc(s.sem["carry"], 1)

                    def outer_maxima():
                        if not mid:
                            return
                        wait(ve, s["hop2"], q + 1)
                        wait(ve, s["cc_done"], q)
                        ve.tensor_tensor(CCM[:, :, :], sm[:, 64:64 + 2 * GV].rearrange("p (k v) -> p k v", k=2),
                                         Vsel[:, :].unsqueeze(1).to_broadcast([P, 2, GV]), ALU.mult).then_inc(s.sem["cc_mul"], 1)

                    def outer_columns():
                        if not mid:
                            return
                        wait(ve, s["cc_mul"], q + 1)
                        wait(ve, s["df"], 2 * q)
                        wait(ve, s["m_done"], q)
                        ve.tensor_reduce(CC[:, :], CCM[:, :, :], AX.X, ALU.add).then_inc(s.sem["cc_done"], 1)

                    def forward_maxima():
                        if not mid:
                            return
                        wait(ve, s["cc_done"], q + 1)
                        wait(ve, s["m_done"], q)
                        ve.tensor_tensor_scan(FF[:, :], p0, score, CC[:, 0:1], ALU.add, ALU.max).then_inc(s.sem["f_done"], 1)

                    def node_maxima():
                        if not mid:
                            return
                        wait(ve, s["f_done"], q + 1)
                        wait(ve, s["dd_ready"], (2 - n) * q)
                        wait(ve, s["df"], 2 * q)
                        ve.tensor_tensor_scan(MM[:, ::-1], p1[:, ::-1], FF[:, ::-1], CC[:, 1:2], ALU.add, ALU.max).then_inc(s.sem["m_done"], 1)

                    def differences():
                        if not mid:
                            return
                        wait(ve, s["m_done"], q + 1)
                        wait(ve, s["p_ready"], q)
                        if n == 0:
                            ve.tensor_tensor(DD[:, 1, :], esT[:, :], MM[:, :], ALU.subtract).then_inc(s.sem["dd_ready"], 1)
                        ve.tensor_tensor(DD[:, 0, :], sT[:, 0:P], MM[:, :], ALU.subtract).then_inc(s.sem["dd_ready"], 1)
                        wait(ve, s["al_mm"], q)
                        wait(ve, s["r8_ready"], q)
                        ve.tensor_tensor(DF[:, 0:1], CC[0:H, 0:1], MM[0:H, 0:1], ALU.subtract).then_inc(s.sem["df"], 1)
                        ve.tensor_scalar(OHF[:, :], iota_n[0:H, 0:BN], first_lid[:, bass.ds(q, 1)], None, op0=ALU.is_equal).then_inc(s.sem["ohf_ready"], 1)

                    def shrink():
                        if not mid:
                            return
                        wait(ve, s["df"], 2 * q + 1)
                        ve.tensor_scalar(DF[:, 1:2], DF[:, 0:1], 0.0, -200.0, op0=ALU.min, op1=ALU.max).then_inc(s.sem["df"], 1)

                    def shrink_heads():
                        if not mid:
                            return
                        wait(ve, s["df"], 2 * q + 2)
                        wait(ve, s["al_mm"], q)
                        ve.tensor_scalar(R8[:, :], ident[0:H, 0:H], DF[:, 1:2], None, op0=ALU.mult).then_inc(s.sem["r8_ready"], 1)

                    def loop_weights():
                        if not mid or n == 1:
                            return
                        wait(ve, s["p_ready"], q + 1)
                        wait(ve, s["pT"], q)
                        ve.scalar_tensor_tensor(PS[:, :], p0, 0.0, EP[:, 1, :], op0=ALU.is_lt, op1=ALU.mult).then_inc(s.sem["ps_ready"], 1)

                    def weigh(j):
                        if not old:
                            return
                        wait(ve, s["pcols"], r + 1)
                        wait(ve, s["mm_done"], GV * r)
                        c0 = F if n else 0
                        rows = G[:, ur, QV * j:QV * j + QV, c0:c0 + F].rearrange("p v (h d) -> p v h d", h=H)
                        ve.tensor_tensor(PV[:, QV * j:QV * j + QV, :, 0:DH], rows,
                                         PV[:, QV * j:QV * j + QV, :, DH:DH + 1].to_broadcast([P, QV, H, DH]), ALU.mult).then_inc(s.sem["pv_ready"], 1)

                    def rescale():
                        if not old:
                            return
                        wait(ve, s["al_ready"], r + 1)
                        wait(ve, s["acc_added"], GV * r)
                        a = acc_f[:, bass.ds(off[0], H * SLOT)].rearrange("p (h k) -> p h k", h=H)
                        ve.tensor_tensor(a, a, AL[:, :].unsqueeze(2).to_broadcast([BN, H, SLOT]), ALU.mult).then_inc(s.sem["rescaled"], 1)

                    def add(v):
                        if not old:
                            return
                        if v == 0:
                            wait(ve, s["rescaled"], r + 1)
                        if v % 2 == 0:
                            wait(ve, s["mm_done"], GV * r + v + 2)
                        wait(ve, s["acc_added"], GV * r + v)
                        a = acc_f[:, bass.ds(off[v], H * SLOT)]
                        o = ms[v % 4 // 2][0:BN, (v % 2) * 256:(v % 2) * 256 + H * SLOT]
                        ve.tensor_tensor(a, a, o, ALU.add).then_inc(s.sem["acc_added"], 1)

                    one_hot(0)
                    load_offsets(0)
                    weigh(0)
                    load_offsets(1)
                    loop_max()
                    weigh(1)
                    edge_scans()
                    rescale()
                    edge_maxima()
                    one_hot(1)
                    add(0)
                    visit_scans()
                    add(1)
                    carry()
                    one_hot(2)
                    add(2)
                    weigh(2)
                    outer_maxima()
                    add(3)
                    outer_columns()
                    add(4)
                    forward_maxima()
                    add(5)
                    node_maxima()
                    one_hot(3)
                    add(6)
                    differences()
                    weigh(3)
                    add(7)
                    shrink()
                    qk_product(0)
                    add(8)
                    shrink_heads()
                    qk_sum(0)
                    add(9)
                    qk_product(1)
                    add(10)
                    loop_weights()
                    qk_sum(1)
                    add(11)
                    qk_product(2)
                    add(12)
                    qk_sum(2)
                    add(13)
                    qk_product(3)
                    score_sum()
                    add(14)
                    qk_sum(3)
                    add(15)
                    scores()

                run_groups(ve, step)
                wait(ve, s["acc_added"], GV * GROUPS)

            layer(0)
            accs = acc[:, :, :].rearrange("p b (h k) -> p b h k", h=H)
            lsum, pself = accs[:, :, :, DH], accs[:, :, :, DH + 1]

            def flat(t):
                return t.rearrange("p b (h d) -> p b h d", d=DH)

            accm = accs[:, :, :, 0:DH]
            then(ve.tensor_tensor(nst[:, 0, :, :], lsum, pself, ALU.add))
            then(ve.tensor_scalar(nst[:, 1, :, :], nst[:, 0, :, :], 0.0, None, op0=ALU.is_equal))
            ve.tensor_tensor(nst[:, 2, :, :], nst[:, 1, :, :], pself, ALU.add).then_inc(s_self, 1)
            then(ve.tensor_tensor(nst[:, 3, :, :], nst[:, 1, :, :], nst[:, 0, :, :], ALU.add))
            then(ve.reciprocal(nst[:, 4, :, :], nst[:, 3, :, :]))
            ve.wait_ge(s_xb, 1)
            ve.wait_ge(s_ebout, 16)
            for k in range(len(CHUNKS) + 4):
                if k < len(CHUNKS):
                    b0, nb = CHUNKS[k]
                    b = slice(b0, b0 + nb)
                    ve.wait_ge(s_hp, k + 1)
                    then(ve.tensor_tensor(flat(hn[:, b, :]), flat(hn[:, b, :]), accm[:, b, :, :], ALU.add))
                    then(ve.tensor_tensor(flat(hn[:, b, :]), flat(hn[:, b, :]), nst[:, 4, b, :].unsqueeze(3).to_broadcast([BN, nb, H, DH]), ALU.mult))
                    then(ve.tensor_tensor(xs[:, b, :], hn[:, b, :], xs[:, b, :], ALU.add))
                    sums_of(L[1], k, xs)
                if 0 <= k - 1 < len(CHUNKS):
                    variance(L[1], k - 1)
                if 0 <= k - 2 < len(CHUNKS):
                    normalise(L[1], k - 2, xs, hn)
                if 0 <= k - 4:
                    b0, nb = CHUNKS[k - 4]
                    for b in range(b0, b0 + nb):
                        wait(ve, L[1]["kv_copied"], b + 1)
                        ve.tensor_tensor(q_sb[:, b, :], feat_bank(b)[0:BN, 0:F], rowv[:, 1, :], ALU.add).then_inc(L[1].sem["feat_out"], 1)
            then(ve.memset(D[:, :, :, :], LOW))
            then(ve.memset(acc[:, :, :], 0.0))
            ve.wait_ge(s_ebe, H)
            layer(1)
            then(ve.tensor_scalar(nst[:, 0, :, :], lsum, 1e-8, None, op0=ALU.add))
            then(ve.reciprocal(nst[:, 1, :, :], nst[:, 0, :, :]))
            for b0, nb in CHUNKS:
                b = slice(b0, b0 + nb)
                ve.tensor_tensor(flat(work2[:, b, :]), accm[:, b, :, :], nst[:, 1, b, :].unsqueeze(3).to_broadcast([BN, nb, H, DH]),
                                 ALU.mult).then_inc(s_fin_on, 1)
            ve.wait_ge(s_hbo, 1)
            for k in range(len(CHUNKS) + 2):
                if k < len(CHUNKS):
                    b0, nb = CHUNKS[k]
                    b = slice(b0, b0 + nb)
                    ve.wait_ge(s_fo, k + 1)
                    ve.tensor_tensor(hn[:, b, :], ex[k % 2][0:BN, 0:nb * F].rearrange("p (b f) -> p b f", b=nb),
                                     hn[:, b, :], ALU.add).then_inc(s_fh, 1)
                    ve.wait_ge(s_fh, k + 1)
                    sums_of(F_, k, hn)
                if 0 <= k - 1 < len(CHUNKS):
                    variance(F_, k - 1)
                if 0 <= k - 2:
                    b0, nb = CHUNKS[k - 2]
                    b = slice(b0, b0 + nb)
                    normalise(F_, k - 2, hn, work)
                    wait(ve, F_["hn"], k - 1)
                    ve.tensor_tensor(work[:, b, :], work[:, b, :], rowv[:, 5, :].unsqueeze(1).to_broadcast([BN, nb, F]),
                                     ALU.mult).then_inc(s_norm, 1)


_INS = ['x', 'src', 'dst', 'edge_attr_32', 'L0_gnn_W', 'L0_gnn_att', 'L0_gnn_bias', 'L1_gnn_Wq', 'L1_gnn_bq',
        'L1_gnn_Wk', 'L1_gnn_bk', 'L1_gnn_Wv', 'L1_gnn_bv', 'L1_gnn_We', 'L1_gnn_be', 'L1_gnn_Wo', 'L1_gnn_bo',
        'L1_gnn_gamma', 'L1_gnn_beta']
_OUTS = [((3125, 128), 'float32')]


def kernel(**inputs):
    import numpy as _np
    import concourse.bacc as _bacc
    from concourse import mybir as _mybir
    from concourse.bass_utils import run_bass_kernel_spmd as _run

    nc = _bacc.Bacc("TRN2", target_bir_lowering=False, num_devices=1)
    arrays, args = {}, []
    for name in _INS:
        a = _np.ascontiguousarray(inputs[name])
        arrays[f"in_{name}_dram"] = a
        args.append(nc.dram_tensor(f"in_{name}_dram", a.shape, _mybir.dt.from_np(a.dtype), kind="ExternalInput").ap())
    for i, (shape, dtype) in enumerate(_OUTS):
        dt = _mybir.dt.from_np(_np.dtype(dtype))
        args.append(nc.dram_tensor(f"out_{i}_dram", shape, dt, kind="ExternalOutput").ap())
    gnn_kernel(nc, *args)
    r = _run(nc, [arrays], core_ids=[0])
    got = tuple(r.results[0][f"out_{i}_dram"] for i in range(len(_OUTS)))
    return got[0]
```
